# Optimizing a Trainium2 kernel written in Bass

```python
import numpy as np
import jax
import jax.numpy as jnp

def _softmax(x, axis=-1):
    return jax.nn.softmax(x, axis=axis)

def _gelu(x):
    return jax.nn.gelu(x, approximate=True)

def _silu(x):
    return jax.nn.silu(x)

def _sigmoid(x):
    return jax.nn.sigmoid(x)

def _layernorm(x, axis=-1, eps=1e-05):
    m = jnp.mean(x, axis=axis, keepdims=True)
    v = jnp.var(x, axis=axis, keepdims=True)
    return (x - m) / jnp.sqrt(v + eps)

def _scatter_add(tgt, idx, src, axis=0):
    return tgt.at[idx].add(src)

def _segment_sum(src, seg, n):
    return jax.ops.segment_sum(src, seg, n)
kernel_name = 'mk_decoder_postln_d1_seqx_r4_9c2466'

def setup_inputs(seed: int=0):
    np.random.seed(seed)
    _w = jnp.asarray

    def _rec_inputs():
        import jax
        import jax.numpy as jnp
        _rk = jax.random.key(seed)
        x = 7.22e-05 + 1 * jax.random.normal(jax.random.fold_in(_rk, 1), (4, 512, 512), jnp.float32)
        _lenS = 512 - jax.random.randint(jax.random.fold_in(_rk, 7), (4,), 0, max(1, 512 // 4) + 1, jnp.int32)
        _lenS2 = 512 - jax.random.randint(jax.random.fold_in(_rk, 8), (4,), 0, max(1, 512 // 4) + 1, jnp.int32)
        _ctx_1024P = jax.random.normal(jax.random.fold_in(_rk, 11), (4, 16, 256), jnp.float32)
        _ctx_1024c = jax.random.dirichlet(jax.random.fold_in(_rk, 511), 0.3 * jnp.ones((16,), jnp.float32), (4, 512))
        _ctx_1024t = jnp.einsum('bsk,bkd->bsd', _ctx_1024c, _ctx_1024P)
        _ctx_1024t = _ctx_1024t * jax.lax.rsqrt(jnp.mean(jnp.square(_ctx_1024t)) + 1e-12) * 0.953939
        ctx_1024 = 2.81802e-05 + 1.00001 * (_ctx_1024t + 0.3 * jax.random.normal(jax.random.fold_in(_rk, 611), (4, 512, 256), jnp.float32))
        return (x, ctx_1024)
    x, ctx_1024 = _rec_inputs()

    def _L0_attn_setup():
        import jax, jax.numpy as jnp
        import numpy as np
        N_HEADS = 16

        def _rope_tables(seq_len, head_dim, dtype=jnp.float32):
            pos = jnp.arange(seq_len, dtype=jnp.float32)[:, None]
            exps = -jnp.arange(0, head_dim, 2, dtype=jnp.float32) / head_dim
            thetas = jnp.repeat(jnp.power(10000.0, exps), 2)
            angles = pos * thetas[None, :]
            return (jnp.cos(angles).astype(dtype), jnp.sin(angles).astype(dtype))

        def _apply_rope(x, cos, sin):
            x_even = x[..., 0::2]
            x_odd = x[..., 1::2]
            x_rot = jnp.stack((-x_odd, x_even), axis=-1).reshape(x.shape)
            return x * cos[None, :, None, :] + x_rot * sin[None, :, None, :]
        key = jax.random.key(seed)
        ks = jax.random.split(key, 5)
        B, S, E = (2, 512, 512)
        scale = 1.0 / np.sqrt(E)
        return {'x': jax.random.normal(ks[0], (B, S, E), dtype=jnp.float32), 'Wq': jax.random.normal(ks[1], (E, E), dtype=jnp.float32) * scale, 'bq': jnp.zeros((E,), dtype=jnp.float32), 'Wk': jax.random.normal(ks[2], (E, E), dtype=jnp.float32) * scale, 'bk': jnp.zeros((E,), dtype=jnp.float32), 'Wv': jax.random.normal(ks[3], (E, E), dtype=jnp.float32) * scale, 'bv': jnp.zeros((E,), dtype=jnp.float32), 'Wo': jax.random.normal(ks[4], (E, E), dtype=jnp.float32) * scale, 'bo': jnp.zeros((E,), dtype=jnp.float32)}
    _L0_attn_all = _L0_attn_setup()
    _L0_attn_in = {k: v for k, v in _L0_attn_all.items() if k in ('Wq', 'bq', 'Wk', 'bk', 'Wv', 'bv', 'Wo', 'bo')}
    del _L0_attn_all

    def _L0_xattn_setup():
        import jax, jax.numpy as jnp
        import numpy as np
        key = jax.random.key(seed)
        ks = jax.random.split(key, 6)
        B, L, N, C, D = (8, 128, 512, 256, 128)
        return {'teacher_logits': jax.random.normal(ks[0], (B, L, N), dtype=jnp.float32), 'teacher_features': jax.random.normal(ks[1], (B, N, C), dtype=jnp.float32), 'Wq': jax.random.normal(ks[2], (D, C), dtype=jnp.float32) * (1.0 / np.sqrt(C)), 'bq': jnp.zeros((D,), dtype=jnp.float32), 'Wk': jax.random.normal(ks[3], (D, C), dtype=jnp.float32) * (1.0 / np.sqrt(C)), 'bk': jnp.zeros((D,), dtype=jnp.float32)}
    _L0_xattn_all = _L0_xattn_setup()
    _L0_xattn_in = {k: v for k, v in _L0_xattn_all.items() if k in ('Wq', 'bq', 'Wk', 'bk')}
    del _L0_xattn_all

    def _L0_ffn_setup():
        import jax, jax.numpy as jnp
        import numpy as np
        DIM_IN = 512
        DIM_HIDDEN = 2048
        key = jax.random.key(seed)
        k_x, k_g, k_u, k_d = jax.random.split(key, 4)
        s_in = 1.0 / np.sqrt(DIM_IN)
        s_hid = 1.0 / np.sqrt(DIM_HIDDEN)
        x = jax.random.normal(k_x, (4, 512, DIM_IN), dtype=jnp.float32)
        w_gate = jax.random.uniform(k_g, (DIM_HIDDEN, DIM_IN), jnp.float32, -s_in, s_in)
        w_up = jax.random.uniform(k_u, (DIM_HIDDEN, DIM_IN), jnp.float32, -s_in, s_in)
        w_down = jax.random.uniform(k_d, (DIM_IN, DIM_HIDDEN), jnp.float32, -s_hid, s_hid)
        return {'x': x, 'w_gate': w_gate, 'w_up': w_up, 'w_down': w_down}
    _L0_ffn_all = _L0_ffn_setup()
    _L0_ffn_in = {k: v for k, v in _L0_ffn_all.items() if k in ('w_gate', 'w_up', 'w_down')}
    del _L0_ffn_all
    return {'x': x, 'ctx_1024': ctx_1024, 'L0_attn_Wq': _L0_attn_in['Wq'], 'L0_attn_bq': _L0_attn_in['bq'], 'L0_attn_Wk': _L0_attn_in['Wk'], 'L0_attn_bk': _L0_attn_in['bk'], 'L0_attn_Wv': _L0_attn_in['Wv'], 'L0_attn_bv': _L0_attn_in['bv'], 'L0_attn_Wo': _L0_attn_in['Wo'], 'L0_attn_bo': _L0_attn_in['bo'], 'L0_xattn_Wq': _L0_xattn_in['Wq'], 'L0_xattn_bq': _L0_xattn_in['bq'], 'L0_xattn_Wk': _L0_xattn_in['Wk'], 'L0_xattn_bk': _L0_xattn_in['bk'], 'L0_ffn_w_gate': _L0_ffn_in['w_gate'], 'L0_ffn_w_up': _L0_ffn_in['w_up'], 'L0_ffn_w_down': _L0_ffn_in['w_down']}

def reference(x, ctx_1024, L0_attn_Wq, L0_attn_bq, L0_attn_Wk, L0_attn_bk, L0_attn_Wv, L0_attn_bv, L0_attn_Wo, L0_attn_bo, L0_xattn_Wq, L0_xattn_bq, L0_xattn_Wk, L0_xattn_bk, L0_ffn_w_gate, L0_ffn_w_up, L0_ffn_w_down):
    import jax
    import jax.numpy as jnp

    def _L0_attn_ref(x, Wq, bq, Wk, bk, Wv, bv, Wo, bo):
        import jax, jax.numpy as jnp
        import numpy as np
        N_HEADS = 16

        def _rope_tables(seq_len, head_dim, dtype=jnp.float32):
            pos = jnp.arange(seq_len, dtype=jnp.float32)[:, None]
            exps = -jnp.arange(0, head_dim, 2, dtype=jnp.float32) / head_dim
            thetas = jnp.repeat(jnp.power(10000.0, exps), 2)
            angles = pos * thetas[None, :]
            return (jnp.cos(angles).astype(dtype), jnp.sin(angles).astype(dtype))

        def _apply_rope(x, cos, sin):
            x_even = x[..., 0::2]
            x_odd = x[..., 1::2]
            x_rot = jnp.stack((-x_odd, x_even), axis=-1).reshape(x.shape)
            return x * cos[None, :, None, :] + x_rot * sin[None, :, None, :]
        B, S, E = x.shape
        H = N_HEADS
        D = E // H
        cos, sin = _rope_tables(S, D, x.dtype)
        q = (x @ Wq + bq).reshape(B, S, H, D)
        k = (x @ Wk + bk).reshape(B, S, H, D)
        v = (x @ Wv + bv).reshape(B, S, H, D)
        q = _apply_rope(q, cos, sin)
        k = _apply_rope(k, cos, sin)
        scores = jnp.einsum('bshd,bthd->bhst', q, k) / jnp.sqrt(jnp.asarray(D, x.dtype))
        causal = jnp.triu(jnp.ones((S, S), dtype=bool), k=1)
        scores = jnp.where(causal[None, None], -jnp.inf, scores)
        attn = jax.nn.softmax(scores, axis=-1)
        out = jnp.einsum('bhst,bthd->bshd', attn, v).reshape(B, S, E)
        return out @ Wo + bo

    def _L0_xattn_ref(teacher_logits, teacher_features, Wq, bq, Wk, bk):
        import jax, jax.numpy as jnp
        import numpy as np
        query = jnp.einsum('bnc,dc->bnd', teacher_features, Wq) + bq
        key = jnp.einsum('bnc,dc->bnd', teacher_features, Wk) + bk
        energy = jnp.einsum('bnd,bmd->bnm', query, key)
        attention = jax.nn.softmax(energy, axis=-1)
        x_m = jnp.einsum('bln,bmn->blm', teacher_logits, attention)
        return x_m

    def _L0_ffn_ref(x, w_gate, w_up, w_down):
        import jax, jax.numpy as jnp
        import numpy as np
        DIM_IN = 512
        DIM_HIDDEN = 2048
        gate = jnp.einsum('bsd,hd->bsh', x, w_gate)
        up = jnp.einsum('bsd,hd->bsh', x, w_up)
        gated = jax.nn.silu(gate) * up
        return jnp.einsum('bsh,dh->bsd', gated, w_down)
    x = _layernorm(x + _L0_attn_ref(x, L0_attn_Wq, L0_attn_bq, L0_attn_Wk, L0_attn_bk, L0_attn_Wv, L0_attn_bv, L0_attn_Wo, L0_attn_bo), axis=-1)
    x = _layernorm(x + _L0_xattn_ref(x, ctx_1024, L0_xattn_Wq, L0_xattn_bq, L0_xattn_Wk, L0_xattn_bk), axis=-1)
    x = _layernorm(x + _L0_ffn_ref(x, L0_ffn_w_gate, L0_ffn_w_up, L0_ffn_w_down), axis=-1)
    return x

_drawn_inputs = setup_inputs


def setup_inputs(seed=0):
    import zlib

    import numpy as np

    out = dict(_drawn_inputs(seed))
    spreads = {'L0_attn_bq': (0.0, 0.615),
     'L0_attn_bk': (0.0, 0.8),
     'L0_attn_bv': (0.0, 0.1),
     'L0_attn_bo': (0.0, 0.1),
     'L0_xattn_bq': (0.0, 0.1),
     'L0_xattn_bk': (0.0, 0.8)}
    factors = {}
    for name, (base, spread) in spreads.items():
        noise = np.random.default_rng([zlib.crc32(name.encode()), seed]).standard_normal(out[name].shape)
        drawn = base * np.exp(spread * noise) if base else spread * noise
        out[name] = jnp.asarray(drawn.astype(out[name].dtype))
    for name, factor in factors.items():
        out[name] = (out[name] * factor).astype(out[name].dtype)
    return out
```

```python
from contextlib import ExitStack

import numpy as np

import concourse.bass as bass
from concourse import mybir

F32 = mybir.dt.float32
F32R = mybir.dt.float32r
ALU = mybir.AluOpType
ACT = mybir.ActivationFunctionType
AX = mybir.AxisListType

P = 128
B, S, E = 4, 512, 512
H, D = 16, 32
CTX, DK = 256, 128
HID = 2048
ST = S // P
KT = E // P
CT = CTX // P
G = H // 4
TILES = 16
SLOTS = G * TILES
HT = HID // P
EPS = 1e-5
MASKED = -1e30
LAG = 3
SWAP = [i ^ 1 for i in range(32)]


def slots():
    project = [("v", 1, 0)]
    for g in (2, 3):
        at = TILES * (g - 1)
        project += [("q", g, at - 6), ("k", g, at - 2), ("v", g, at + 2)]
    values = {5: 1, TILES + 7: 2, 2 * TILES + 7: 3}
    after = {TILES * (g + 1): g for g in range(G - 1)}
    return project, values, after


class Count:

    def __init__(self, sem, per, base=0):
        self.sem, self.per, self.base = sem, per, base

    def at(self, b, k):
        return b * self.per + (self.base + k)


def passed(eng, b, count):
    if not isinstance(b, int):
        eng.sem_inc(count.sem, 1)


def attention_phase(nc, ctx, d, x1_dram):
    def sb(name, shape, dt=F32):
        return ctx.enter_context(nc.sbuf_tensor(name, shape, dt))

    def sem(name, per=0, base=0):
        return Count(ctx.enter_context(nc.semaphore(name)), per, base)

    w_hi = sb("w_hi", [P, 3 * G, KT, P], F32R)
    w_lo = sb("w_lo", [P, 3 * G, KT, P], F32R)
    wo_hi = sb("wo_hi", [P, KT, E], F32R)
    wo_lo = sb("wo_lo", [P, KT, E], F32R)
    x_raw = sb("x_raw", [P, KT, S])
    xT_hi = sb("xT_hi", [P, KT, S], F32R)
    xT_lo = sb("xT_lo", [P, KT, S], F32R)
    res = sb("res", [P, ST, E])
    qs = sb("qs", [P, 2, 4, S], F32R)
    ks = sb("ks", [P, 2, 4, S], F32R)
    raw = sb("raw", [P, 2, S])
    swp = sb("swp", [P, S])
    rot = sb("rot", [P, S])
    qk_hi = sb("qk_hi", [P, 2, S], F32R)
    qk_lo = sb("qk_lo", [P, 2, S], F32R)
    vT = sb("vT", [P, S])
    vg = sb("vg", [P, 2, ST, P])
    prob = sb("prob", [P, 4, S])
    pT = sb("pT", [P, 4, 10 * P])
    nmax = sb("nmax", [P, 2, TILES])
    rsum = sb("rsum", [P, 2, ST, 4])
    rrec = sb("rrec", [P, TILES])
    rb = sb("rb", [P, ST, 4, D])
    o = sb("heads", [P, S])
    oT_hi = sb("oT_hi", [P, G, S], F32R)
    oT_lo = sb("oT_lo", [P, G, S], F32R)
    cos = sb("cos", [P, S])
    sin = sb("sin", [P, S])
    mask = sb("mask", [P, S])
    ident = sb("ident", [P, P])
    bcol = sb("bcol", [P, 3 * G])
    bo = sb("bo", [P, E])
    stats = sb("stats", [P, ST, 6])
    mv = sb("mv", [P, ST, 2])
    rstd = sb("rstd", [P, ST])
    veps = sb("veps", [P, ST])
    mhalf = sb("mhalf", [P, 1])

    def w_stage(c):
        if c < G - 1:
            return pT[:].rearrange("p h n -> p (h n)")[:, 3 * KT * P * c:3 * KT * P * (c + 1)]
        return res[:].rearrange("p s e -> p (s e)")[:, 0:3 * KT * P if c < G else KT * E]

    pj = ctx.enter_context(nc.psum_tensor("pj", [P, 2, S], F32))
    ps = ctx.enter_context(nc.psum_tensor("ps", [P, 2, S], F32))
    pa = ctx.enter_context(nc.psum_tensor("pa", [P, S], F32))
    pb = ctx.enter_context(nc.psum_tensor("pb", [P, S], F32))
    pc = ctx.enter_context(nc.psum_tensor("pc", [P, S], F32))
    pv = ctx.enter_context(nc.psum_tensor("pv", [P, S], F32))

    scratch = nc.dram_tensor("qk_scratch", (4 * P, S), F32, kind="Internal").ap()

    AT = [0, 4 * P, 8 * P, 7 * P]

    const_in = sem("const_in")
    sp_passed, dve_passed, pool_passed = (sem(f"{n}_passed") for n in ("sp", "dve", "pool"))
    w_in = [sem(f"w_in{c}") for c in range(G + 1)]
    w_hi_done, w_lo_done = sem("w_hi_done"), sem("w_lo_done")
    x_in = sem("x_in", 16, 16)
    xhi_done = sem("xhi_done", KT, KT)
    xlo_done = sem("xlo_done", KT, KT)
    pj_full = sem("pj_full", 20, 6)
    pj_moved = sem("pj_moved", 20, 6)
    swap_done = sem("swap_done", 2 * G, 2)
    sin_done = sem("sin_done", 2 * G, 2)
    cos_done = sem("cos_done", 2 * G, 2)
    rot_done = sem("rot_done", 2 * G, 2)
    qkhi_done = sem("qkhi_done", 2 * G, 2)
    qklo_done = sem("qklo_done", 2 * G, 2)
    stored = sem("stored", 64 * G, 64)
    stacked = sem("stacked", 128 * G, 128)
    s_done = sem("s_done", SLOTS)
    max_done = sem("max_done", SLOTS)
    exp_done = sem("exp_done", SLOTS)
    t_done = sem("t_done", SLOTS)
    a_moved, b_moved, c_moved = (sem(f"{n}_moved", H) for n in "abc")
    rec_done = sem("rec_done", G)
    rb_done = sem("rb_done", G)
    av_done = sem("av_done", G)
    o_done = sem("o_done", G)
    ohi_done, olo_done = sem("ohi_done", G), sem("olo_done", G)
    wo_done = sem("wo_done", ST)
    res_in = sem("res_in", 16)
    res_done = sem("res_done", ST)
    z_done = sem("z_done", ST)
    stats_done = sem("stats_done", ST)
    mv_done = sem("mv_done", ST)
    rstd_done = sem("rstd_done", ST)
    veps_done = sem("veps_done", ST)
    x1_done = sem("x1_done", ST)
    x1_stored = sem("x1_stored", 16)
    half_done = sem("half_done")


    PROLOGUE = {key: n - 6 for n, key in enumerate(
        [("q", 0), ("k", 0), ("v", 0), ("t", 0), ("q", 1), ("k", 1)])}
    project, value_slots, ends = slots()

    def uses(last):
        order = [("v", 1), ("t", 1)]
        for g in (2, 3):
            order += [("q", g), ("k", g), ("r", g - 2), ("v", g), ("t", g)]
        order += [("r", 2)]
        order += [("r", 3)] if last else [("q", 4), ("r", 3), ("k", 4), ("v", 4), ("t", 4), ("q", 5), ("k", 5)]
        return {key: n for n, key in enumerate(order)} | PROLOGUE

    USES = {False: uses(False), True: uses(True)}

    def wait_moved(eng, b, last, kind, g):
        eng.wait_ge(pj_moved.sem, pj_moved.at(b, USES[last][kind, g] + 1))

    block = ctx.enter_context(nc.Block())

    @block.sync
    def _(sp):
        sp.dma_start(x_raw[:], d["xT"][0:P, :]).then_inc(x_in.sem, 16)
        sp.dma_start(w_stage(0), d["w_qkv"][0:P, :]).then_inc(w_in[0].sem, 16)
        for dst, name in ((bcol, "bcol"), (cos, "cos"), (sin, "sin"), (ident, "ident"), (mask, "mask")):
            sp.dma_start(dst[:], d[name]).then_inc(const_in.sem, 16)
        for g in range(1, G):
            sp.dma_start(w_stage(g), d["w_qkv"][g * P:(g + 1) * P, :]).then_inc(w_in[g].sem, 16)
        sp.dma_start(bo[:], d["bo"]).then_inc(const_in.sem, 16)
        sp.wait_ge(w_hi_done.sem, G)
        sp.wait_ge(w_lo_done.sem, G)
        sp.dma_start(w_stage(G), d["wo"]).then_inc(w_in[G].sem, 16)

        def stack(b, g):
            for u in range(2):
                m = 2 * (g - 1) + u
                rows = 2 * u * P
                if g and not u:
                    sp.wait_ge(stacked.sem, stacked.at(b, 128 * (g - 1)))
                    passed(sp, b, sp_passed)
                sp.wait_ge(qkhi_done.sem, qkhi_done.at(b, m + 1))
                sp.dma_start(scratch[rows // 2:rows // 2 + P, :], qk_hi[:, u, :].bitcast(F32)).then_inc(stored.sem, 16)
                sp.wait_ge(qklo_done.sem, qklo_done.at(b, m + 1))
                sp.dma_start(scratch[2 * P + u * P:3 * P + u * P, :], qk_lo[:, u, :].bitcast(F32)).then_inc(stored.sem, 16)
                sp.wait_ge(stored.sem, stored.at(b, 32 * (m + 1)))
                passed(sp, b, sp_passed)
                if g >= 2:
                    sp.wait_ge(s_done.sem, s_done.at(b, TILES * (g - 1)))
                for j in range(4):
                    lo = j // 2 if u == 0 else j % 2
                    src = scratch[2 * P * lo + u * P:2 * P * lo + u * P + P, :]
                    dst = qs if u == 0 else ks
                    sp.dma_start(dst[D * j:D * j + D, g % 2, :, :].bitcast(F32),
                                 src.rearrange("(r d) s -> d r s", d=D)).then_inc(stacked.sem, 16)

        def batch(b, last):
            rows = bass.ts(b, P)
            sp.dma_start(res[:], d["x"][rows, :]).then_inc(res_in.sem, 16)
            if not last:
                sp.wait_ge(xhi_done.sem, xhi_done.at(b, 0))
                passed(sp, b, sp_passed)
                sp.wait_ge(xlo_done.sem, xlo_done.at(b, 0))
                passed(sp, b, sp_passed)
                sp.dma_start(x_raw[:], d["xT"][bass.ts(b + 1, P), :]).then_inc(x_in.sem, 16)
            for g in range(1, G if last else G + 1):
                stack(b, g)
            sp.wait_ge(x1_done.sem, x1_done.at(b, ST))
            sp.dma_start(x1_dram[rows, :], res[:]).then_inc(x1_stored.sem, 16)
            sp.wait_ge(x1_stored.sem, x1_stored.at(b, 16))
            passed(sp, b, sp_passed)

        stack(0, 0)
        sp.wait_ge(w_hi_done.sem, G + 1)
        sp.wait_ge(w_lo_done.sem, G + 1)
        with sp.Fori(0, B - 1) as b:
            batch(b, False)
        batch(B - 1, True)

    @block.tensor
    def _(pe):
        def open_pj(b, last, key):
            n = USES[last][key]
            if n >= -4:
                pe.wait_ge(pj_moved.sem, pj_moved.at(b, n - 1))
            return n % 2

        def close(mm, count):
            mm.then_inc(count.sem, 1)

        def projection(b, last, kind, g):
            bank = open_pj(b, last, (kind, g))
            if kind == "q" and g in (0, G):
                pe.wait_ge(xhi_done.sem, xhi_done.at(b, 0 if g < G else KT))
                pe.wait_ge(xlo_done.sem, xlo_done.at(b, 0 if g < G else KT))
            tile = 3 * (g % G) + "qkv".index(kind)
            for k in range(KT):
                for part, (w, x) in enumerate(((w_hi, xT_hi), (w_lo, xT_hi), (w_hi, xT_lo))):
                    mm = pe.matmul(pj[:, bank, :], w[:, tile, k, :], x[:, k, :],
                                   start=(part == 0 and k == 0), stop=(part == 2 and k == KT - 1))
                if k == KT - 1:
                    close(mm, pj_full)
                yield

        def values(b, last, g):
            bank = open_pj(b, last, ("t", g))
            wait_moved(pe, b, last, "v", g)
            for s in range(ST):
                mm = pe.transpose(pj[:, bank, s * P:(s + 1) * P], vT[:, s * P:(s + 1) * P], ident[:])
            close(mm, pj_full)

        def recips(b, last, g):
            bank = open_pj(b, last, ("r", g))
            pe.wait_ge(rb_done.sem, rb_done.at(b, g + 1))
            for s in range(ST):
                mm = pe.transpose(pj[:, bank, s * P:(s + 1) * P], rb[:, s, :, :].rearrange("p r d -> p (r d)"), ident[:])
            close(mm, pj_full)

        def scores(b, t):
            g, r, s = t // TILES, t % TILES // ST, t % ST
            if t % TILES == 0:
                pe.wait_ge(stacked.sem, stacked.at(b, 128 * g))
            if t >= 2:
                pe.wait_ge(max_done.sem, max_done.at(b, t - 1))
            w = max(2, s + 1) * P
            close(pe.matmul(ps[:, t % 2, 0:w], qs[:, g % 2, r, s * P:(s + 1) * P], ks[:, g % 2, r, 0:w],
                            start=True, stop=True), s_done)

        def transposes(b, t):
            h, s = t // ST, t % ST
            pe.wait_ge(exp_done.sem, exp_done.at(b, t + 1))
            if h and s < 3:
                moved = (a_moved, b_moved, c_moved)[s]
                pe.wait_ge(moved.sem, moved.at(b, h))
            for k in range(s + 1):
                dst = (pa, pb, pc, pb)[k]
                c = (s, s - 1, s - 2, 3)[k] * P
                mm = pe.transpose(dst[:, c:c + P], prob[:, t % 4, k * P:(k + 1) * P], ident[:])
            close(mm, t_done)

        def weighted(b, g):
            for moved in (a_moved, b_moved, c_moved):
                pe.wait_ge(moved.sem, moved.at(b, 4 * g + 4))
            wait_moved(pe, b, False, "t", g)
            if g:
                pe.wait_ge(o_done.sem, o_done.at(b, g))
            for k in range(ST):
                for r in range(4):
                    mm = pe.matmul(pv[D * r:D * r + D, k * P:S], vg[:, g % 2, k, D * r:D * r + D],
                                   pT[:, r, AT[k]:AT[k] + (ST - k) * P], start=(k == 0), stop=(k == ST - 1),
                                   tile_position=(0, D * r))
            close(mm, av_done)

        def output(b, s):
            if s == 0:
                pe.wait_ge(w_hi_done.sem, G + 1)
                pe.wait_ge(w_lo_done.sem, G + 1)
                pe.wait_ge(ohi_done.sem, ohi_done.at(b, G))
                pe.wait_ge(olo_done.sem, olo_done.at(b, G))
            if s >= 2:
                pe.wait_ge(z_done.sem, z_done.at(b, s - 1))
            for part, (w, x) in enumerate(((wo_hi, oT_hi), (wo_lo, oT_hi), (wo_hi, oT_lo))):
                for k in range(KT):
                    mm = pe.matmul(ps[:, s % 2, :], x[:, k, s * P:(s + 1) * P], w[:, k, :],
                                   start=(part == 0 and k == 0), stop=(part == 2 and k == KT - 1))
            close(mm, wo_done)

        def batch(b, last):
            work = [(first, projection(b, last, kind, g)) for kind, g, first in project]
            for t in range(SLOTS):
                scores(b, t)
                if t - 2 in ends:
                    recips(b, last, ends[t - 2])
                for first, parts in work:
                    if first <= t < first + 4:
                        next(parts)
                if t in value_slots:
                    values(b, last, value_slots[t])
                if t >= LAG and (t - LAG) % ST:
                    if (t - LAG) % ST == 1:
                        transposes(b, t - LAG - 1)
                    transposes(b, t - LAG)
                if t - 5 in ends:
                    weighted(b, ends[t - 5])
            work = {} if last else {(kind, g): projection(b, last, kind, g)
                                    for kind, g in (("q", 4), ("k", 4), ("v", 4), ("q", 5), ("k", 5))}

            def fill(key, n=4):
                if work:
                    for _ in range(n):
                        next(work[key])
            for t in range(SLOTS - ST, SLOTS):
                transposes(b, t)
                fill(("q", 4), 1)
            recips(b, last, G - 1)
            fill(("k", 4))
            weighted(b, G - 1)
            fill(("v", 4))
            if not last:
                values(b, last, G)
            fill(("q", 5))
            fill(("k", 5))
            for s in range(ST):
                output(b, s)
            pe.wait_ge(z_done.sem, z_done.at(b, ST))

        pe.wait_ge(w_hi_done.sem, 1)
        pe.wait_ge(w_lo_done.sem, 1)
        for kind in "qkv":
            for _ in projection(0, False, kind, 0):
                pass
        pe.wait_ge(const_in.sem, 16 * 6)
        values(0, False, 0)
        pe.wait_ge(w_hi_done.sem, 2)
        pe.wait_ge(w_lo_done.sem, 2)
        for kind in "qk":
            for _ in projection(0, False, kind, 1):
                pass
        pe.wait_ge(w_hi_done.sem, G)
        pe.wait_ge(w_lo_done.sem, G)
        with pe.Fori(0, B - 1) as b:
            batch(b, False)
        batch(B - 1, True)

    @block.scalar
    def _(act):
        def w_half(c):
            act.wait_ge(w_in[c].sem, 16)
            dst = w_hi[:, 3 * c:3 * c + 3, :, :] if c < G else wo_hi[:]
            flat = "p a k m -> p (a k m)" if c < G else "p k m -> p (k m)"
            act.copy(dst.rearrange(flat), w_stage(c)).then_inc(w_hi_done.sem, 1)

        def x_half(b, k, first=False):
            if not first and k == 0:
                n = USES[False]["v", G - 1]
                act.wait_ge(pj_full.sem, pj_full.at(b, n + 1))
                act.wait_ge(x_in.sem, x_in.at(b, 16))
            act.copy(xT_hi[:, k, :], x_raw[:, k, :]).then_inc(xhi_done.sem, 1)

        def from_pj(b, last, kind, g):
            n = USES[last][kind, g]
            act.wait_ge(pj_full.sem, pj_full.at(b, n + 1))
            src = pj[:, n % 2, :]
            if kind in "qk":
                u = "qk".index(kind)
                m = 2 * (g - 1) + u
                if g:
                    act.wait_ge(swap_done.sem, swap_done.at(b, m - 1))
                    act.wait_ge(cos_done.sem, cos_done.at(b, m - 1))
                ins = act.activation(raw[:, u, :], src, ACT.Identity, bias=bcol[:, 3 * (g % G) + u:3 * (g % G) + u + 1])
            elif kind == "v":
                ins = act.activation(vT[:], src, ACT.Identity, bias=bcol[:, 3 * (g % G) + 2:3 * (g % G) + 3])
            elif kind == "t":
                if g >= 2:
                    act.wait_ge(av_done.sem, av_done.at(b, g - 1))
                ins = act.copy(vg[:, g % 2, :, :].rearrange("p s m -> p (s m)"), src)
            else:
                if g:
                    act.wait_ge(olo_done.sem, olo_done.at(b, g))
                ins = act.copy(o[:], src)
            ins.then_inc(pj_moved.sem, 1)

        def qk_half(b, u, g):
            m = 2 * (g - 1) + u
            act.wait_ge(rot_done.sem, rot_done.at(b, m + 1))
            if g:
                act.wait_ge(stored.sem, stored.at(b, 64 * (g - 1)))
            act.copy(qk_hi[:, u, :], rot[:]).then_inc(qkhi_done.sem, 1)

        def exp(b, t):
            g, i, w = t // TILES, t % TILES, (t % ST + 1) * P
            act.wait_ge(max_done.sem, max_done.at(b, t + 1))
            act.activation(prob[:, t % 4, 0:w], prob[:, t % 4, 0:w], ACT.Exp, bias=nmax[:, g % 2, i:i + 1], scale=-1.0,
                           accum_out=rsum[:, g % 2, t % ST, i // ST:i // ST + 1]).then_inc(exp_done.sem, 1)

        def move_a(b, h):
            if h >= 4:
                act.wait_ge(av_done.sem, av_done.at(b, h // 4))
            act.wait_ge(t_done.sem, t_done.at(b, 4 * h + 4))
            act.copy(pT[:, h % 4, 0:S], pa[:]).then_inc(a_moved.sem, 1)

        def o_half(b, g):
            act.wait_ge(o_done.sem, o_done.at(b, g + 1))
            act.copy(oT_hi[:, g, :], o[:]).then_inc(ohi_done.sem, 1)

        def batch(b, last):
            halves = {1: (0, 1), 4: (1, 1)}
            moves = {}
            for kind, g, first in project:
                moves[first + 3] = (kind, g)
                if kind in "qk":
                    halves[first + 6] = ("qk".index(kind), g)
            for t in range(SLOTS):
                exp(b, t)
                if t % ST == 2 and t > LAG:
                    move_a(b, (t - LAG) // ST)
                if t in moves:
                    from_pj(b, last, *moves[t])
                if t - 1 in value_slots:
                    from_pj(b, last, "t", value_slots[t - 1])
                if t in halves:
                    qk_half(b, *halves[t])
                if t - 2 in ends:
                    from_pj(b, last, "r", ends[t - 2])
                if t - 7 in ends:
                    o_half(b, ends[t - 7])
                if not last and t in (41, 43, 45, 47):
                    x_half(b, (t - 41) // 2)
            if not last:
                from_pj(b, last, "q", 4)
            move_a(b, H - 1)
            from_pj(b, last, "r", G - 1)
            if not last:
                qk_half(b, 0, 4)
                from_pj(b, last, "k", 4)
            o_half(b, G - 1)
            if not last:
                from_pj(b, last, "v", 4)
                from_pj(b, last, "t", 4)
                qk_half(b, 1, 4)
                from_pj(b, last, "q", 5)
                from_pj(b, last, "k", 5)

        act.wait_ge(x_in.sem, 16)
        for k in range(KT):
            x_half(0, k, True)
        w_half(0)
        act.wait_ge(const_in.sem, 16 * 6)
        for u in range(2):
            from_pj(0, False, "qk"[u], 0)
        w_half(1)
        qk_half(0, 0, 0)
        from_pj(0, False, "v", 0)
        qk_half(0, 1, 0)
        from_pj(0, False, "t", 0)
        for kind in "qk":
            from_pj(0, False, kind, 1)
        for c in range(2, G + 1):
            w_half(c)
        with act.Fori(0, B - 1) as b:
            batch(b, False)
        batch(B - 1, True)

    @block.vector
    def _(dve):
        def w_half(c):
            dve.wait_ge(w_hi_done.sem, c + 1)
            hi, lo = (w_hi[:, 3 * c:3 * c + 3, :, :], w_lo[:, 3 * c:3 * c + 3, :, :]) if c < G else (wo_hi[:], wo_lo[:])
            flat = "p a k m -> p (a k m)" if c < G else "p k m -> p (k m)"
            dve.tensor_tensor(lo.rearrange(flat), w_stage(c), hi.rearrange(flat).bitcast(F32),
                              ALU.subtract).then_inc(w_lo_done.sem, 1)

        def rotate(b, last, u, g):
            m = 2 * (g - 1) + u
            wait_moved(dve, b, last, "qk"[u], g)
            if g or u:
                dve.wait_ge(rot_done.sem, rot_done.at(b, m))
            passed(dve, b, dve_passed)
            dve.stream_shuffle(swp[:], raw[:, u, :], SWAP).then_inc(swap_done.sem, 1)
            dve.wait_ge(swap_done.sem, swap_done.at(b, m + 1))
            dve.tensor_tensor(swp[:], swp[:], sin[:], ALU.mult).then_inc(sin_done.sem, 1)

        def row_max(b, t):
            g, i, s = t // TILES, t % TILES, t % ST
            w = (s + 1) * P
            dve.wait_ge(s_done.sem, s_done.at(b, t + 1))
            if t >= 4:
                dve.wait_ge(t_done.sem, t_done.at(b, t - 3))
            passed(dve, b, dve_passed)
            dve.tensor_tensor_reduce(prob[:, t % 4, 0:w], ps[:, t % 2, 0:w], mask[:, S - w:S], -D ** -0.5, 3e38,
                                     ALU.add, ALU.min, accum_out=nmax[:, g % 2, i:i + 1]).then_inc(max_done.sem, 1)

        def move_bc(b, h):
            if h >= 4:
                dve.wait_ge(av_done.sem, av_done.at(b, h // 4))
            dve.wait_ge(t_done.sem, t_done.at(b, 4 * h + 4))
            dve.tensor_copy(pT[:, h % 4, S:2 * S], pb[:]).then_inc(b_moved.sem, 1)
            dve.tensor_copy(pT[:, h % 4, 2 * S:10 * P], pc[:, 0:2 * P]).then_inc(c_moved.sem, 1)

        def recips(b, g):
            dve.wait_ge(exp_done.sem, exp_done.at(b, TILES * (g + 1)))
            dve.reciprocal(rrec[:], rsum[:, g % 2, :, :].rearrange("p s r -> p (s r)")).then_inc(rec_done.sem, 1)
            dve.wait_ge(rec_done.sem, rec_done.at(b, g + 1))
            dve.tensor_copy(rb[:], rrec[:].rearrange("p (s r) -> p s r", r=4).unsqueeze(3)
                            .to_broadcast([P, ST, 4, D])).then_inc(rb_done.sem, 1)

        def normalize(b, last, g):
            dve.wait_ge(av_done.sem, av_done.at(b, g + 1))
            wait_moved(dve, b, last, "r", g)
            dve.tensor_tensor(o[:], pv[:], o[:], ALU.mult).then_inc(o_done.sem, 1)

        def layer_norm(b):
            for s in range(ST):
                if s == 0:
                    dve.wait_ge(res_done.sem, res_done.at(b, ST))
                dve.wait_ge(wo_done.sem, wo_done.at(b, s + 1))
                dve.tensor_tensor(res[:, s, :], ps[:, s % 2, :], res[:, s, :], ALU.add).then_inc(z_done.sem, 1)
                dve.wait_ge(z_done.sem, z_done.at(b, s + 1))
                dve.bn_stats(stats[:, s, :], res[:, s, :]).then_inc(stats_done.sem, 1)
                dve.wait_ge(stats_done.sem, stats_done.at(b, s + 1))
                passed(dve, b, dve_passed)
                dve.bn_aggr(mv[:, s, :], stats[:, s, :]).then_inc(mv_done.sem, 1)
            for s in range(ST):
                dve.wait_ge(rstd_done.sem, rstd_done.at(b, s + 1))
                dve.tensor_scalar(res[:, s, :], res[:, s, :], mv[:, s, 0:1], rstd[:, s:s + 1],
                                  ALU.subtract, ALU.mult).then_inc(x1_done.sem, 1)

        def batch(b, last):
            turns = {0: (0, 1), 2: (1, 1)}
            for kind, g, first in project:
                if kind in "qk":
                    turns[first + 4] = ("qk".index(kind), g)
            for t in range(SLOTS):
                row_max(b, t)
                if t in ends:
                    recips(b, ends[t])
                if t % ST == 2 and t > LAG:
                    move_bc(b, (t - LAG) // ST)
                if t in turns:
                    rotate(b, last, *turns[t])
                if t - 6 in ends:
                    normalize(b, last, ends[t - 6])
            recips(b, G - 1)
            move_bc(b, H - 1)
            if not last:
                rotate(b, last, 0, 4)
            normalize(b, last, G - 1)
            if not last:
                rotate(b, last, 1, 4)
            layer_norm(b)

        w_half(0)
        dve.wait_ge(const_in.sem, 16 * 6)
        rotate(0, False, 0, 0)
        rotate(0, False, 1, 0)
        for c in range(1, G + 1):
            w_half(c)
        with dve.Fori(0, B - 1) as b:
            batch(b, False)
        batch(B - 1, True)

    @block.gpsimd
    def _(pool):
        def x_half(b, k, first=False):
            pool.wait_ge(xhi_done.sem, k + 1 if first else xhi_done.at(b, k + 1))
            pool.tensor_tensor(xT_lo[:, k, :], x_raw[:, k, :], xT_hi[:, k, :].bitcast(F32),
                               ALU.subtract).then_inc(xlo_done.sem, 1)

        def rotate(b, last, u, g):
            m = 2 * (g - 1) + u
            wait_moved(pool, b, last, "qk"[u], g)
            if g or u:
                pool.wait_ge(qklo_done.sem, qklo_done.at(b, m))
            pool.tensor_tensor(rot[:], raw[:, u, :], cos[:], ALU.mult).then_inc(cos_done.sem, 1)
            pool.wait_ge(cos_done.sem, cos_done.at(b, m + 1))
            pool.wait_ge(sin_done.sem, sin_done.at(b, m + 1))
            pool.tensor_tensor(rot[:], rot[:], swp[:], ALU.add).then_inc(rot_done.sem, 1)
            pool.wait_ge(qkhi_done.sem, qkhi_done.at(b, m + 1))
            pool.tensor_tensor(qk_lo[:, u, :], rot[:], qk_hi[:, u, :].bitcast(F32),
                               ALU.subtract).then_inc(qklo_done.sem, 1)

        def o_half(b, g):
            pool.wait_ge(ohi_done.sem, ohi_done.at(b, g + 1))
            pool.tensor_tensor(oT_lo[:, g, :], o[:], oT_hi[:, g, :].bitcast(F32),
                               ALU.subtract).then_inc(olo_done.sem, 1)

        def residual(b):
            pool.wait_ge(res_in.sem, res_in.at(b, 16))
            for s in range(ST):
                pool.tensor_tensor(res[:, s, :], res[:, s, :], bo[:], ALU.add).then_inc(res_done.sem, 1)

        def batch(b, last):
            for g in range(1, G):
                rotate(b, last, 0, g)
                rotate(b, last, 1, g)
                if g > 1:
                    o_half(b, g - 2)
            if not last:
                for k in range(KT):
                    x_half(b, k)
            residual(b)
            o_half(b, G - 2)
            if not last:
                rotate(b, last, 0, 4)
            o_half(b, G - 1)
            if not last:
                rotate(b, last, 1, 4)
            for s in range(ST):
                pool.wait_ge(mv_done.sem, mv_done.at(b, s + 1))
                passed(pool, b, pool_passed)
                pool.tensor_scalar(veps[:, s:s + 1], mv[:, s, 1:2], EPS, None, ALU.add).then_inc(veps_done.sem, 1)
                pool.wait_ge(veps_done.sem, veps_done.at(b, s + 1))
                pool.tensor_tensor(rstd[:, s:s + 1], veps[:, s:s + 1], mhalf[:], ALU.pow).then_inc(rstd_done.sem, 1)

        pool.memset(mhalf[:], -0.5).then_inc(half_done.sem, 1)
        for k in range(KT):
            x_half(0, k, True)
        pool.wait_ge(const_in.sem, 16 * 6)
        rotate(0, False, 0, 0)
        rotate(0, False, 1, 0)
        pool.wait_ge(half_done.sem, 1)
        with pool.Fori(0, B - 1) as b:
            batch(b, False)
        batch(B - 1, True)


NR = 4
BESIDE = {0: [("ctx", 0)], 1: [("qk", 0)], 2: [("e", 0), ("e", 1)], 3: [("e", 2), ("e", 3)],
          4: [("a", 0), ("a", 1)], 5: [("a", 2), ("a", 3)], 6: [("t", 0), ("t", 1)], 7: [("t", 2), ("t", 3)],
          8: [("m", 0)], 9: [("m", 1)], 10: [("m", 2)], 11: [("m", 3)]}


def feed_forward_phase(nc, ctx, d, x1_dram, out):
    def sb(name, shape, dt=F32):
        return ctx.enter_context(nc.sbuf_tensor(name, shape, dt))

    def sem(name, per=0, base=0):
        return Count(ctx.enter_context(nc.semaphore(name)), per, base)

    f_raw = sb("f_raw", [P, NR, 2 * KT * P + E])
    gu_hi = sb("gu_hi", [P, 2, 2, KT, P], F32R)
    gu_lo = sb("gu_lo", [P, 2, 2, KT, P], F32R)
    dn_hi = sb("dn_hi", [P, 2, E], F32R)
    dn_lo = sb("dn_lo", [P, 2, E], F32R)
    c_raw = sb("c_raw", [P, CT, S])
    c_hi = sb("c_hi", [P, CT, S], F32R)
    c_lo = sb("c_lo", [P, CT, S], F32R)
    p_raw = sb("p_raw", [P, 2, CT, DK])
    p_hi = sb("p_hi", [P, 2, CT, DK], F32R)
    p_lo = sb("p_lo", [P, 2, CT, DK], F32R)
    pbias = sb("pbias", [P, 2])
    qk = sb("cqk", [P, 2, S])
    qk_hi = sb("cqk_hi", [P, 2, S], F32R)
    qk_lo = sb("cqk_lo", [P, 2, S], F32R)
    e = sb("e", [P, KT, S])
    att_hi = sb("att_hi", [P, KT, S], F32R)
    att_lo = sb("att_lo", [P, KT, S], F32R)
    emax = sb("emax", [P, KT])
    nemax = sb("nemax", [P, KT])
    esum = sb("esum", [P, KT])
    erec = sb("erec", [P, KT])
    x = sb("x12", [P, ST, E])
    x1T_hi = sb("x1T_hi", [P, KT, S], F32R)
    x1T_lo = sb("x1T_lo", [P, KT, S], F32R)
    x2T_hi = sb("x2T_hi", [P, KT, S], F32R)
    x2T_lo = sb("x2T_lo", [P, KT, S], F32R)
    fin = sb("fin", [P, ST, E])
    th = sb("th", [P, S])
    half = sb("half", [P, S])
    gated = sb("gated", [P, S])
    g_hi = sb("g_hi", [P, 2, S], F32R)
    g_lo = sb("g_lo", [P, 2, S], F32R)
    ident = sb("ident2", [P, P])
    mhalf = sb("mhalf2", [P, 1])
    one = sb("one", [P, 1])
    stats, mv, veps, rstd = ([sb(f"{n}{k}", [P, ST, w]) for k in (2, 3)]
                             for n, w in (("stats", 6), ("mv", 2), ("veps", 1), ("rstd", 1)))

    pg = ctx.enter_context(nc.psum_tensor("pg", [P, S], F32))
    pu = ctx.enter_context(nc.psum_tensor("pu", [P, S], F32))
    pd = ctx.enter_context(nc.psum_tensor("pd", [P, ST, E], F32))
    px = ctx.enter_context(nc.psum_tensor("px", [P, 2, S], F32))

    const_in = sem("const2_in")
    sp_passed, dve_passed, pool_passed = (sem(f"{n}_passed2") for n in ("sp", "dve", "pool"))
    p_hi_done, p_lo_done = sem("p_hi_done"), sem("p_lo_done")
    half_done = sem("half2_done")
    x1_in = sem("x1_in", 16, 16)
    c_in = sem("c_in", 16, 16)
    chi_done, clo_done = sem("chi_done", 1, 1), sem("clo_done", 1, 1)
    qk_full, qk_moved = sem("cqk_full", 2, 2), sem("cqk_moved", 2, 2)
    qkhi_done, qklo_done = sem("cqkhi_done", 2, 2), sem("cqklo_done", 2, 2)
    e_full = sem("e_full", KT, KT)
    emax_done, nemax_done = sem("emax_done", KT, KT), sem("nemax_done", KT, KT)
    e_done = sem("e_done", KT, KT)
    erec_done, att_done = sem("erec_done", KT, KT), sem("att_done", KT, KT)
    a_full = sem("a_full", KT, KT)
    ahi_done, alo_done = sem("ahi_done", KT, KT), sem("alo_done", KT, KT)
    t1_full, t1hi_done, t1lo_done = (sem(n, ST, ST) for n in ("t1_full", "t1hi_done", "t1lo_done"))
    t2_full, t2hi_done, t2lo_done = (sem(n, ST, ST) for n in ("t2_full", "t2hi_done", "t2lo_done"))
    m_full = sem("m_full", ST, ST)
    raw_in = [sem(f"raw_in{n}", 16 * HT // NR) for n in range(NR)]
    guhi_done, gulo_done = sem("guhi_done", HT), sem("gulo_done", HT)
    dnhi_done, dnlo_done = sem("dnhi_done", HT), sem("dnlo_done", HT)
    g_full, u_full, d_full = sem("g_full", HT), sem("u_full", HT), sem("d_full", HT)
    th_done, half_done3, gated_done = sem("th_done", HT), sem("gate_read", HT), sem("gated_done", HT)
    ghi_done, glo_done = sem("ghi_done", HT), sem("glo_done", HT)
    fin_in = sem("fin_in", 16)
    out_done = sem("out_done", 16)
    z_done = [sem("z2_done", ST, ST), sem("z3_done", ST, 1)]
    stats_done, mv_done, veps_done, rstd_done, ln_done = (
        [sem(f"{n}{k}_done", ST, (ST, 0)[k - 2]) for k in (2, 3)] for n in ("stats", "mv", "veps", "rstd", "ln"))

    block = ctx.enter_context(nc.Block())

    @block.sync
    def _(sp):
        def context(b):
            sp.dma_start(c_raw[:], d["cT"][bass.ts(b + 1, P), :]).then_inc(c_in.sem, 16)

        def features(b):
            sp.dma_start(x[:], x1_dram[bass.ts(b + 1, P), :]).then_inc(x1_in.sem, 16)

        def weights(c):
            sp.dma_start(f_raw[:, c % NR, :], d["w_ffn"][c * P:(c + 1) * P, :]).then_inc(raw_in[c % NR].sem, 16)

        def batch(b, last):
            if not last:
                sp.wait_ge(chi_done.sem, chi_done.at(b, 0))
                passed(sp, b, sp_passed)
                sp.wait_ge(clo_done.sem, clo_done.at(b, 0))
                passed(sp, b, sp_passed)
                context(b)
            sp.wait_ge(ln_done[0].sem, ln_done[0].at(b, 0))
            sp.dma_start(fin[:], x[:]).then_inc(fin_in.sem, 16)
            sp.wait_ge(fin_in.sem, fin_in.at(b, 16))
            passed(sp, b, sp_passed)
            if not last:
                sp.wait_ge(t2lo_done.sem, t2lo_done.at(b, 0))
                passed(sp, b, sp_passed)
                features(b)
            for j in range(HT - NR if last else HT):
                sp.wait_ge(gulo_done.sem, gulo_done.at(b, j + 1))
                passed(sp, b, sp_passed)
                sp.wait_ge(dnlo_done.sem, dnlo_done.at(b, j + 1))
                weights((j + NR) % HT)
            sp.wait_ge(ln_done[1].sem, ln_done[1].at(b, ST))
            sp.dma_start(out[bass.ts(b, P), :], fin[:]).then_inc(out_done.sem, 16)
            sp.wait_ge(out_done.sem, out_done.at(b, 16))
            passed(sp, b, sp_passed)

        sp.dma_start(p_raw[:], d["w_ctx"]).then_inc(const_in.sem, 16)
        sp.dma_start(pbias[:], d["bctx"]).then_inc(const_in.sem, 16)
        sp.dma_start(ident[:], d["ident"]).then_inc(const_in.sem, 16)
        context(-1)
        features(-1)
        for c in range(NR):
            weights(c)
        with sp.Fori(0, B - 1) as b:
            batch(b, False)
        batch(B - 1, True)

    @block.tensor
    def _(pe):
        def close(mm, count):
            mm.then_inc(count.sem, 1)

        def three(dst, n, stationary, moving, first=True, final=True):
            for part, (a, c) in enumerate(((0, 0), (1, 0), (0, 1))):
                for k in range(n):
                    mm = pe.matmul(dst, stationary(k)[a], moving(k)[c], start=(first and part == 0 and k == 0),
                                   stop=(final and part == 2 and k == n - 1))
            return mm

        def transposed(b, full, s, bank, src=x):
            for k in range(KT):
                mm = pe.transpose(px[:, bank, k * P:(k + 1) * P], src[:, s, k * P:(k + 1) * P], ident[:])
            close(mm, full)

        def beside(b, kind, n):
            if kind == "qk":
                pe.wait_ge(clo_done.sem, clo_done.at(b, 1))
                pe.wait_ge(chi_done.sem, chi_done.at(b, 1))
                for u in range(2):
                    close(three(px[:, u, :], CT, lambda k: (p_hi[:, u, k, :], p_lo[:, u, k, :]),
                                lambda k: (c_hi[:, k, :], c_lo[:, k, :])), qk_full)
            elif kind == "e":
                if n < 2:
                    pe.wait_ge(qk_moved.sem, qk_moved.at(b, 2))
                    pe.wait_ge(qkhi_done.sem, qkhi_done.at(b, 2))
                    pe.wait_ge(qklo_done.sem, qklo_done.at(b, 2))
                else:
                    pe.wait_ge(e_done.sem, e_done.at(b, n - 1))
                cols = slice(n * P, (n + 1) * P)
                close(three(px[:, n % 2, :], 1, lambda k: (qk_hi[:, 0, cols], qk_lo[:, 0, cols]),
                            lambda k: (qk_hi[:, 1, :], qk_lo[:, 1, :])), e_full)
            elif kind == "a":
                pe.wait_ge(att_done.sem, att_done.at(b, n + 1))
                if n < 2:
                    pe.wait_ge(e_done.sem, e_done.at(b, n + 3))
                else:
                    pe.wait_ge(alo_done.sem, alo_done.at(b, n - 1))
                transposed(b, a_full, n, n % 2, e)
            elif kind == "t":
                if n == 0:
                    pe.wait_ge(x1_in.sem, x1_in.at(b, 16))
                if n < 2:
                    pe.wait_ge(alo_done.sem, alo_done.at(b, n + 3))
                else:
                    pe.wait_ge(t1lo_done.sem, t1lo_done.at(b, n - 1))
                transposed(b, t1_full, n, n % 2)
            elif kind == "m":
                if n == 0:
                    pe.wait_ge(ahi_done.sem, ahi_done.at(b, KT))
                    pe.wait_ge(alo_done.sem, alo_done.at(b, KT))
                if n < 2:
                    pe.wait_ge(t1lo_done.sem, t1lo_done.at(b, 3 + n))
                else:
                    pe.wait_ge(z_done[0].sem, z_done[0].at(b, n - 1))
                cols = slice(n * P, (n + 1) * P)
                close(three(px[:, n % 2, :], KT, lambda k: (x1T_hi[:, k, cols], x1T_lo[:, k, cols]),
                            lambda k: (att_hi[:, k, :], att_lo[:, k, :])), m_full)
            elif kind == "u":
                for s in range(ST):
                    pe.wait_ge(ln_done[0].sem, ln_done[0].at(b, s + 1))
                    if s < 2:
                        pe.wait_ge(z_done[0].sem, z_done[0].at(b, s + 3))
                    else:
                        pe.wait_ge(t2lo_done.sem, t2lo_done.at(b, s - 1))
                    transposed(b, t2_full, s, s % 2)

        def hidden(b, j, u):
            if u == 0:
                pe.wait_ge(guhi_done.sem, guhi_done.at(b, j + 1))
                pe.wait_ge(gulo_done.sem, gulo_done.at(b, j + 1))
                if j == 0:
                    pe.wait_ge(t2hi_done.sem, t2hi_done.at(b, 0))
                    pe.wait_ge(t2lo_done.sem, t2lo_done.at(b, 0))
                else:
                    pe.wait_ge(half_done3.sem, half_done3.at(b, j))
            elif j:
                pe.wait_ge(gated_done.sem, gated_done.at(b, j))
            close(three((pg, pu)[u][:], KT, lambda k: (gu_hi[:, j % 2, u, k, :], gu_lo[:, j % 2, u, k, :]),
                        lambda k: (x2T_hi[:, k, :], x2T_lo[:, k, :])), (g_full, u_full)[u])

        def down(b, j):
            if j == 0:
                pe.wait_ge(z_done[1].sem, z_done[1].at(b, 0))
            pe.wait_ge(dnhi_done.sem, dnhi_done.at(b, j + 1))
            pe.wait_ge(dnlo_done.sem, dnlo_done.at(b, j + 1))
            pe.wait_ge(ghi_done.sem, ghi_done.at(b, j + 1))
            pe.wait_ge(glo_done.sem, glo_done.at(b, j + 1))
            for s in range(ST):
                cols = slice(s * P, (s + 1) * P)
                mm = three(pd[:, s, :], 1, lambda k: (g_hi[:, j % 2, cols], g_lo[:, j % 2, cols]),
                           lambda k: (dn_hi[:, j % 2, :], dn_lo[:, j % 2, :]), j == 0, j == HT - 1)
            close(mm, d_full)

        def batch(b, last):
            for j in range(HT):
                hidden(b, j, 0)
                hidden(b, j, 1)
                if not last:
                    for kind, n in BESIDE.get(j, []):
                        beside(b, kind, n)
                    if j == HT - 1:
                        beside(b, "u", 0)
                if j:
                    down(b, j - 1)
            down(b, HT - 1)

        pe.wait_ge(p_hi_done.sem, 1)
        pe.wait_ge(p_lo_done.sem, 1)
        pe.wait_ge(const_in.sem, 48)
        for steps in BESIDE.values():
            for kind, n in steps:
                beside(-1, kind, n)
        beside(-1, "u", 0)
        with pe.Fori(0, B - 1) as b:
            batch(b, False)
        batch(B - 1, True)

    @block.scalar
    def _(act):
        def gu_half(b, j):
            act.wait_ge(raw_in[j % NR].sem, raw_in[j % NR].at(b, 16 * (j // NR + 1)))
            if j >= 2:
                act.wait_ge(u_full.sem, u_full.at(b, j - 1))
            act.copy(gu_hi[:, j % 2, :, :, :].rearrange("p u k m -> p (u k m)"),
                     f_raw[:, j % NR, 0:2 * KT * P]).then_inc(guhi_done.sem, 1)

        def dn_half(b, j):
            if j >= 2:
                act.wait_ge(d_full.sem, d_full.at(b, j - 1))
            act.copy(dn_hi[:, j % 2, :], f_raw[:, j % NR, 2 * KT * P:]).then_inc(dnhi_done.sem, 1)

        def t_half(b, full, done, dst, s):
            act.wait_ge(full.sem, full.at(b, s + 1))
            act.copy(dst[:, :, s * P:(s + 1) * P], px[:, s % 2, :].rearrange("p (k m) -> p k m", m=P)).then_inc(done.sem, 1)

        def beside(b, steps):
            for kind, n in steps:
                if kind == "ctx":
                    act.wait_ge(c_in.sem, c_in.at(b, 16))
                    act.copy(c_hi[:].rearrange("p k s -> p (k s)"), c_raw[:].rearrange("p k s -> p (k s)")).then_inc(chi_done.sem, 1)
                elif kind == "qk":
                    for u in range(2):
                        act.wait_ge(qk_full.sem, qk_full.at(b, u + 1))
                        act.activation(qk[:, u, :], px[:, u, :], ACT.Identity, bias=pbias[:, u:u + 1]).then_inc(qk_moved.sem, 1)
                    for u in range(2):
                        act.wait_ge(qk_moved.sem, qk_moved.at(b, u + 1))
                        act.copy(qk_hi[:, u, :], qk[:, u, :]).then_inc(qkhi_done.sem, 1)
                elif kind == "e":
                    act.wait_ge(nemax_done.sem, nemax_done.at(b, n + 1))
                    act.activation(e[:, n, :], px[:, n % 2, :], ACT.Exp, bias=nemax[:, n:n + 1], scale=1.0,
                                   accum_out=esum[:, n:n + 1]).then_inc(e_done.sem, 1)
                elif kind == "a":
                    t_half(b, a_full, ahi_done, att_hi, n)
                elif kind == "t":
                    t_half(b, t1_full, t1hi_done, x1T_hi, n)

        def transposed(b):
            for s in range(ST):
                t_half(b, t2_full, t2hi_done, x2T_hi, s)

        def batch(b, last):
            for j in range(HT):
                act.wait_ge(g_full.sem, g_full.at(b, j + 1))
                if j:
                    act.wait_ge(half_done3.sem, half_done3.at(b, j))
                act.activation(th[:], pg[:], ACT.Tanh, scale=0.5).then_inc(th_done.sem, 1)
                more = j < HT - 1 or not last
                if more:
                    gu_half(b, j + 1)
                if j == HT - 1 and not last:
                    transposed(b)
                act.wait_ge(gated_done.sem, gated_done.at(b, j + 1))
                if j >= 2:
                    act.wait_ge(d_full.sem, d_full.at(b, j - 1))
                act.copy(g_hi[:, j % 2, :], gated[:]).then_inc(ghi_done.sem, 1)
                if not last:
                    beside(b, BESIDE.get(j, []))
                if more:
                    dn_half(b, j + 1)

        act.wait_ge(const_in.sem, 48)
        act.copy(p_hi[:].rearrange("p u k m -> p (u k m)"), p_raw[:].rearrange("p u k m -> p (u k m)")).then_inc(p_hi_done.sem, 1)
        beside(-1, BESIDE[0])
        gu_half(0, 0)
        dn_half(0, 0)
        for j in list(BESIDE)[1:]:
            beside(-1, BESIDE[j])
        transposed(-1)
        with act.Fori(0, B - 1) as b:
            batch(b, False)
        batch(B - 1, True)

    @block.vector
    def _(dve):
        def gu_half(b, j):
            dve.wait_ge(guhi_done.sem, guhi_done.at(b, j + 1))
            if j >= 2:
                dve.wait_ge(u_full.sem, u_full.at(b, j - 1))
            flat = "p u k m -> p (u k m)"
            dve.tensor_tensor(gu_lo[:, j % 2, :, :, :].rearrange(flat), f_raw[:, j % NR, 0:2 * KT * P],
                              gu_hi[:, j % 2, :, :, :].rearrange(flat).bitcast(F32), ALU.subtract).then_inc(gulo_done.sem, 1)

        def dn_half(b, j):
            dve.wait_ge(dnhi_done.sem, dnhi_done.at(b, j + 1))
            if j >= 2:
                dve.wait_ge(d_full.sem, d_full.at(b, j - 1))
            dve.tensor_tensor(dn_lo[:, j % 2, :], f_raw[:, j % NR, 2 * KT * P:], dn_hi[:, j % 2, :].bitcast(F32),
                              ALU.subtract).then_inc(dnlo_done.sem, 1)

        def t_half(b, hi_done, done, hi, lo, s):
            cols = slice(s * P, (s + 1) * P)
            dve.wait_ge(hi_done.sem, hi_done.at(b, s + 1))
            dve.tensor_tensor(lo[:, :, cols], px[:, s % 2, :].rearrange("p (k m) -> p k m", m=P),
                              hi[:, :, cols].bitcast(F32), ALU.subtract).then_inc(done.sem, 1)

        def summed(b, which, full, src, dst, s, n):
            z, st, m = z_done[which], stats_done[which], mv_done[which]
            dve.wait_ge(full.sem, full.at(b, n))
            dve.tensor_tensor(dst[:, s, :], src, dst[:, s, :], ALU.add).then_inc(z.sem, 1)
            dve.wait_ge(z.sem, z.at(b, s + 1))
            dve.bn_stats(stats[which][:, s, :], dst[:, s, :]).then_inc(st.sem, 1)
            dve.wait_ge(st.sem, st.at(b, s + 1))
            passed(dve, b, dve_passed)
            dve.bn_aggr(mv[which][:, s, :], stats[which][:, s, :]).then_inc(m.sem, 1)

        def normalized(b, which, dst, s):
            dve.wait_ge(rstd_done[which].sem, rstd_done[which].at(b, s + 1))
            dve.tensor_scalar(dst[:, s, :], dst[:, s, :], mv[which][:, s, 0:1], rstd[which][:, s, :],
                              ALU.subtract, ALU.mult).then_inc(ln_done[which].sem, 1)

        def beside(b, steps):
            for kind, n in steps:
                if kind == "e":
                    dve.wait_ge(e_full.sem, e_full.at(b, n + 1))
                    dve.reduce_max(emax[:, n:n + 1], px[:, n % 2, :], AX.X).then_inc(emax_done.sem, 1)
                    dve.wait_ge(emax_done.sem, emax_done.at(b, n + 1))
                    dve.tensor_scalar(nemax[:, n:n + 1], emax[:, n:n + 1], -1.0, None, ALU.mult).then_inc(nemax_done.sem, 1)
                elif kind == "a":
                    t_half(b, ahi_done, alo_done, att_hi, att_lo, n)
                elif kind == "t":
                    t_half(b, t1hi_done, t1lo_done, x1T_hi, x1T_lo, n)
                elif kind == "m":
                    summed(b, 0, m_full, px[:, n % 2, :], x, n, n + 1)
            for kind, n in steps:
                if kind == "e":
                    dve.wait_ge(e_done.sem, e_done.at(b, n + 1))
                    dve.reciprocal(erec[:, n:n + 1], esum[:, n:n + 1]).then_inc(erec_done.sem, 1)
                    dve.wait_ge(erec_done.sem, erec_done.at(b, n + 1))
                    dve.tensor_scalar(e[:, n, :], e[:, n, :], erec[:, n:n + 1], None, ALU.mult).then_inc(att_done.sem, 1)

        def after(b, steps):
            for kind, n in steps:
                if kind == "m":
                    normalized(b, 0, x, n)

        def transposed(b):
            for s in range(ST):
                t_half(b, t2hi_done, t2lo_done, x2T_hi, x2T_lo, s)

        def batch(b, last):
            for j in range(HT):
                dve.wait_ge(th_done.sem, th_done.at(b, j + 1))
                if j:
                    dve.wait_ge(gated_done.sem, gated_done.at(b, j))
                dve.scalar_tensor_tensor(half[:], th[:], 1.0, pg[:], ALU.add, ALU.mult).then_inc(half_done3.sem, 1)
                more = j < HT - 1 or not last
                if more:
                    gu_half(b, j + 1)
                dve.wait_ge(u_full.sem, u_full.at(b, j + 1))
                dve.wait_ge(half_done3.sem, half_done3.at(b, j + 1))
                if j:
                    dve.wait_ge(glo_done.sem, glo_done.at(b, j))
                dve.scalar_tensor_tensor(gated[:], half[:], 0.5, pu[:], ALU.mult, ALU.mult).then_inc(gated_done.sem, 1)
                if j == HT - 1 and not last:
                    transposed(b)
                if not last:
                    beside(b, BESIDE.get(j, []))
                if more:
                    dn_half(b, j + 1)
                if not last:
                    after(b, BESIDE.get(j, []))
            dve.wait_ge(fin_in.sem, fin_in.at(b, 16))
            for s in range(ST):
                summed(b, 1, d_full, pd[:, s, :], fin, s, HT)
            for s in range(ST):
                normalized(b, 1, fin, s)

        dve.memset(one[:], 1.0).then_inc(z_done[1].sem, 1)
        dve.wait_ge(p_hi_done.sem, 1)
        flat = "p u k m -> p (u k m)"
        dve.tensor_tensor(p_lo[:].rearrange(flat), p_raw[:].rearrange(flat), p_hi[:].rearrange(flat).bitcast(F32),
                          ALU.subtract).then_inc(p_lo_done.sem, 1)
        gu_half(0, 0)
        dn_half(0, 0)
        for steps in BESIDE.values():
            beside(-1, steps)
            after(-1, steps)
        transposed(-1)
        with dve.Fori(0, B - 1) as b:
            batch(b, False)
        batch(B - 1, True)

    @block.gpsimd
    def _(pool):
        def root(b, which, s):
            pool.wait_ge(mv_done[which].sem, mv_done[which].at(b, s + 1))
            passed(pool, b, pool_passed)
            pool.tensor_scalar(veps[which][:, s, :], mv[which][:, s, 1:2], EPS, None, ALU.add).then_inc(veps_done[which].sem, 1)
            pool.wait_ge(veps_done[which].sem, veps_done[which].at(b, s + 1))
            pool.tensor_tensor(rstd[which][:, s, :], veps[which][:, s, :], mhalf[:], ALU.pow).then_inc(rstd_done[which].sem, 1)

        def beside(b, steps):
            for kind, n in steps:
                if kind == "ctx":
                    pool.wait_ge(chi_done.sem, chi_done.at(b, 1))
                    pool.tensor_tensor(c_lo[:].rearrange("p k s -> p (k s)"), c_raw[:].rearrange("p k s -> p (k s)"),
                                       c_hi[:].rearrange("p k s -> p (k s)").bitcast(F32), ALU.subtract).then_inc(clo_done.sem, 1)
                elif kind == "qk":
                    for u in range(2):
                        pool.wait_ge(qkhi_done.sem, qkhi_done.at(b, u + 1))
                        pool.tensor_tensor(qk_lo[:, u, :], qk[:, u, :], qk_hi[:, u, :].bitcast(F32),
                                           ALU.subtract).then_inc(qklo_done.sem, 1)
                elif kind == "m":
                    root(b, 0, n)

        def batch(b, last):
            for j in range(HT):
                pool.wait_ge(ghi_done.sem, ghi_done.at(b, j + 1))
                if j >= 2:
                    pool.wait_ge(d_full.sem, d_full.at(b, j - 1))
                pool.tensor_tensor(g_lo[:, j % 2, :], gated[:], g_hi[:, j % 2, :].bitcast(F32),
                                   ALU.subtract).then_inc(glo_done.sem, 1)
                if not last:
                    beside(b, BESIDE.get(j, []))
            for s in range(ST):
                root(b, 1, s)

        pool.memset(mhalf[:], -0.5).then_inc(half_done.sem, 1)
        pool.wait_ge(half_done.sem, 1)
        for steps in BESIDE.values():
            beside(-1, steps)
        with pool.Fori(0, B - 1) as b:
            batch(b, False)
        batch(B - 1, True)


def layouts(a):
    def tiles(w):
        return w.reshape(-1, P, w.shape[1]).transpose(1, 0, 2)

    pos = np.arange(S, dtype=np.float32)
    theta = np.power(np.float32(10000.0), -np.arange(0, D, 2, dtype=np.float32) / D)
    angle = pos[None, :] * np.tile(np.repeat(theta, 2), 4)[:, None]
    sign = np.tile(np.array([-1.0, 1.0], np.float32), P // 2)[:, None]
    mask = np.zeros((P, S), np.float32)
    mask[:, S - P:] = np.triu(np.full((P, P), MASKED, np.float32), 1)
    x = a["x"]
    qkv = np.stack([tiles(a[f"L0_attn_W{n}"]).reshape(P, KT, G, P) for n in "qkv"])
    return {
        "xT": x.reshape(B, S, KT, P).transpose(0, 3, 2, 1).reshape(B * P, KT * S),
        "x": x.reshape(B, ST, P, E).transpose(0, 2, 1, 3).reshape(B * P, ST * E),
        "w_qkv": qkv.transpose(3, 1, 0, 2, 4).reshape(G * P, 3 * KT * P),
        "wo": tiles(a["L0_attn_Wo"]).reshape(P, KT * E),
        "bcol": np.stack([a[f"L0_attn_b{n}"].reshape(G, P) for n in "qkv"]).transpose(2, 1, 0).reshape(P, 3 * G),
        "bo": np.broadcast_to(a["L0_attn_bo"], (P, E)),
        "cos": np.cos(angle), "sin": np.sin(angle) * sign,
        "mask": mask, "ident": np.eye(P, dtype=np.float32),
        "cT": a["ctx_1024"].reshape(B, S, CT, P).transpose(0, 3, 2, 1).reshape(B * P, CT * S),
        "w_ctx": np.stack([tiles(a[f"L0_xattn_W{n}"].T) for n in "qk"]).transpose(1, 0, 2, 3).reshape(P, 2 * CT * DK),
        "bctx": np.stack([a["L0_xattn_bq"], a["L0_xattn_bk"]]).T,
        "w_ffn": np.concatenate(
            [w.reshape(HT, P, KT, P).transpose(0, 3, 2, 1).reshape(HT, P, KT * P)
             for w in (a["L0_ffn_w_gate"], a["L0_ffn_w_up"])] +
            [a["L0_ffn_w_down"].T.reshape(HT, P, E)], axis=2).reshape(HT * P, 2 * KT * P + E),
    }


def decoder_layer(nc, d, out):
    x1_dram = nc.dram_tensor("x1_scratch", (B * P, ST * E), F32, kind="Internal").ap()
    with ExitStack() as ctx:
        attention_phase(nc, ctx, d, x1_dram)
    with ExitStack() as ctx:
        feed_forward_phase(nc, ctx, d, x1_dram, out)


def kernel(**inputs):
    import concourse.bacc as bacc
    from concourse.bass_utils import run_bass_kernel_spmd

    nc = bacc.Bacc("TRN2", target_bir_lowering=False, num_devices=1)
    arrays, d = {}, {}
    for name, a in layouts({k: np.asarray(v) for k, v in inputs.items()}).items():
        a = np.ascontiguousarray(a)
        arrays[f"in_{name}"] = a
        d[name] = nc.dram_tensor(f"in_{name}", a.shape, F32, kind="ExternalInput").ap()
    out = nc.dram_tensor("out", (B * P, ST * E), F32, kind="ExternalOutput").ap()
    decoder_layer(nc, d, out)
    got = run_bass_kernel_spmd(nc, [arrays], core_ids=[0]).results[0]["out"]
    return got.reshape(B, P, ST, E).transpose(0, 2, 1, 3).reshape(B, S, E)
```

```python
from contextlib import ExitStack

import numpy as np

import concourse.bass as bass
from concourse import mybir

F32 = mybir.dt.float32
F32R = mybir.dt.float32r
ALU = mybir.AluOpType
ACT = mybir.ActivationFunctionType
AX = mybir.AxisListType

P = 128
B, S, E = 4, 512, 512
H, D = 16, 32
CTX, DK = 256, 128
HID = 2048
ST = S // P
KT = E // P
CT = CTX // P
G = H // 4
TILES = 16
PROBS = 4
SLOTS = G * TILES
HT = HID // P
EPS = 1e-5
MASKED = -1e30
LAG = 3
ROW = (3, 2, 0, 1)
SWAP = [i ^ 1 for i in range(32)]


FIRST = TILES + 3
PLAN = {("r", 0): 21, ("v", 2): 22, ("t", 2): 27, ("q", 3): 27, ("k", 3): 31, ("v", 3): 35, ("r", 1): 39,
        ("t", 3): 41, ("q", 4): 44, ("k", 4): 48, ("v", 4): 52, ("r", 2): 56, ("t", 4): 58, ("q", 5): 60,
        ("k", 5): 64, ("r", 3): 68, ("v", 5): 69, ("t", 5): 74, ("q", 6): 75, ("k", 6): 79}
SPLIT_X = (39, 40, 41, 42)
OUTPUT = {71: 0, 73: 1, 75: 2, 77: 3}


def plan(turn):
    if turn == "first":
        return {(kind, g - G): t - SLOTS for (kind, g), t in PLAN.items() if t >= SLOTS and kind != "r"}
    return {(kind, g): t for (kind, g), t in PLAN.items() if turn == "loop" or g < G}


def halves(turn, later):
    keys = [(("q", 1), PLAN["q", G + 1] - SLOTS)] + list(plan("first").items()) + list(plan("loop").items())
    keys = [((kind, g), t + later) for (kind, g), t in keys if kind in "qk" and (turn != "last" or g < G)]
    return [(key, t) for key, t in keys if t in span(turn)]


def span(turn):
    return range(FIRST) if turn == "first" else range(FIRST, FIRST + SLOTS)


class Count:

    def __init__(self, sem, per, base=0):
        self.sem, self.per, self.base = sem, per, base

    def at(self, b, k):
        return b * self.per + (self.base + k)


def passed(eng, b, count):
    if not isinstance(b, int):
        eng.sem_inc(count.sem, 1)


def attention_phase(nc, ctx, d, x1_dram):
    def sb(name, shape, dt=F32):
        return ctx.enter_context(nc.sbuf_tensor(name, shape, dt))

    def sem(name, per=0, base=0):
        return Count(ctx.enter_context(nc.semaphore(name)), per, base)

    w_hi = sb("w_hi", [P, 3 * G, KT, P], F32R)
    w_lo = sb("w_lo", [P, 3 * G, KT, P], F32R)
    wo_hi = sb("wo_hi", [P, KT, E], F32R)
    wo_lo = sb("wo_lo", [P, KT, E], F32R)
    x_raw = sb("x_raw", [P, KT, S])
    xT_hi = sb("xT_hi", [P, KT, S], F32R)
    xT_lo = sb("xT_lo", [P, KT, S], F32R)
    res = sb("res", [P, ST, E])
    qs = sb("qs", [P, 2, 4, S], F32R)
    ks = sb("ks", [P, 2, 4, S], F32R)
    raw = sb("raw", [P, 2, S])
    swp = sb("swp", [P, S])
    rot = sb("rot", [P, S])
    qk_hi = sb("qk_hi", [P, 2, S], F32R)
    qk_lo = sb("qk_lo", [P, 2, S], F32R)
    vT = sb("vT", [P, S])
    vg = sb("vg", [P, 2, ST, P])
    prob = sb("prob", [P, PROBS, S])
    pT = sb("pT", [P, 4, 10 * P])
    nmax = sb("nmax", [P, 2, TILES])
    rsum = sb("rsum", [P, 2, ST, 4])
    rrec = sb("rrec", [P, TILES])
    rb = sb("rb", [P, ST, 4, D])
    o = sb("heads", [P, S])
    oT_hi = sb("oT_hi", [P, G, S], F32R)
    oT_lo = sb("oT_lo", [P, G, S], F32R)
    cos = sb("cos", [P, S])
    sin = sb("sin", [P, S])
    mask = sb("mask", [P, S])
    ident = sb("ident", [P, P])
    bcol = sb("bcol", [P, 3 * G])
    bo = sb("bo", [P, E])
    stats = sb("stats", [P, ST, 6])
    mv = sb("mv", [P, ST, 2])
    rstd = sb("rstd", [P, ST])
    veps = sb("veps", [P, ST])
    mhalf = sb("mhalf", [P, 1])

    def w_stage(c):
        if c < G - 1:
            return pT[:].rearrange("p h n -> p (h n)")[:, 3 * KT * P * c:3 * KT * P * (c + 1)]
        return res[:].rearrange("p s e -> p (s e)")[:, 0:3 * KT * P if c < G else KT * E]

    pj = ctx.enter_context(nc.psum_tensor("pj", [P, 2, S], F32))
    ps = ctx.enter_context(nc.psum_tensor("ps", [P, 2, S], F32))
    pa = ctx.enter_context(nc.psum_tensor("pa", [P, S], F32))
    pb = ctx.enter_context(nc.psum_tensor("pb", [P, S], F32))
    pc = ctx.enter_context(nc.psum_tensor("pc", [P, S], F32))
    pv = ctx.enter_context(nc.psum_tensor("pv", [P, S], F32))

    scratch = nc.dram_tensor("qk_scratch", (4 * P, S), F32, kind="Internal").ap()

    WEIGHTED = [(0, 0, 1, 6), (0, 1, 1, 8), (1, 1, 1, 9), (0, 2, 2, 0), (1, 2, 2, 2), (2, 2, 2, 4), (3, 3, 1, 7)]

    const_in = sem("const_in")
    sp_passed, dve_passed, pool_passed = (sem(f"{n}_passed") for n in ("sp", "dve", "pool"))
    w_in = [sem(f"w_in{c}") for c in range(G + 1)]
    w_hi_done, w_lo_done = sem("w_hi_done"), sem("w_lo_done")
    x_in = sem("x_in", 16, 16)
    xhi_done = sem("xhi_done", KT, KT)
    xlo_done = sem("xlo_done", KT, KT)
    pj_full = sem("pj_full", len(PLAN), 10)
    pj_moved = sem("pj_moved", len(PLAN), 10)
    swap_done = sem("swap_done", 2 * G, 2)
    sin_done = sem("sin_done", 2 * G, 2)
    cos_done = sem("cos_done", 2 * G, 2)
    rot_done = sem("rot_done", 2 * G, 2)
    qkhi_done = sem("qkhi_done", 2 * G, 2)
    qklo_done = sem("qklo_done", 2 * G, 2)
    stored = sem("stored", 64 * G, 64)
    stacked = sem("stacked", 128 * G, 128)
    s_done = sem("s_done", SLOTS)
    max_done = sem("max_done", SLOTS)
    exp_done = sem("exp_done", SLOTS)
    t_done = sem("t_done", SLOTS)
    a_moved, b_moved, c_moved = (sem(f"{n}_moved", H) for n in "abc")
    rec_done = sem("rec_done", G)
    rb_done = sem("rb_done", G)
    av_done = sem("av_done", G)
    o_done = sem("o_done", G)
    ohi_done, olo_done = sem("ohi_done", G), sem("olo_done", G)
    wo_done = sem("wo_done", ST)
    res_in = sem("res_in", 16)
    res_done = sem("res_done", ST)
    z_done = sem("z_done", ST)
    stats_done = sem("stats_done", ST)
    mv_done = sem("mv_done", ST)
    rstd_done = sem("rstd_done", ST)
    veps_done = sem("veps_done", ST)
    x1_done = sem("x1_done", ST)
    x1_stored = sem("x1_stored", 16, 16)
    half_done = sem("half_done")


    before = [("q", 0), ("k", 0), ("v", 0), ("t", 0), ("q", 1)] + list(plan("first"))
    USES = {turn: {key: n for n, key in enumerate(plan(turn))} | {key: n - len(before) for n, key in enumerate(before)}
            for turn in ("loop", "last")}
    USES["first"] = USES["loop"]

    def wait_moved(eng, b, turn, kind, g):
        eng.wait_ge(pj_moved.sem, pj_moved.at(b, USES[turn][kind, g] + 1))

    block = ctx.enter_context(nc.Block())

    @block.sync
    def _(sp):
        sp.dma_start(w_stage(0), d["w_qkv"][0:P, :]).then_inc(w_in[0].sem, 16)
        sp.dma_start(x_raw[:], d["xT"][0:P, :]).then_inc(x_in.sem, 16)
        for dst, name in ((bcol, "bcol"), (cos, "cos"), (sin, "sin"), (ident, "ident"), (mask, "mask")):
            sp.dma_start(dst[:], d[name]).then_inc(const_in.sem, 16)
        for g in range(1, G):
            sp.dma_start(w_stage(g), d["w_qkv"][g * P:(g + 1) * P, :]).then_inc(w_in[g].sem, 16)
        sp.dma_start(bo[:], d["bo"]).then_inc(const_in.sem, 16)

        def stack(b, g):
            for u in range(2):
                m = 2 * (g - 1) + u
                rows = 2 * u * P
                if g and not u:
                    sp.wait_ge(stacked.sem, stacked.at(b, 128 * (g - 1)))
                    passed(sp, b, sp_passed)
                sp.wait_ge(qkhi_done.sem, qkhi_done.at(b, m + 1))
                sp.dma_start(scratch[rows // 2:rows // 2 + P, :], qk_hi[:, u, :].bitcast(F32)).then_inc(stored.sem, 16)
                sp.wait_ge(qklo_done.sem, qklo_done.at(b, m + 1))
                sp.dma_start(scratch[2 * P + u * P:3 * P + u * P, :], qk_lo[:, u, :].bitcast(F32)).then_inc(stored.sem, 16)
                sp.wait_ge(stored.sem, stored.at(b, 32 * (m + 1)))
                passed(sp, b, sp_passed)
                if g >= 2:
                    sp.wait_ge(s_done.sem, s_done.at(b, TILES * (g - 1)))
                for j in range(4):
                    lo = j // 2 if u == 0 else j % 2
                    src = scratch[2 * P * lo + u * P:2 * P * lo + u * P + P, :]
                    dst = qs if u == 0 else ks
                    sp.dma_start(dst[D * j:D * j + D, g % 2, :, :].bitcast(F32),
                                 src.rearrange("(r d) s -> d r s", d=D)).then_inc(stacked.sem, 16)

        def turn(b, kind):
            stack(b, 2)
            if kind == "loop":
                sp.wait_ge(xhi_done.sem, xhi_done.at(b, 0))
                passed(sp, b, sp_passed)
                sp.wait_ge(xlo_done.sem, xlo_done.at(b, 0))
                passed(sp, b, sp_passed)
                sp.dma_start(x_raw[:], d["xT"][bass.ts(b + 1, P), :]).then_inc(x_in.sem, 16)
            sp.wait_ge(x1_stored.sem, x1_stored.at(b, 0))
            passed(sp, b, sp_passed)
            sp.dma_start(res[:], d["x"][bass.ts(b, P), :]).then_inc(res_in.sem, 16)
            for g in range(3, G + 2 if kind == "loop" else G):
                stack(b, g)
            sp.wait_ge(x1_done.sem, x1_done.at(b, ST))
            passed(sp, b, sp_passed)
            sp.dma_start(x1_dram[bass.ts(b, P), :], res[:]).then_inc(x1_stored.sem, 16)

        sp.sem_inc(x1_stored.sem, 16)
        stack(0, 0)
        sp.wait_ge(w_hi_done.sem, G)
        sp.wait_ge(w_lo_done.sem, G)
        sp.dma_start(w_stage(G), d["wo"]).then_inc(w_in[G].sem, 16)
        stack(0, 1)
        sp.wait_ge(w_hi_done.sem, G + 1)
        sp.wait_ge(w_lo_done.sem, G + 1)
        with sp.Fori(0, B - 1) as b:
            turn(b, "loop")
        turn(B - 1, "last")
        sp.wait_ge(x1_stored.sem, x1_stored.at(B - 1, 16))

    @block.tensor
    def _(pe):
        def open_pj(b, turn, key):
            n = USES[turn][key]
            if n >= 2 - len(before):
                pe.wait_ge(pj_moved.sem, pj_moved.at(b, n - 1))
            return n % 2

        def close(mm, count):
            mm.then_inc(count.sem, 1)

        def projection(b, turn, kind, g, k):
            if k == 0:
                open_pj(b, turn, (kind, g))
                if kind == "q" and g == G:
                    pe.wait_ge(xhi_done.sem, xhi_done.at(b, KT))
                    pe.wait_ge(xlo_done.sem, xlo_done.at(b, KT))
            if kind == "q" and g == 0:
                pe.wait_ge(xhi_done.sem, k + 1)
                pe.wait_ge(xlo_done.sem, k + 1)
            bank = USES[turn][kind, g] % 2
            tile = 3 * (g % G) + "qkv".index(kind)
            for part, (w, x) in enumerate(((w_hi, xT_hi), (w_lo, xT_hi), (w_hi, xT_lo))):
                mm = pe.matmul(pj[:, bank, :], w[:, tile, k, :], x[:, k, :],
                               start=(part == 0 and k == 0), stop=(part == 2 and k == KT - 1))
            if k == KT - 1:
                close(mm, pj_full)

        def values(b, turn, g):
            bank = open_pj(b, turn, ("t", g))
            wait_moved(pe, b, turn, "v", g)
            for s in range(ST):
                mm = pe.transpose(pj[:, bank, s * P:(s + 1) * P], vT[:, s * P:(s + 1) * P], ident[:])
            close(mm, pj_full)

        def recips(b, turn, g):
            bank = open_pj(b, turn, ("r", g))
            pe.wait_ge(rb_done.sem, rb_done.at(b, g + 1))
            for s in range(ST):
                mm = pe.transpose(pj[:, bank, s * P:(s + 1) * P], rb[:, s, :, :].rearrange("p r d -> p (r d)"), ident[:])
            close(mm, pj_full)

        def scores(b, t):
            g, r, s = t // TILES, t % TILES // ST, ROW[t % ST]
            if t % TILES == 0:
                pe.wait_ge(stacked.sem, stacked.at(b, 128 * g))
            if t >= 2:
                pe.wait_ge(max_done.sem, max_done.at(b, t - 1))
            w = max(2, s + 1) * P
            close(pe.matmul(ps[:, t % 2, 0:w], qs[:, g % 2, r, s * P:(s + 1) * P], ks[:, g % 2, r, 0:w],
                            start=True, stop=True), s_done)

        def transposes(b, t):
            h, s = t // ST, ROW[t % ST]
            pe.wait_ge(exp_done.sem, exp_done.at(b, t + 1))
            if h and s:
                moved = (c_moved, b_moved, a_moved)[s - 1]
                pe.wait_ge(moved.sem, moved.at(b, h))
            for k in range(s + 1):
                dst = (pb, pc, pb, pa)[s]
                c = (k if s else 3) * P
                mm = pe.transpose(dst[:, c:c + P], prob[:, t % PROBS, k * P:(k + 1) * P], ident[:])
            close(mm, t_done)

        def weighted(b, turn, g):
            for moved in (a_moved, b_moved, c_moved):
                pe.wait_ge(moved.sem, moved.at(b, 4 * g + 4))
            wait_moved(pe, b, turn, "t", g)
            if g:
                pe.wait_ge(o_done.sem, o_done.at(b, g))
            for k, s, n, at in WEIGHTED:
                for r in range(4):
                    mm = pe.matmul(pv[D * r:D * r + D, s * P:(s + n) * P], vg[:, g % 2, k, D * r:D * r + D],
                                   pT[:, r, at * P:(at + n) * P], start=(k == 0), stop=(k == s + n - 1),
                                   tile_position=(0, D * r))
            close(mm, av_done)

        def output(b, s, part):
            if part == 0:
                if s == 0:
                    pe.wait_ge(w_hi_done.sem, G + 1)
                    pe.wait_ge(w_lo_done.sem, G + 1)
                    pe.wait_ge(ohi_done.sem, ohi_done.at(b, G))
                    pe.wait_ge(olo_done.sem, olo_done.at(b, G))
                else:
                    pe.wait_ge(z_done.sem, z_done.at(b, s))
            for k in range(KT // 2 * part, KT // 2 * (part + 1)):
                for p, (w, x) in enumerate(((wo_hi, oT_hi), (wo_lo, oT_hi), (wo_hi, oT_lo))):
                    mm = pe.matmul(pv[:], x[:, k, s * P:(s + 1) * P], w[:, k, :],
                                   start=(p == 0 and k == 0), stop=(p == 2 and k == KT - 1))
            if part:
                close(mm, wo_done)

        def slots(b, turn):
            end = SLOTS if turn == "last" else FIRST + SLOTS
            for t in span(turn):
                if t < end:
                    scores(b, t)
                for (kind, g), first in plan(turn).items():
                    if kind in "qkv" and first <= t < first + 4:
                        projection(b, turn, kind, g, t - first)
                    elif kind == "t" and t == first:
                        values(b, turn, g)
                    elif kind == "r" and t == first:
                        recips(b, turn, g)
                if LAG <= t < end + LAG:
                    transposes(b, t - LAG)
                if turn != "first" and t % TILES == 3 and t // TILES <= G:
                    weighted(b, turn, t // TILES - 1)
                if turn != "first":
                    for part in range(2):
                        if t - part in OUTPUT:
                            output(b, OUTPUT[t - part], part)

        def load_wait(c):
            pe.wait_ge(w_hi_done.sem, c)
            pe.wait_ge(w_lo_done.sem, c)

        load_wait(1)
        for kind in "qkv":
            for k in range(KT):
                projection(0, "first", kind, 0, k)
        pe.wait_ge(const_in.sem, 16 * 6)
        values(0, "first", 0)
        load_wait(2)
        for k in range(KT):
            projection(0, "first", "q", 1, k)
        load_wait(G)
        slots(0, "first")
        with pe.Fori(0, B - 1) as b:
            slots(b, "loop")
        slots(B - 1, "last")

    @block.scalar
    def _(act):
        def w_half(c):
            act.wait_ge(w_in[c].sem, 16)
            dst = w_hi[:, 3 * c:3 * c + 3, :, :] if c < G else wo_hi[:]
            flat = "p a k m -> p (a k m)" if c < G else "p k m -> p (k m)"
            act.copy(dst.rearrange(flat), w_stage(c)).then_inc(w_hi_done.sem, 1)

        def x_half(b, k, first=False):
            if not first and k == 0:
                n = USES["loop"]["v", G - 1]
                act.wait_ge(pj_full.sem, pj_full.at(b, n + 1))
                act.wait_ge(x_in.sem, x_in.at(b, 16))
            act.copy(xT_hi[:, k, :], x_raw[:, k, :]).then_inc(xhi_done.sem, 1)

        def from_pj(b, turn, kind, g):
            n = USES[turn][kind, g]
            act.wait_ge(pj_full.sem, pj_full.at(b, n + 1))
            src = pj[:, n % 2, :]
            if kind in "qk":
                u = "qk".index(kind)
                m = 2 * (g - 1) + u
                if g:
                    act.wait_ge(swap_done.sem, swap_done.at(b, m - 1))
                    act.wait_ge(cos_done.sem, cos_done.at(b, m - 1))
                ins = act.activation(raw[:, u, :], src, ACT.Identity, bias=bcol[:, 3 * (g % G) + u:3 * (g % G) + u + 1])
            elif kind == "v":
                ins = act.activation(vT[:], src, ACT.Identity, bias=bcol[:, 3 * (g % G) + 2:3 * (g % G) + 3])
            elif kind == "t":
                if g >= 2:
                    act.wait_ge(av_done.sem, av_done.at(b, g - 1))
                ins = act.copy(vg[:, g % 2, :, :].rearrange("p s m -> p (s m)"), src)
            else:
                if g:
                    act.wait_ge(olo_done.sem, olo_done.at(b, g))
                ins = act.copy(o[:], src)
            ins.then_inc(pj_moved.sem, 1)

        def qk_half(b, u, g):
            m = 2 * (g - 1) + u
            act.wait_ge(rot_done.sem, rot_done.at(b, m + 1))
            if g:
                act.wait_ge(stored.sem, stored.at(b, 64 * (g - 1)))
            act.copy(qk_hi[:, u, :], rot[:]).then_inc(qkhi_done.sem, 1)

        def exp(b, t):
            g, i, s = t // TILES, t % TILES, ROW[t % ST]
            w = (s + 1) * P
            act.wait_ge(max_done.sem, max_done.at(b, t + 1))
            act.activation(prob[:, t % PROBS, 0:w], prob[:, t % PROBS, 0:w], ACT.Exp, bias=nmax[:, g % 2, i:i + 1], scale=-1.0,
                           accum_out=rsum[:, g % 2, s, i // ST:i // ST + 1]).then_inc(exp_done.sem, 1)

        def move_a(b, h):
            if h >= 4:
                act.wait_ge(av_done.sem, av_done.at(b, h // 4))
            act.wait_ge(t_done.sem, t_done.at(b, ST * h + 1))
            act.copy(pT[:, h % 4, 0:8 * P].rearrange("p (k u m) -> p u k m", u=2, m=P)[:, 1, :, :],
                     pa[:].rearrange("p (k m) -> p k m", m=P)).then_inc(a_moved.sem, 1)

        def o_half(b, g):
            act.wait_ge(o_done.sem, o_done.at(b, g + 1))
            act.copy(oT_hi[:, g, :], o[:]).then_inc(ohi_done.sem, 1)

        def slots(b, turn):
            end = SLOTS if turn == "last" else FIRST + SLOTS
            for t in span(turn):
                if t < end:
                    exp(b, t)
                if t % ST == 0 and ST <= t < end + ST:
                    move_a(b, t // ST - 1)
                for (kind, g), first in plan(turn).items():
                    if t == first + (3 if kind in "qkv" else 0):
                        from_pj(b, turn, kind, g)
                for (kind, g), first in halves(turn, 6):
                    if t == first:
                        qk_half(b, "qk".index(kind), g)
                for g in range(G):
                    if turn != "first" and t == PLAN["r", g] + 1:
                        o_half(b, g)
                if turn == "loop" and t in SPLIT_X:
                    x_half(b, SPLIT_X.index(t))

        w_half(0)
        act.wait_ge(x_in.sem, 16)
        for k in range(KT):
            x_half(0, k, True)
        act.wait_ge(const_in.sem, 16 * 6)
        for u in range(2):
            from_pj(0, "first", "qk"[u], 0)
        w_half(1)
        qk_half(0, 0, 0)
        from_pj(0, "first", "v", 0)
        qk_half(0, 1, 0)
        from_pj(0, "first", "t", 0)
        from_pj(0, "first", "q", 1)
        for c in range(2, G + 1):
            w_half(c)
        slots(0, "first")
        with act.Fori(0, B - 1) as b:
            slots(b, "loop")
        slots(B - 1, "last")

    @block.vector
    def _(dve):
        def w_half(c):
            dve.wait_ge(w_hi_done.sem, c + 1)
            hi, lo = (w_hi[:, 3 * c:3 * c + 3, :, :], w_lo[:, 3 * c:3 * c + 3, :, :]) if c < G else (wo_hi[:], wo_lo[:])
            flat = "p a k m -> p (a k m)" if c < G else "p k m -> p (k m)"
            dve.tensor_tensor(lo.rearrange(flat), w_stage(c), hi.rearrange(flat).bitcast(F32),
                              ALU.subtract).then_inc(w_lo_done.sem, 1)

        def rotate(b, turn, u, g):
            m = 2 * (g - 1) + u
            wait_moved(dve, b, turn, "qk"[u], g)
            if g or u:
                dve.wait_ge(rot_done.sem, rot_done.at(b, m))
            passed(dve, b, dve_passed)
            dve.stream_shuffle(swp[:], raw[:, u, :], SWAP).then_inc(swap_done.sem, 1)
            dve.wait_ge(swap_done.sem, swap_done.at(b, m + 1))
            dve.tensor_tensor(swp[:], swp[:], sin[:], ALU.mult).then_inc(sin_done.sem, 1)

        def row_max(b, t):
            g, i, s = t // TILES, t % TILES, ROW[t % ST]
            w = (s + 1) * P
            dve.wait_ge(s_done.sem, s_done.at(b, t + 1))
            if t >= PROBS:
                dve.wait_ge(t_done.sem, t_done.at(b, t + 1 - PROBS))
            passed(dve, b, dve_passed)
            dve.tensor_tensor_reduce(prob[:, t % PROBS, 0:w], ps[:, t % 2, 0:w], mask[:, S - w:S], -D ** -0.5, 3e38,
                                     ALU.add, ALU.min, accum_out=nmax[:, g % 2, i:i + 1]).then_inc(max_done.sem, 1)

        def move_b(b, h):
            if h >= 4:
                dve.wait_ge(av_done.sem, av_done.at(b, h // 4))
            dve.wait_ge(t_done.sem, t_done.at(b, ST * h + 3))
            dve.tensor_copy(pT[:, h % 4, 0:8 * P].rearrange("p (k u m) -> p u k m", u=2, m=P)[:, 0, :, :],
                            pb[:].rearrange("p (k m) -> p k m", m=P)).then_inc(b_moved.sem, 1)

        def move_c(b, h):
            dve.wait_ge(t_done.sem, t_done.at(b, ST * h + 4))
            dve.tensor_copy(pT[:, h % 4, 8 * P:10 * P], pc[:, 0:2 * P]).then_inc(c_moved.sem, 1)

        def recips(b, g):
            dve.wait_ge(exp_done.sem, exp_done.at(b, TILES * (g + 1)))
            dve.reciprocal(rrec[:], rsum[:, g % 2, :, :].rearrange("p s r -> p (s r)")).then_inc(rec_done.sem, 1)
            dve.wait_ge(rec_done.sem, rec_done.at(b, g + 1))
            dve.tensor_copy(rb[:], rrec[:].rearrange("p (s r) -> p s r", r=4).unsqueeze(3)
                            .to_broadcast([P, ST, 4, D])).then_inc(rb_done.sem, 1)

        def normalize(b, turn, g):
            dve.wait_ge(av_done.sem, av_done.at(b, g + 1))
            wait_moved(dve, b, turn, "r", g)
            dve.tensor_tensor(o[:], pv[:], o[:], ALU.mult).then_inc(o_done.sem, 1)

        def x_half(b, k, first=False):
            dve.wait_ge(xhi_done.sem, k + 1 if first else xhi_done.at(b, k + 1))
            dve.tensor_tensor(xT_lo[:, k, :], x_raw[:, k, :], xT_hi[:, k, :].bitcast(F32),
                              ALU.subtract).then_inc(xlo_done.sem, 1)

        def summed(b, s):
            if s == 0:
                dve.wait_ge(res_done.sem, res_done.at(b, ST))
            dve.wait_ge(wo_done.sem, wo_done.at(b, s + 1))
            dve.tensor_tensor(res[:, s, :], pv[:], res[:, s, :], ALU.add).then_inc(z_done.sem, 1)

        def moments(b, s):
            dve.wait_ge(z_done.sem, z_done.at(b, s + 1))
            dve.bn_stats(stats[:, s, :], res[:, s, :]).then_inc(stats_done.sem, 1)
            dve.wait_ge(stats_done.sem, stats_done.at(b, s + 1))
            passed(dve, b, dve_passed)
            dve.bn_aggr(mv[:, s, :], stats[:, s, :]).then_inc(mv_done.sem, 1)

        def layer_norm(b, s):
            dve.wait_ge(rstd_done.sem, rstd_done.at(b, s + 1))
            dve.tensor_scalar(res[:, s, :], res[:, s, :], mv[:, s, 0:1], rstd[:, s:s + 1],
                              ALU.subtract, ALU.mult).then_inc(x1_done.sem, 1)

        def slots(b, turn):
            end = SLOTS if turn == "last" else FIRST + SLOTS
            for t in span(turn):
                if t < end:
                    row_max(b, t)
                if t % ST == 1 and ST <= t < end + ST:
                    move_b(b, t // ST - 1)
                if t % ST == 2 and ST <= t < end + ST:
                    move_c(b, t // ST - 1)
                if turn != "first" and t % TILES == 3 and t // TILES <= G:
                    recips(b, t // TILES - 1)
                for (kind, g), first in halves(turn, 4):
                    if t == first:
                        rotate(b, turn, "qk".index(kind), g)
                if turn == "first":
                    continue
                if turn == "loop" and t - 1 in SPLIT_X[1::2]:
                    x_half(b, SPLIT_X.index(t - 1))
                for g in range(G):
                    if t == PLAN["r", g] + 1:
                        normalize(b, turn, g)
                if t - 1 in OUTPUT:
                    summed(b, OUTPUT[t - 1])
                if t - 2 in OUTPUT:
                    moments(b, OUTPUT[t - 2])
                if t - 4 in OUTPUT:
                    layer_norm(b, OUTPUT[t - 4])

        w_half(0)
        for k in range(KT):
            x_half(0, k, True)
        dve.wait_ge(const_in.sem, 16 * 6)
        rotate(0, "first", 0, 0)
        rotate(0, "first", 1, 0)
        for c in range(1, G + 1):
            w_half(c)
        slots(0, "first")
        with dve.Fori(0, B - 1) as b:
            slots(b, "loop")
        slots(B - 1, "last")

    @block.gpsimd
    def _(pool):
        def x_half(b, k):
            pool.wait_ge(xhi_done.sem, xhi_done.at(b, k + 1))
            pool.tensor_tensor(xT_lo[:, k, :], x_raw[:, k, :], xT_hi[:, k, :].bitcast(F32),
                               ALU.subtract).then_inc(xlo_done.sem, 1)

        def rotate(b, turn, u, g):
            m = 2 * (g - 1) + u
            wait_moved(pool, b, turn, "qk"[u], g)
            if g or u:
                pool.wait_ge(qklo_done.sem, qklo_done.at(b, m))
            pool.tensor_tensor(rot[:], raw[:, u, :], cos[:], ALU.mult).then_inc(cos_done.sem, 1)
            pool.wait_ge(cos_done.sem, cos_done.at(b, m + 1))
            pool.wait_ge(sin_done.sem, sin_done.at(b, m + 1))
            pool.tensor_tensor(rot[:], rot[:], swp[:], ALU.add).then_inc(rot_done.sem, 1)

        def qk_half(b, u, g):
            m = 2 * (g - 1) + u
            pool.wait_ge(qkhi_done.sem, qkhi_done.at(b, m + 1))
            pool.tensor_tensor(qk_lo[:, u, :], rot[:], qk_hi[:, u, :].bitcast(F32),
                               ALU.subtract).then_inc(qklo_done.sem, 1)

        def o_half(b, g):
            pool.wait_ge(ohi_done.sem, ohi_done.at(b, g + 1))
            pool.tensor_tensor(oT_lo[:, g, :], o[:], oT_hi[:, g, :].bitcast(F32),
                               ALU.subtract).then_inc(olo_done.sem, 1)

        def residual(b):
            pool.wait_ge(res_in.sem, res_in.at(b, 16))
            for s in range(ST):
                pool.tensor_tensor(res[:, s, :], res[:, s, :], bo[:], ALU.add).then_inc(res_done.sem, 1)

        def root(b, s):
            pool.wait_ge(mv_done.sem, mv_done.at(b, s + 1))
            passed(pool, b, pool_passed)
            pool.tensor_scalar(veps[:, s:s + 1], mv[:, s, 1:2], EPS, None, ALU.add).then_inc(veps_done.sem, 1)
            pool.wait_ge(veps_done.sem, veps_done.at(b, s + 1))
            pool.tensor_tensor(rstd[:, s:s + 1], veps[:, s:s + 1], mhalf[:], ALU.pow).then_inc(rstd_done.sem, 1)

        def slots(b, turn):
            for t in span(turn):
                if turn != "first" and t - 2 in OUTPUT:
                    root(b, OUTPUT[t - 2])
                for (kind, g), first in halves(turn, 4):
                    if t == first:
                        rotate(b, turn, "qk".index(kind), g)
                for (kind, g), first in halves(turn, 6):
                    if t == first:
                        qk_half(b, "qk".index(kind), g)
                if turn == "first":
                    continue
                if turn == "loop" and t in SPLIT_X[::2]:
                    x_half(b, SPLIT_X.index(t))
                for g in range(G):
                    if t == PLAN["r", g] + 1:
                        o_half(b, g)
                if t == PLAN["q", G]:
                    residual(b)

        pool.memset(mhalf[:], -0.5).then_inc(half_done.sem, 1)
        pool.wait_ge(const_in.sem, 16 * 6)
        for u in range(2):
            rotate(0, "first", u, 0)
            qk_half(0, u, 0)
        pool.wait_ge(half_done.sem, 1)
        slots(0, "first")
        with pool.Fori(0, B - 1) as b:
            slots(b, "loop")
        slots(B - 1, "last")


NR = 4
BESIDE = {3: [("ctx", 0)], 4: [("qk", 0)], 5: [("e", 0), ("e", 1)], 6: [("e", 2), ("e", 3)],
          7: [("a", 0), ("a", 1)], 8: [("a", 2), ("a", 3)], 9: [("t", 0), ("t", 1)], 10: [("t", 2), ("t", 3)],
          11: [("m", 0)], 12: [("m", 1)], 13: [("m", 2)], 14: [("m", 3)]}
AHEAD = 2


def tiles(turn):
    return range(*{"first": (0, AHEAD), "loop": (AHEAD, HT + AHEAD), "last": (AHEAD, HT)}[turn])


def feed_forward_phase(nc, ctx, d, x1_dram, out):
    def sb(name, shape, dt=F32):
        return ctx.enter_context(nc.sbuf_tensor(name, shape, dt))

    def sem(name, per=0, base=0):
        return Count(ctx.enter_context(nc.semaphore(name)), per, base)

    f_raw = sb("f_raw", [P, NR, 2 * KT * P + E])
    gu_hi = sb("gu_hi", [P, 2, 2, KT, P], F32R)
    gu_lo = sb("gu_lo", [P, 2, 2, KT, P], F32R)
    dn_hi = sb("dn_hi", [P, 2, E], F32R)
    dn_lo = sb("dn_lo", [P, 2, E], F32R)
    c_raw = sb("c_raw", [P, CT, S])
    c_hi = sb("c_hi", [P, CT, S], F32R)
    c_lo = sb("c_lo", [P, CT, S], F32R)
    p_raw = sb("p_raw", [P, 2, CT, DK])
    p_hi = sb("p_hi", [P, 2, CT, DK], F32R)
    p_lo = sb("p_lo", [P, 2, CT, DK], F32R)
    pbias = sb("pbias", [P, 2])
    qk = sb("cqk", [P, 2, S])
    qk_hi = sb("cqk_hi", [P, 2, S], F32R)
    qk_lo = sb("cqk_lo", [P, 2, S], F32R)
    e = sb("e", [P, KT, S])
    att_hi = sb("att_hi", [P, KT, S], F32R)
    att_lo = sb("att_lo", [P, KT, S], F32R)
    emax = sb("emax", [P, KT])
    nemax = sb("nemax", [P, KT])
    esum = sb("esum", [P, KT])
    erec = sb("erec", [P, KT])
    x = sb("x12", [P, ST, E])
    x1T_hi = sb("x1T_hi", [P, KT, S], F32R)
    x1T_lo = sb("x1T_lo", [P, KT, S], F32R)
    x2T_hi = sb("x2T_hi", [P, KT, S], F32R)
    x2T_lo = sb("x2T_lo", [P, KT, S], F32R)
    fin = sb("fin", [P, ST, E])
    th = sb("th", [P, S])
    half = sb("half", [P, S])
    gated = sb("gated", [P, S])
    g_hi = sb("g_hi", [P, 2, S], F32R)
    g_lo = sb("g_lo", [P, 2, S], F32R)
    ident = sb("ident2", [P, P])
    mhalf = sb("mhalf2", [P, 1])
    one = sb("one", [P, 1])
    stats, mv, veps, rstd = ([sb(f"{n}{k}", [P, ST, w]) for k in (2, 3)]
                             for n, w in (("stats", 6), ("mv", 2), ("veps", 1), ("rstd", 1)))

    pg = ctx.enter_context(nc.psum_tensor("pg", [P, S], F32))
    pu = ctx.enter_context(nc.psum_tensor("pu", [P, S], F32))
    pd = ctx.enter_context(nc.psum_tensor("pd", [P, ST, E], F32))
    px = ctx.enter_context(nc.psum_tensor("px", [P, 2, S], F32))

    const_in = sem("const2_in")
    sp_passed, dve_passed, pool_passed = (sem(f"{n}_passed2") for n in ("sp", "dve", "pool"))
    p_hi_done, p_lo_done = sem("p_hi_done"), sem("p_lo_done")
    half_done = sem("half2_done")
    x1_in = sem("x1_in", 16, 16)
    c_in = sem("c_in", 16, 16)
    chi_done, clo_done = sem("chi_done", 1, 1), sem("clo_done", 1, 1)
    qk_full, qk_moved = sem("cqk_full", 2, 2), sem("cqk_moved", 2, 2)
    qkhi_done, qklo_done = sem("cqkhi_done", 2, 2), sem("cqklo_done", 2, 2)
    e_full = sem("e_full", KT, KT)
    emax_done, nemax_done = sem("emax_done", KT, KT), sem("nemax_done", KT, KT)
    e_done = sem("e_done", KT, KT)
    erec_done, att_done = sem("erec_done", KT, KT), sem("att_done", KT, KT)
    a_full = sem("a_full", KT, KT)
    ahi_done, alo_done = sem("ahi_done", KT, KT), sem("alo_done", KT, KT)
    t1_full, t1hi_done, t1lo_done = (sem(n, ST, ST) for n in ("t1_full", "t1hi_done", "t1lo_done"))
    t2_full, t2hi_done, t2lo_done = (sem(n, ST, ST) for n in ("t2_full", "t2hi_done", "t2lo_done"))
    m_full = sem("m_full", ST, ST)
    raw_in = [sem(f"raw_in{n}", 16 * HT // NR) for n in range(NR)]
    guhi_done, gulo_done = sem("guhi_done", HT), sem("gulo_done", HT)
    dnhi_done, dnlo_done = sem("dnhi_done", HT), sem("dnlo_done", HT)
    g_full, u_full, d_full = sem("g_full", HT), sem("u_full", HT), sem("d_full", HT)
    th_done, half_done3, gated_done = sem("th_done", HT), sem("gate_read", HT), sem("gated_done", HT)
    ghi_done, glo_done = sem("ghi_done", HT), sem("glo_done", HT)
    fin_in = sem("fin_in", 16)
    out_done = sem("out_done", 16, 16)
    z_done = [sem("z2_done", ST, ST), sem("z3_done", ST, 1)]
    stats_done, mv_done, veps_done, rstd_done, ln_done = (
        [sem(f"{n}{k}_done", ST, (ST, 0)[k - 2]) for k in (2, 3)] for n in ("stats", "mv", "veps", "rstd", "ln"))

    block = ctx.enter_context(nc.Block())

    @block.sync
    def _(sp):
        def context(b):
            sp.dma_start(c_raw[:], d["cT"][bass.ts(b + 1, P), :]).then_inc(c_in.sem, 16)

        def features(b):
            sp.dma_start(x[:], x1_dram[bass.ts(b + 1, P), :]).then_inc(x1_in.sem, 16)

        def weights(c):
            sp.dma_start(f_raw[:, c % NR, :], d["w_ffn"][c * P:(c + 1) * P, :]).then_inc(raw_in[c % NR].sem, 16)

        def reload(b, js):
            for j in js:
                sp.wait_ge(gulo_done.sem, gulo_done.at(b, j + 1))
                passed(sp, b, sp_passed)
                sp.wait_ge(dnlo_done.sem, dnlo_done.at(b, j + 1))
                weights((j + NR) % HT)

        def slots(b, turn):
            if turn == "loop":
                sp.wait_ge(chi_done.sem, chi_done.at(b, 0))
                passed(sp, b, sp_passed)
                sp.wait_ge(clo_done.sem, clo_done.at(b, 0))
                passed(sp, b, sp_passed)
                context(b)
            sp.wait_ge(ln_done[0].sem, ln_done[0].at(b, 0))
            passed(sp, b, sp_passed)
            sp.wait_ge(out_done.sem, out_done.at(b, 0))
            sp.dma_start(fin[:], x[:]).then_inc(fin_in.sem, 16)
            sp.wait_ge(fin_in.sem, fin_in.at(b, 16))
            passed(sp, b, sp_passed)
            if turn == "loop":
                sp.wait_ge(t2lo_done.sem, t2lo_done.at(b, 0))
                passed(sp, b, sp_passed)
                features(b)
            reload(b, tiles("loop") if turn == "loop" else range(AHEAD, HT - NR))
            sp.wait_ge(ln_done[1].sem, ln_done[1].at(b, ST))
            passed(sp, b, sp_passed)
            sp.dma_start(out[bass.ts(b, P), :], fin[:]).then_inc(out_done.sem, 16)

        sp.sem_inc(out_done.sem, 16)
        sp.dma_start(p_raw[:], d["w_ctx"]).then_inc(const_in.sem, 16)
        sp.dma_start(pbias[:], d["bctx"]).then_inc(const_in.sem, 16)
        sp.dma_start(ident[:], d["ident"]).then_inc(const_in.sem, 16)
        context(-1)
        features(-1)
        for c in range(NR):
            weights(c)
        reload(0, tiles("first"))
        with sp.Fori(0, B - 1) as b:
            slots(b, "loop")
        slots(B - 1, "last")
        sp.wait_ge(out_done.sem, out_done.at(B - 1, 16))

    @block.tensor
    def _(pe):
        def close(mm, count):
            mm.then_inc(count.sem, 1)

        def three(dst, n, stationary, moving, first=True, final=True):
            for part, (a, c) in enumerate(((0, 0), (1, 0), (0, 1))):
                for k in range(n):
                    mm = pe.matmul(dst, stationary(k)[a], moving(k)[c], start=(first and part == 0 and k == 0),
                                   stop=(final and part == 2 and k == n - 1))
            return mm

        def transposed(b, full, s, bank, src=x):
            for k in range(KT):
                mm = pe.transpose(px[:, bank, k * P:(k + 1) * P], src[:, s, k * P:(k + 1) * P], ident[:])
            close(mm, full)

        def beside(b, kind, n):
            if kind == "qk":
                pe.wait_ge(clo_done.sem, clo_done.at(b, 1))
                pe.wait_ge(chi_done.sem, chi_done.at(b, 1))
                for u in range(2):
                    close(three(px[:, u, :], CT, lambda k: (p_hi[:, u, k, :], p_lo[:, u, k, :]),
                                lambda k: (c_hi[:, k, :], c_lo[:, k, :])), qk_full)
            elif kind == "e":
                if n < 2:
                    pe.wait_ge(qk_moved.sem, qk_moved.at(b, 2))
                    pe.wait_ge(qkhi_done.sem, qkhi_done.at(b, 2))
                    pe.wait_ge(qklo_done.sem, qklo_done.at(b, 2))
                else:
                    pe.wait_ge(e_done.sem, e_done.at(b, n - 1))
                cols = slice(n * P, (n + 1) * P)
                close(three(px[:, n % 2, :], 1, lambda k: (qk_hi[:, 0, cols], qk_lo[:, 0, cols]),
                            lambda k: (qk_hi[:, 1, :], qk_lo[:, 1, :])), e_full)
            elif kind == "a":
                pe.wait_ge(att_done.sem, att_done.at(b, n + 1))
                if n < 2:
                    pe.wait_ge(e_done.sem, e_done.at(b, n + 3))
                else:
                    pe.wait_ge(alo_done.sem, alo_done.at(b, n - 1))
                transposed(b, a_full, n, n % 2, e)
            elif kind == "t":
                if n == 0:
                    pe.wait_ge(x1_in.sem, x1_in.at(b, 16))
                if n < 2:
                    pe.wait_ge(alo_done.sem, alo_done.at(b, n + 3))
                else:
                    pe.wait_ge(t1lo_done.sem, t1lo_done.at(b, n - 1))
                transposed(b, t1_full, n, n % 2)
            elif kind == "m":
                if n == 0:
                    pe.wait_ge(ahi_done.sem, ahi_done.at(b, KT))
                    pe.wait_ge(alo_done.sem, alo_done.at(b, KT))
                if n < 2:
                    pe.wait_ge(t1lo_done.sem, t1lo_done.at(b, 3 + n))
                else:
                    pe.wait_ge(z_done[0].sem, z_done[0].at(b, n - 1))
                cols = slice(n * P, (n + 1) * P)
                close(three(px[:, n % 2, :], KT, lambda k: (x1T_hi[:, k, cols], x1T_lo[:, k, cols]),
                            lambda k: (att_hi[:, k, :], att_lo[:, k, :])), m_full)
            elif kind == "u":
                for s in range(ST):
                    pe.wait_ge(ln_done[0].sem, ln_done[0].at(b, s + 1))
                    if s < 2:
                        pe.wait_ge(z_done[0].sem, z_done[0].at(b, s + 3))
                    else:
                        pe.wait_ge(t2lo_done.sem, t2lo_done.at(b, s - 1))
                    transposed(b, t2_full, s, s % 2)

        def hidden(b, j, u):
            if u == 0:
                pe.wait_ge(guhi_done.sem, guhi_done.at(b, j + 1))
                pe.wait_ge(gulo_done.sem, gulo_done.at(b, j + 1))
                if j % HT == 0:
                    pe.wait_ge(t2hi_done.sem, t2hi_done.at(b, ST * (j // HT)))
                    pe.wait_ge(t2lo_done.sem, t2lo_done.at(b, ST * (j // HT)))
                if j:
                    pe.wait_ge(half_done3.sem, half_done3.at(b, j))
            elif j:
                pe.wait_ge(gated_done.sem, gated_done.at(b, j))
            close(three((pg, pu)[u][:], KT, lambda k: (gu_hi[:, j % 2, u, k, :], gu_lo[:, j % 2, u, k, :]),
                        lambda k: (x2T_hi[:, k, :], x2T_lo[:, k, :])), (g_full, u_full)[u])

        def down(b, j):
            if j % HT == 0:
                pe.wait_ge(z_done[1].sem, z_done[1].at(b, ST * (j // HT)))
            pe.wait_ge(dnhi_done.sem, dnhi_done.at(b, j + 1))
            pe.wait_ge(dnlo_done.sem, dnlo_done.at(b, j + 1))
            pe.wait_ge(ghi_done.sem, ghi_done.at(b, j + 1))
            pe.wait_ge(glo_done.sem, glo_done.at(b, j + 1))
            for s in range(ST):
                cols = slice(s * P, (s + 1) * P)
                mm = three(pd[:, s, :], 1, lambda k: (g_hi[:, j % 2, cols], g_lo[:, j % 2, cols]),
                           lambda k: (dn_hi[:, j % 2, :], dn_lo[:, j % 2, :]), j % HT == 0, j % HT == HT - 1)
            close(mm, d_full)

        def slots(b, turn):
            for j in tiles(turn):
                hidden(b, j, 0)
                hidden(b, j, 1)
                if turn == "loop":
                    for kind, n in BESIDE.get(j, []):
                        beside(b, kind, n)
                    if j == HT - 1:
                        beside(b, "u", 0)
                if j:
                    down(b, j - 1)
            if turn == "last":
                down(b, HT - 1)

        pe.wait_ge(p_hi_done.sem, 1)
        pe.wait_ge(p_lo_done.sem, 1)
        pe.wait_ge(const_in.sem, 48)
        for steps in BESIDE.values():
            for kind, n in steps:
                beside(-1, kind, n)
        beside(-1, "u", 0)
        slots(0, "first")
        with pe.Fori(0, B - 1) as b:
            slots(b, "loop")
        slots(B - 1, "last")

    @block.scalar
    def _(act):
        def gu_half(b, j):
            act.wait_ge(raw_in[j % NR].sem, raw_in[j % NR].at(b, 16 * (j // NR + 1)))
            if j >= 2:
                act.wait_ge(u_full.sem, u_full.at(b, j - 1))
            act.copy(gu_hi[:, j % 2, :, :, :].rearrange("p u k m -> p (u k m)"),
                     f_raw[:, j % NR, 0:2 * KT * P]).then_inc(guhi_done.sem, 1)

        def dn_half(b, j):
            if j >= 2:
                act.wait_ge(d_full.sem, d_full.at(b, j - 1))
            act.copy(dn_hi[:, j % 2, :], f_raw[:, j % NR, 2 * KT * P:]).then_inc(dnhi_done.sem, 1)

        def t_half(b, full, done, dst, s):
            act.wait_ge(full.sem, full.at(b, s + 1))
            act.copy(dst[:, :, s * P:(s + 1) * P], px[:, s % 2, :].rearrange("p (k m) -> p k m", m=P)).then_inc(done.sem, 1)

        def beside(b, steps):
            for kind, n in steps:
                if kind == "ctx":
                    act.wait_ge(c_in.sem, c_in.at(b, 16))
                    act.copy(c_hi[:].rearrange("p k s -> p (k s)"), c_raw[:].rearrange("p k s -> p (k s)")).then_inc(chi_done.sem, 1)
                elif kind == "qk":
                    for u in range(2):
                        act.wait_ge(qk_full.sem, qk_full.at(b, u + 1))
                        act.activation(qk[:, u, :], px[:, u, :], ACT.Identity, bias=pbias[:, u:u + 1]).then_inc(qk_moved.sem, 1)
                    for u in range(2):
                        act.wait_ge(qk_moved.sem, qk_moved.at(b, u + 1))
                        act.copy(qk_hi[:, u, :], qk[:, u, :]).then_inc(qkhi_done.sem, 1)
                elif kind == "e":
                    act.wait_ge(nemax_done.sem, nemax_done.at(b, n + 1))
                    act.activation(e[:, n, :], px[:, n % 2, :], ACT.Exp, bias=nemax[:, n:n + 1], scale=1.0,
                                   accum_out=esum[:, n:n + 1]).then_inc(e_done.sem, 1)
                elif kind == "a":
                    t_half(b, a_full, ahi_done, att_hi, n)
                elif kind == "t":
                    t_half(b, t1_full, t1hi_done, x1T_hi, n)

        def transposed(b):
            for s in range(ST):
                t_half(b, t2_full, t2hi_done, x2T_hi, s)

        def slots(b, turn):
            for j in tiles(turn):
                act.wait_ge(g_full.sem, g_full.at(b, j + 1))
                if j:
                    act.wait_ge(half_done3.sem, half_done3.at(b, j))
                act.activation(th[:], pg[:], ACT.Tanh, scale=0.5).then_inc(th_done.sem, 1)
                more = turn != "last" or j < HT - 1
                if more:
                    gu_half(b, j + 1)
                if j == HT - 1 and turn == "loop":
                    transposed(b)
                act.wait_ge(gated_done.sem, gated_done.at(b, j + 1))
                if j >= 2:
                    act.wait_ge(d_full.sem, d_full.at(b, j - 1))
                act.copy(g_hi[:, j % 2, :], gated[:]).then_inc(ghi_done.sem, 1)
                if turn == "loop":
                    beside(b, BESIDE.get(j, []))
                if more:
                    dn_half(b, j + 1)

        steps = list(BESIDE.values())
        act.wait_ge(const_in.sem, 48)
        act.copy(p_hi[:].rearrange("p u k m -> p (u k m)"), p_raw[:].rearrange("p u k m -> p (u k m)")).then_inc(p_hi_done.sem, 1)
        beside(-1, steps[0])
        gu_half(0, 0)
        dn_half(0, 0)
        for step in steps[1:]:
            beside(-1, step)
        transposed(-1)
        slots(0, "first")
        with act.Fori(0, B - 1) as b:
            slots(b, "loop")
        slots(B - 1, "last")

    @block.vector
    def _(dve):
        def gu_half(b, j):
            dve.wait_ge(guhi_done.sem, guhi_done.at(b, j + 1))
            if j >= 2:
                dve.wait_ge(u_full.sem, u_full.at(b, j - 1))
            flat = "p u k m -> p (u k m)"
            dve.tensor_tensor(gu_lo[:, j % 2, :, :, :].rearrange(flat), f_raw[:, j % NR, 0:2 * KT * P],
                              gu_hi[:, j % 2, :, :, :].rearrange(flat).bitcast(F32), ALU.subtract).then_inc(gulo_done.sem, 1)

        def dn_half(b, j):
            dve.wait_ge(dnhi_done.sem, dnhi_done.at(b, j + 1))
            if j >= 2:
                dve.wait_ge(d_full.sem, d_full.at(b, j - 1))
            dve.tensor_tensor(dn_lo[:, j % 2, :], f_raw[:, j % NR, 2 * KT * P:], dn_hi[:, j % 2, :].bitcast(F32),
                              ALU.subtract).then_inc(dnlo_done.sem, 1)

        def t_half(b, hi_done, done, hi, lo, s):
            cols = slice(s * P, (s + 1) * P)
            dve.wait_ge(hi_done.sem, hi_done.at(b, s + 1))
            dve.tensor_tensor(lo[:, :, cols], px[:, s % 2, :].rearrange("p (k m) -> p k m", m=P),
                              hi[:, :, cols].bitcast(F32), ALU.subtract).then_inc(done.sem, 1)

        def summed(b, which, full, src, dst, s, n):
            if which == 1 and s == 0:
                dve.wait_ge(fin_in.sem, fin_in.at(b, 16))
            dve.wait_ge(full.sem, full.at(b, n))
            dve.tensor_tensor(dst[:, s, :], src, dst[:, s, :], ALU.add).then_inc(z_done[which].sem, 1)

        def moments(b, which, dst, s):
            z, st, m = z_done[which], stats_done[which], mv_done[which]
            dve.wait_ge(z.sem, z.at(b, s + 1))
            dve.bn_stats(stats[which][:, s, :], dst[:, s, :]).then_inc(st.sem, 1)
            dve.wait_ge(st.sem, st.at(b, s + 1))
            passed(dve, b, dve_passed)
            dve.bn_aggr(mv[which][:, s, :], stats[which][:, s, :]).then_inc(m.sem, 1)

        def normalized(b, which, dst, s):
            dve.wait_ge(rstd_done[which].sem, rstd_done[which].at(b, s + 1))
            dve.tensor_scalar(dst[:, s, :], dst[:, s, :], mv[which][:, s, 0:1], rstd[which][:, s, :],
                              ALU.subtract, ALU.mult).then_inc(ln_done[which].sem, 1)

        def beside(b, steps):
            for kind, n in steps:
                if kind == "e":
                    dve.wait_ge(e_full.sem, e_full.at(b, n + 1))
                    dve.reduce_max(emax[:, n:n + 1], px[:, n % 2, :], AX.X).then_inc(emax_done.sem, 1)
                    dve.wait_ge(emax_done.sem, emax_done.at(b, n + 1))
                    dve.tensor_scalar(nemax[:, n:n + 1], emax[:, n:n + 1], -1.0, None, ALU.mult).then_inc(nemax_done.sem, 1)
                elif kind == "a":
                    t_half(b, ahi_done, alo_done, att_hi, att_lo, n)
                elif kind == "t":
                    t_half(b, t1hi_done, t1lo_done, x1T_hi, x1T_lo, n)
                elif kind == "m":
                    summed(b, 0, m_full, px[:, n % 2, :], x, n, n + 1)
                    moments(b, 0, x, n)
            for kind, n in steps:
                if kind == "e":
                    dve.wait_ge(e_done.sem, e_done.at(b, n + 1))
                    dve.reciprocal(erec[:, n:n + 1], esum[:, n:n + 1]).then_inc(erec_done.sem, 1)
                    dve.wait_ge(erec_done.sem, erec_done.at(b, n + 1))
                    dve.tensor_scalar(e[:, n, :], e[:, n, :], erec[:, n:n + 1], None, ALU.mult).then_inc(att_done.sem, 1)

        def after(b, steps):
            for kind, n in steps:
                if kind == "m":
                    normalized(b, 0, x, n)

        def transposed(b):
            for s in range(ST):
                t_half(b, t2hi_done, t2lo_done, x2T_hi, x2T_lo, s)

        def slots(b, turn):
            for j in tiles(turn):
                dve.wait_ge(th_done.sem, th_done.at(b, j + 1))
                if j:
                    dve.wait_ge(gated_done.sem, gated_done.at(b, j))
                dve.scalar_tensor_tensor(half[:], th[:], 1.0, pg[:], ALU.add, ALU.mult).then_inc(half_done3.sem, 1)
                more = turn != "last" or j < HT - 1
                if more:
                    gu_half(b, j + 1)
                dve.wait_ge(u_full.sem, u_full.at(b, j + 1))
                dve.wait_ge(half_done3.sem, half_done3.at(b, j + 1))
                if j:
                    dve.wait_ge(glo_done.sem, glo_done.at(b, j))
                dve.scalar_tensor_tensor(gated[:], half[:], 0.5, pu[:], ALU.mult, ALU.mult).then_inc(gated_done.sem, 1)
                if j == HT - 1 and turn == "loop":
                    transposed(b)
                if turn == "loop":
                    beside(b, BESIDE.get(j, []))
                if j == HT + 1:
                    for s in range(ST):
                        moments(b, 1, fin, s)
                if more:
                    dn_half(b, j + 1)
                if j == HT:
                    for s in range(ST):
                        summed(b, 1, d_full, pd[:, s, :], fin, s, HT)
                if j == HT + 1:
                    for s in range(ST):
                        normalized(b, 1, fin, s)
                if turn == "loop":
                    after(b, BESIDE.get(j, []))
            if turn == "last":
                for s in range(ST):
                    summed(b, 1, d_full, pd[:, s, :], fin, s, HT)
                    moments(b, 1, fin, s)
                for s in range(ST):
                    normalized(b, 1, fin, s)

        dve.memset(one[:], 1.0).then_inc(z_done[1].sem, 1)
        dve.wait_ge(p_hi_done.sem, 1)
        flat = "p u k m -> p (u k m)"
        dve.tensor_tensor(p_lo[:].rearrange(flat), p_raw[:].rearrange(flat), p_hi[:].rearrange(flat).bitcast(F32),
                          ALU.subtract).then_inc(p_lo_done.sem, 1)
        gu_half(0, 0)
        dn_half(0, 0)
        for steps in BESIDE.values():
            beside(-1, steps)
            after(-1, steps)
        transposed(-1)
        slots(0, "first")
        with dve.Fori(0, B - 1) as b:
            slots(b, "loop")
        slots(B - 1, "last")

    @block.gpsimd
    def _(pool):
        def root(b, which, s):
            pool.wait_ge(mv_done[which].sem, mv_done[which].at(b, s + 1))
            passed(pool, b, pool_passed)
            pool.tensor_scalar(veps[which][:, s, :], mv[which][:, s, 1:2], EPS, None, ALU.add).then_inc(veps_done[which].sem, 1)
            pool.wait_ge(veps_done[which].sem, veps_done[which].at(b, s + 1))
            pool.tensor_tensor(rstd[which][:, s, :], veps[which][:, s, :], mhalf[:], ALU.pow).then_inc(rstd_done[which].sem, 1)

        def beside(b, steps):
            for kind, n in steps:
                if kind == "ctx":
                    pool.wait_ge(chi_done.sem, chi_done.at(b, 1))
                    pool.tensor_tensor(c_lo[:].rearrange("p k s -> p (k s)"), c_raw[:].rearrange("p k s -> p (k s)"),
                                       c_hi[:].rearrange("p k s -> p (k s)").bitcast(F32), ALU.subtract).then_inc(clo_done.sem, 1)
                elif kind == "qk":
                    for u in range(2):
                        pool.wait_ge(qkhi_done.sem, qkhi_done.at(b, u + 1))
                        pool.tensor_tensor(qk_lo[:, u, :], qk[:, u, :], qk_hi[:, u, :].bitcast(F32),
                                           ALU.subtract).then_inc(qklo_done.sem, 1)
                elif kind == "m":
                    root(b, 0, n)

        def slots(b, turn):
            for j in tiles(turn):
                pool.wait_ge(ghi_done.sem, ghi_done.at(b, j + 1))
                if j >= 2:
                    pool.wait_ge(d_full.sem, d_full.at(b, j - 1))
                pool.tensor_tensor(g_lo[:, j % 2, :], gated[:], g_hi[:, j % 2, :].bitcast(F32),
                                   ALU.subtract).then_inc(glo_done.sem, 1)
                if turn == "loop":
                    beside(b, BESIDE.get(j, []))
                if j == HT + 1:
                    for s in range(ST):
                        root(b, 1, s)
            if turn == "last":
                for s in range(ST):
                    root(b, 1, s)

        pool.memset(mhalf[:], -0.5).then_inc(half_done.sem, 1)
        pool.wait_ge(half_done.sem, 1)
        for steps in BESIDE.values():
            beside(-1, steps)
        slots(0, "first")
        with pool.Fori(0, B - 1) as b:
            slots(b, "loop")
        slots(B - 1, "last")


def layouts(a):
    def tiles(w):
        return w.reshape(-1, P, w.shape[1]).transpose(1, 0, 2)

    pos = np.arange(S, dtype=np.float32)
    theta = np.power(np.float32(10000.0), -np.arange(0, D, 2, dtype=np.float32) / D)
    angle = pos[None, :] * np.tile(np.repeat(theta, 2), 4)[:, None]
    sign = np.tile(np.array([-1.0, 1.0], np.float32), P // 2)[:, None]
    mask = np.zeros((P, S), np.float32)
    mask[:, S - P:] = np.triu(np.full((P, P), MASKED, np.float32), 1)
    x = a["x"]
    qkv = np.stack([tiles(a[f"L0_attn_W{n}"]).reshape(P, KT, G, P) for n in "qkv"])
    return {
        "xT": x.reshape(B, S, KT, P).transpose(0, 3, 2, 1).reshape(B * P, KT * S),
        "x": x.reshape(B, ST, P, E).transpose(0, 2, 1, 3).reshape(B * P, ST * E),
        "w_qkv": qkv.transpose(3, 1, 0, 2, 4).reshape(G * P, 3 * KT * P),
        "wo": tiles(a["L0_attn_Wo"]).reshape(P, KT * E),
        "bcol": np.stack([a[f"L0_attn_b{n}"].reshape(G, P) for n in "qkv"]).transpose(2, 1, 0).reshape(P, 3 * G),
        "bo": np.broadcast_to(a["L0_attn_bo"], (P, E)),
        "cos": np.cos(angle), "sin": np.sin(angle) * sign,
        "mask": mask, "ident": np.eye(P, dtype=np.float32),
        "cT": a["ctx_1024"].reshape(B, S, CT, P).transpose(0, 3, 2, 1).reshape(B * P, CT * S),
        "w_ctx": np.stack([tiles(a[f"L0_xattn_W{n}"].T) for n in "qk"]).transpose(1, 0, 2, 3).reshape(P, 2 * CT * DK),
        "bctx": np.stack([a["L0_xattn_bq"], a["L0_xattn_bk"]]).T,
        "w_ffn": np.concatenate(
            [w.reshape(HT, P, KT, P).transpose(0, 3, 2, 1).reshape(HT, P, KT * P)
             for w in (a["L0_ffn_w_gate"], a["L0_ffn_w_up"])] +
            [a["L0_ffn_w_down"].T.reshape(HT, P, E)], axis=2).reshape(HT * P, 2 * KT * P + E),
    }


def decoder_layer(nc, d, out):
    x1_dram = nc.dram_tensor("x1_scratch", (B * P, ST * E), F32, kind="Internal").ap()
    with ExitStack() as ctx:
        attention_phase(nc, ctx, d, x1_dram)
    with ExitStack() as ctx:
        feed_forward_phase(nc, ctx, d, x1_dram, out)


def kernel(**inputs):
    import concourse.bacc as bacc
    from concourse.bass_utils import run_bass_kernel_spmd

    nc = bacc.Bacc("TRN2", target_bir_lowering=False, num_devices=1)
    arrays, d = {}, {}
    for name, a in layouts({k: np.asarray(v) for k, v in inputs.items()}).items():
        a = np.ascontiguousarray(a)
        arrays[f"in_{name}"] = a
        d[name] = nc.dram_tensor(f"in_{name}", a.shape, F32, kind="ExternalInput").ap()
    out = nc.dram_tensor("out", (B * P, ST * E), F32, kind="ExternalOutput").ap()
    decoder_layer(nc, d, out)
    got = run_bass_kernel_spmd(nc, [arrays], core_ids=[0]).results[0]["out"]
    return got.reshape(B, P, ST, E).transpose(0, 2, 1, 3).reshape(B, S, E)
```

```python
from contextlib import ExitStack

import numpy as np

import concourse.bass as bass
from concourse import mybir

F32 = mybir.dt.float32
F32R = mybir.dt.float32r
ALU = mybir.AluOpType
ACT = mybir.ActivationFunctionType
AX = mybir.AxisListType

P = 128
B, S, E = 4, 512, 512
H, D = 16, 32
CTX, DK = 256, 128
HID = 2048
ST = S // P
KT = E // P
CT = CTX // P
G = H // 4
TILES = 16
SLOTS = G * TILES
PROBS = 4
HT = HID // P
EPS = 1e-5
MASKED = -1e30
LAG = 3
ROW = (3, 2, 0, 1)
SWAP = [i ^ 1 for i in range(32)]


FIRST = TILES + 3
PLAN = {("r", 0): 21, ("v", 2): 20, ("t", 2): 26, ("q", 3): 26, ("k", 3): 30, ("v", 3): 34, ("r", 1): 37,
        ("t", 3): 39, ("q", 4): 42, ("k", 4): 46, ("v", 4): 50, ("r", 2): 54, ("t", 4): 56, ("q", 5): 60,
        ("k", 5): 64, ("r", 3): 68, ("v", 5): 68, ("t", 5): 74, ("q", 6): 75, ("k", 6): 79}
ROTATE, SPLIT_QK, NORMALIZE, SPLIT_O = 4, 5, 2, 2
SPLIT_X = (39, 40, 41, 42)
SPLIT_WO = (9, 11, 13, 15)
SPLIT_CONTEXT = 66
OUTPUT = {72: 0, 74: 1, 76: 2, 78: 3}


def plan(turn):
    if turn == "first":
        return {(kind, g - G): t - SLOTS for (kind, g), t in PLAN.items() if t >= SLOTS and kind != "r"}
    return {(kind, g): t for (kind, g), t in PLAN.items() if turn == "loop" or g < G}


def halves(turn, later):
    keys = [(("q", 1), PLAN["q", G + 1] - SLOTS)] + list(plan("first").items()) + list(plan("loop").items())
    keys = [((kind, g), t + later) for (kind, g), t in keys if kind in "qk" and (turn != "last" or g < G)]
    return [(key, t) for key, t in keys if t in span(turn)]


def span(turn):
    return range(FIRST) if turn == "first" else range(FIRST, FIRST + SLOTS)


class Count:

    def __init__(self, sem, per, base=0):
        self.sem, self.per, self.base = sem, per, base

    def at(self, b, k):
        return b * self.per + (self.base + k)


def passed(eng, b, count):
    if not isinstance(b, int):
        eng.sem_inc(count.sem, 1)


class Between:

    def __init__(self, nc, ctx):
        def sb(name, shape, dt=F32):
            return ctx.enter_context(nc.sbuf_tensor(name, shape, dt))

        def sem(name, per=0, base=0):
            return Count(ctx.enter_context(nc.semaphore(name)), per, base)

        with ExitStack() as first:
            self.w_hi, self.w_lo, self.xT_hi, self.xT_lo, self.x_raw = (
                first.enter_context(nc.sbuf_tensor(name, shape, dt)) for name, shape, dt in (
                    ("w_hi", [P, 3 * G, KT, P], F32R), ("w_lo", [P, 3 * G, KT, P], F32R),
                    ("xT_hi", [P, KT, S], F32R), ("xT_lo", [P, KT, S], F32R), ("x_raw", [P, KT, S], F32)))
        self.f_raw = sb("f_raw", [P, NR, 2 * KT * P + E])
        self.p_raw, self.c_raw = sb("p_raw", [P, 2, CT, DK]), sb("c_raw", [P, CT, S])
        self.p_hi, self.p_lo = sb("p_hi", [P, 2, CT, DK], F32R), sb("p_lo", [P, 2, CT, DK], F32R)
        self.c_hi, self.c_lo = sb("c_hi", [P, CT, S], F32R), sb("c_lo", [P, CT, S], F32R)
        self.x = sb("x12", [P, ST, E])
        self.qk = sb("cqk", [P, 2, S])
        self.qk_hi, self.qk_lo = sb("cqk_hi", [P, 2, S], F32R), sb("cqk_lo", [P, 2, S], F32R)
        below = 2 * 3 * G * KT * P + 3 * KT * S
        above = NR * (2 * KT * P + E) + 3 * (2 * CT * DK + CT * S) + ST * E + 3 * 2 * S
        sb("unused", [P, below - above])
        self.pbias = sb("pbias", [P, 2])
        self.ident = sb("ident", [P, P])
        self.mhalf = sb("mhalf", [P, 1])
        self.x1_stored = sem("x1_stored", 16, 16)
        self.p_in, self.p_hi_done, self.p_lo_done = sem("p_in"), sem("p_hi_done"), sem("p_lo_done")
        self.c_in, self.chi_done, self.clo_done = sem("c_in", 16, 16), sem("chi_done", 1, 1), sem("clo_done", 1, 1)
        self.x1_in = sem("x1_in", 16, 16)
        self.qk_full, self.qk_moved = sem("cqk_full", 2, 2), sem("cqk_moved", 2, 2)
        self.qkhi_done, self.qklo_done = sem("cqkhi_done", 2, 2), sem("cqklo_done", 2, 2)
        self.raw_in = [sem(f"raw_in{n}", 16 * HT // NR) for n in range(NR)]


def load_between(sp, d, m, x1_dram):
    sp.dma_start(m.p_raw[:], d["w_ctx"]).then_inc(m.p_in.sem, 16)
    sp.dma_start(m.pbias[:], d["bctx"]).then_inc(m.p_in.sem, 16)
    sp.dma_start(m.c_raw[:], d["cT"][0:P, :]).then_inc(m.c_in.sem, 16)
    sp.dma_start(m.x[:], x1_dram[0:P, :]).then_inc(m.x1_in.sem, 16)
    for c in range(NR):
        sp.dma_start(m.f_raw[:, c, :], d["w_ffn"][c * P:(c + 1) * P, :]).then_inc(m.raw_in[c].sem, 16)


def attention_phase(nc, ctx, d, x1_dram, m):
    def sb(name, shape, dt=F32):
        return ctx.enter_context(nc.sbuf_tensor(name, shape, dt))

    def sem(name, per=0, base=0):
        return Count(ctx.enter_context(nc.semaphore(name)), per, base)

    w_hi, w_lo = m.w_hi, m.w_lo
    wo_hi = sb("wo_hi", [P, KT, E], F32R)
    wo_lo = sb("wo_lo", [P, KT, E], F32R)
    x_raw, xT_hi, xT_lo = m.x_raw, m.xT_hi, m.xT_lo
    res = sb("res", [P, ST, E])
    qs = sb("qs", [P, 2, 4, S], F32R)
    ks = sb("ks", [P, 2, 4, S], F32R)
    raw = sb("raw", [P, 2, S])
    swp = sb("swp", [P, S])
    rot = sb("rot", [P, S])
    qk_hi = sb("qk_hi", [P, 2, S], F32R)
    qk_lo = sb("qk_lo", [P, 2, S], F32R)
    vT = sb("vT", [P, S])
    vg = sb("vg", [P, 2, ST, P])
    prob = sb("prob", [P, PROBS, S])
    pT = sb("pT", [P, 4, 10 * P])
    nmax = sb("nmax", [P, 2, TILES])
    rsum = sb("rsum", [P, 2, ST, 4])
    rrec = sb("rrec", [P, TILES])
    rb = sb("rb", [P, ST, 4, D])
    o = sb("heads", [P, S])
    oT_hi = sb("oT_hi", [P, G, S], F32R)
    oT_lo = sb("oT_lo", [P, G, S], F32R)
    cos = sb("cos", [P, S])
    sin = sb("sin", [P, S])
    mask = sb("mask", [P, S])
    ident, mhalf = m.ident, m.mhalf
    bcol = sb("bcol", [P, 3 * G])
    bo = sb("bo", [P, E])
    stats = sb("stats", [P, ST, 6])
    mv = sb("mv", [P, ST, 2])
    rstd = sb("rstd", [P, ST])
    veps = sb("veps", [P, ST])

    def w_stage(c):
        if c < G - 1:
            return pT[:].rearrange("p h n -> p (h n)")[:, 3 * KT * P * c:3 * KT * P * (c + 1)]
        return res[:].rearrange("p s e -> p (s e)")[:, 0:3 * KT * P if c < G else KT * E]

    pj = ctx.enter_context(nc.psum_tensor("pj", [P, 2, S], F32))
    ps = ctx.enter_context(nc.psum_tensor("ps", [P, 2, S], F32))
    pa = ctx.enter_context(nc.psum_tensor("pa", [P, S], F32))
    pb = ctx.enter_context(nc.psum_tensor("pb", [P, S], F32))
    pc = ctx.enter_context(nc.psum_tensor("pc", [P, S], F32))
    pv = ctx.enter_context(nc.psum_tensor("pv", [P, S], F32))

    def output_bank(turn, s):
        return pa[:] if turn == "last" and s % 2 else pv[:]

    scratch = nc.dram_tensor("qk_scratch", (4 * P, S), F32, kind="Internal").ap()

    WEIGHTED = [(0, 0, 1, 6), (0, 1, 1, 8), (1, 1, 1, 9), (0, 2, 2, 0), (1, 2, 2, 2), (2, 2, 2, 4), (3, 3, 1, 7)]

    const_in = sem("const_in")
    sp_passed, dve_passed, pool_passed = (sem(f"{n}_passed") for n in ("sp", "dve", "pool"))
    w_in = [sem(f"w_in{c}") for c in range(G + 1)]
    w_hi_done, w_lo_done = sem("w_hi_done"), sem("w_lo_done")
    x_in = sem("x_in", 16, 16)
    xhi_done = sem("xhi_done", KT, KT)
    xlo_done = sem("xlo_done", KT, KT)
    pj_full = sem("pj_full", len(PLAN), 10)
    pj_moved = sem("pj_moved", len(PLAN), 10)
    swap_done = sem("swap_done", 2 * G, 2)
    sin_done = sem("sin_done", 2 * G, 2)
    cos_done = sem("cos_done", 2 * G, 2)
    rot_done = sem("rot_done", 2 * G, 2)
    qkhi_done = sem("qkhi_done", 2 * G, 2)
    qklo_done = sem("qklo_done", 2 * G, 2)
    stored = sem("stored", 64 * G, 64)
    stacked = sem("stacked", 128 * G, 128)
    s_done = sem("s_done", SLOTS)
    max_done = sem("max_done", SLOTS)
    exp_done = sem("exp_done", SLOTS)
    t_done = sem("t_done", SLOTS)
    a_moved, b_moved, c_moved = (sem(f"{n}_moved", H) for n in "abc")
    rec_done = sem("rec_done", G)
    rb_done = sem("rb_done", G)
    av_done = sem("av_done", G)
    o_done = sem("o_done", G)
    ohi_done, olo_done = sem("ohi_done", G), sem("olo_done", G)
    wo_done = sem("wo_done", ST)
    res_in = sem("res_in", 16)
    res_done = sem("res_done", ST)
    z_done = sem("z_done", ST)
    stats_done = sem("stats_done", ST)
    mv_done = sem("mv_done", ST)
    rstd_done = sem("rstd_done", ST)
    veps_done = sem("veps_done", ST)
    x1_done = sem("x1_done", ST)
    x1_stored = m.x1_stored
    mhalf_done = sem("mhalf_done")

    before = [("q", 0), ("k", 0), ("v", 0), ("t", 0), ("q", 1)] + list(plan("first"))
    USES = {turn: {key: n for n, key in enumerate(plan(turn))} | {key: n - len(before) for n, key in enumerate(before)}
            for turn in ("loop", "last")}
    USES["first"] = USES["loop"]

    def wait_moved(eng, b, turn, kind, g):
        eng.wait_ge(pj_moved.sem, pj_moved.at(b, USES[turn][kind, g] + 1))

    block = ctx.enter_context(nc.Block())

    @block.sync
    def _(sp):
        sp.dma_start(w_stage(0), d["w_qkv"][0:P, :]).then_inc(w_in[0].sem, 16)
        sp.dma_start(x_raw[:], d["xT"][0:P, :]).then_inc(x_in.sem, 16)
        for dst, name in ((bcol, "bcol"), (cos, "cos"), (sin, "sin"), (ident, "ident"), (mask, "mask"), (bo, "bo")):
            sp.dma_start(dst[:], d[name]).then_inc(const_in.sem, 16)
        for g in range(1, G):
            sp.dma_start(w_stage(g), d["w_qkv"][g * P:(g + 1) * P, :]).then_inc(w_in[g].sem, 16)

        def stack(b, g):
            for u in range(2):
                m = 2 * (g - 1) + u
                rows = 2 * u * P
                if g and not u:
                    sp.wait_ge(stacked.sem, stacked.at(b, 128 * (g - 1)))
                    passed(sp, b, sp_passed)
                sp.wait_ge(qkhi_done.sem, qkhi_done.at(b, m + 1))
                sp.dma_start(scratch[rows // 2:rows // 2 + P, :], qk_hi[:, u, :].bitcast(F32)).then_inc(stored.sem, 16)
                sp.wait_ge(qklo_done.sem, qklo_done.at(b, m + 1))
                sp.dma_start(scratch[2 * P + u * P:3 * P + u * P, :], qk_lo[:, u, :].bitcast(F32)).then_inc(stored.sem, 16)
                sp.wait_ge(stored.sem, stored.at(b, 32 * (m + 1)))
                passed(sp, b, sp_passed)
                if g >= 2:
                    sp.wait_ge(s_done.sem, s_done.at(b, TILES * (g - 1)))
                for j in range(4):
                    lo = j // 2 if u == 0 else j % 2
                    src = scratch[2 * P * lo + u * P:2 * P * lo + u * P + P, :]
                    dst = qs if u == 0 else ks
                    sp.dma_start(dst[D * j:D * j + D, g % 2, :, :].bitcast(F32),
                                 src.rearrange("(r d) s -> d r s", d=D)).then_inc(stacked.sem, 16)

        def turn(b, kind):
            stack(b, 2)
            if kind == "loop":
                sp.wait_ge(xhi_done.sem, xhi_done.at(b, 0))
                passed(sp, b, sp_passed)
                sp.wait_ge(xlo_done.sem, xlo_done.at(b, 0))
                passed(sp, b, sp_passed)
                sp.dma_start(x_raw[:], d["xT"][bass.ts(b + 1, P), :]).then_inc(x_in.sem, 16)
            sp.wait_ge(x1_stored.sem, x1_stored.at(b, 0))
            passed(sp, b, sp_passed)
            sp.dma_start(res[:], d["x"][bass.ts(b, P), :]).then_inc(res_in.sem, 16)
            for g in range(3, G + 2 if kind == "loop" else G):
                stack(b, g)
            if kind == "last":
                n = USES["last"]["v", G - 1]
                sp.wait_ge(pj_full.sem, pj_full.at(b, n + 1))
                load_between(sp, d, m, x1_dram)
            sp.wait_ge(x1_done.sem, x1_done.at(b, ST))
            passed(sp, b, sp_passed)
            sp.dma_start(x1_dram[bass.ts(b, P), :], res[:]).then_inc(x1_stored.sem, 16)

        sp.sem_inc(x1_stored.sem, 16)
        stack(0, 0)
        sp.wait_ge(w_hi_done.sem, G)
        sp.wait_ge(w_lo_done.sem, G)
        sp.dma_start(w_stage(G), d["wo"]).then_inc(w_in[G].sem, 16)
        stack(0, 1)
        sp.wait_ge(w_hi_done.sem, G + KT)
        sp.wait_ge(w_lo_done.sem, G + KT)
        with sp.Fori(0, B - 1) as b:
            turn(b, "loop")
        turn(B - 1, "last")

    @block.tensor
    def _(pe):
        def open_pj(b, turn, key):
            n = USES[turn][key]
            if n >= 2 - len(before):
                pe.wait_ge(pj_moved.sem, pj_moved.at(b, n - 1))
            return n % 2

        def close(mm, count):
            mm.then_inc(count.sem, 1)

        def projection(b, turn, kind, g, k):
            if k == 0:
                open_pj(b, turn, (kind, g))
            if kind == "q" and g in (0, G):
                pe.wait_ge(xhi_done.sem, xhi_done.at(b, k + 1 - (KT if g == 0 else 0)))
                pe.wait_ge(xlo_done.sem, xlo_done.at(b, k + 1 - (KT if g == 0 else 0)))
            bank = USES[turn][kind, g] % 2
            tile = 3 * (g % G) + "qkv".index(kind)
            for part, (w, x) in enumerate(((w_hi, xT_hi), (w_lo, xT_hi), (w_hi, xT_lo))):
                mm = pe.matmul(pj[:, bank, :], w[:, tile, k, :], x[:, k, :],
                               start=(part == 0 and k == 0), stop=(part == 2 and k == KT - 1))
            if k == KT - 1:
                close(mm, pj_full)

        def values(b, turn, g):
            bank = open_pj(b, turn, ("t", g))
            wait_moved(pe, b, turn, "v", g)
            for s in range(ST):
                mm = pe.transpose(pj[:, bank, s * P:(s + 1) * P], vT[:, s * P:(s + 1) * P], ident[:])
            close(mm, pj_full)

        def recips(b, turn, g):
            bank = open_pj(b, turn, ("r", g))
            pe.wait_ge(rb_done.sem, rb_done.at(b, g + 1))
            for s in range(ST):
                mm = pe.transpose(pj[:, bank, s * P:(s + 1) * P], rb[:, s, :, :].rearrange("p r d -> p (r d)"), ident[:])
            close(mm, pj_full)

        def scores(b, t):
            g, r, s = t // TILES, t % TILES // ST, ROW[t % ST]
            if t % TILES == 0:
                pe.wait_ge(stacked.sem, stacked.at(b, 128 * g))
            if t >= 2:
                pe.wait_ge(max_done.sem, max_done.at(b, t - 1))
            w = max(2, s + 1) * P
            close(pe.matmul(ps[:, t % 2, 0:w], qs[:, g % 2, r, s * P:(s + 1) * P], ks[:, g % 2, r, 0:w],
                            start=True, stop=True), s_done)

        def transposes(b, t):
            h, s = t // ST, ROW[t % ST]
            pe.wait_ge(exp_done.sem, exp_done.at(b, t + 1))
            if h and s:
                moved = (c_moved, b_moved, a_moved)[s - 1]
                pe.wait_ge(moved.sem, moved.at(b, h))
            for k in range(s + 1):
                dst = (pb, pc, pb, pa)[s]
                c = (k if s else 3) * P
                mm = pe.transpose(dst[:, c:c + P], prob[:, t % PROBS, k * P:(k + 1) * P], ident[:])
            close(mm, t_done)

        def weighted(b, turn, g):
            for moved in (a_moved, b_moved, c_moved):
                pe.wait_ge(moved.sem, moved.at(b, 4 * g + 4))
            wait_moved(pe, b, turn, "t", g)
            if g:
                pe.wait_ge(o_done.sem, o_done.at(b, g))
            for k, s, n, at in WEIGHTED:
                for r in range(4):
                    mm = pe.matmul(pv[D * r:D * r + D, s * P:(s + n) * P], vg[:, g % 2, k, D * r:D * r + D],
                                   pT[:, r, at * P:(at + n) * P], start=(k == 0), stop=(k == s + n - 1),
                                   tile_position=(0, D * r))
            close(mm, av_done)

        def output(b, turn, s, part):
            if part == 0:
                if s == 0:
                    pe.wait_ge(w_hi_done.sem, G + KT)
                    pe.wait_ge(w_lo_done.sem, G + KT)
                    pe.wait_ge(ohi_done.sem, ohi_done.at(b, G))
                    pe.wait_ge(olo_done.sem, olo_done.at(b, G))
                elif turn == "loop" or s >= 2:
                    pe.wait_ge(z_done.sem, z_done.at(b, s if turn == "loop" else s - 1))
            for k in range(KT // 2 * part, KT // 2 * (part + 1)):
                for p, (w, x) in enumerate(((wo_hi, oT_hi), (wo_lo, oT_hi), (wo_hi, oT_lo))):
                    mm = pe.matmul(output_bank(turn, s), x[:, k, s * P:(s + 1) * P], w[:, k, :],
                                   start=(p == 0 and k == 0), stop=(p == 2 and k == KT - 1))
            if part:
                close(mm, wo_done)

        def context_projection():
            wait_moved(pe, B - 1, "last", "r", G - 1)
            pe.wait_ge(m.p_lo_done.sem, 1)
            pe.wait_ge(m.clo_done.sem, 1)
            for u in range(2):
                for part, (w, c) in enumerate(((m.p_hi, m.c_hi), (m.p_lo, m.c_hi), (m.p_hi, m.c_lo))):
                    for k in range(CT):
                        mm = pe.matmul(pj[:, u, :], w[:, u, k, :], c[:, k, :], start=(part == 0 and k == 0),
                                       stop=(part == 2 and k == CT - 1))
                close(mm, m.qk_full)

        def slots(b, turn):
            end = SLOTS if turn == "last" else FIRST + SLOTS
            for t in span(turn):
                if t < end:
                    scores(b, t)
                for (kind, g), first in plan(turn).items():
                    if kind in "qkv" and first <= t < first + 4:
                        projection(b, turn, kind, g, t - first)
                    elif kind == "t" and t == first:
                        values(b, turn, g)
                    elif kind == "r" and t == first:
                        recips(b, turn, g)
                if LAG <= t < end + LAG:
                    transposes(b, t - LAG)
                if turn != "first" and t % TILES == 3 and t // TILES <= G:
                    weighted(b, turn, t // TILES - 1)
                if turn == "last" and t == SPLIT_CONTEXT + 4:
                    context_projection()
                if turn != "first":
                    for part in range(2):
                        if t - part in OUTPUT:
                            output(b, turn, OUTPUT[t - part], part)

        def load_wait(c):
            pe.wait_ge(w_hi_done.sem, c)
            pe.wait_ge(w_lo_done.sem, c)

        load_wait(1)
        for kind in "qkv":
            for k in range(KT):
                projection(0, "first", kind, 0, k)
        pe.wait_ge(const_in.sem, 16 * 6)
        values(0, "first", 0)
        load_wait(2)
        for k in range(KT):
            projection(0, "first", "q", 1, k)
        load_wait(G)
        slots(0, "first")
        with pe.Fori(0, B - 1) as b:
            slots(b, "loop")
        slots(B - 1, "last")

    @block.scalar
    def _(act):
        def w_half(c):
            act.wait_ge(w_in[c].sem, 16)
            act.copy(w_hi[:, 3 * c:3 * c + 3, :, :].rearrange("p a k m -> p (a k m)"), w_stage(c)).then_inc(w_hi_done.sem, 1)

        def wo_half(k):
            act.wait_ge(w_in[G].sem, 16)
            act.copy(wo_hi[:, k, :], w_stage(G)[:, k * E:(k + 1) * E]).then_inc(w_hi_done.sem, 1)

        def x_half(b, k, first=False):
            if not first and k == 0:
                n = USES["loop"]["v", G - 1]
                act.wait_ge(pj_full.sem, pj_full.at(b, n + 1))
                act.wait_ge(x_in.sem, x_in.at(b, 16))
            act.copy(xT_hi[:, k, :], x_raw[:, k, :]).then_inc(xhi_done.sem, 1)

        def from_pj(b, turn, kind, g):
            n = USES[turn][kind, g]
            act.wait_ge(pj_full.sem, pj_full.at(b, n + 1))
            src = pj[:, n % 2, :]
            if kind in "qk":
                u = "qk".index(kind)
                m = 2 * (g - 1) + u
                if g:
                    act.wait_ge(swap_done.sem, swap_done.at(b, m - 1))
                    act.wait_ge(cos_done.sem, cos_done.at(b, m - 1))
                ins = act.activation(raw[:, u, :], src, ACT.Identity, bias=bcol[:, 3 * (g % G) + u:3 * (g % G) + u + 1])
            elif kind == "v":
                ins = act.activation(vT[:], src, ACT.Identity, bias=bcol[:, 3 * (g % G) + 2:3 * (g % G) + 3])
            elif kind == "t":
                if g >= 2:
                    act.wait_ge(av_done.sem, av_done.at(b, g - 1))
                ins = act.copy(vg[:, g % 2, :, :].rearrange("p s m -> p (s m)"), src)
            else:
                if g:
                    act.wait_ge(olo_done.sem, olo_done.at(b, g))
                ins = act.copy(o[:], src)
            ins.then_inc(pj_moved.sem, 1)

        def qk_half(b, u, g):
            m = 2 * (g - 1) + u
            act.wait_ge(rot_done.sem, rot_done.at(b, m + 1))
            if g:
                act.wait_ge(stored.sem, stored.at(b, 64 * (g - 1)))
            act.copy(qk_hi[:, u, :], rot[:]).then_inc(qkhi_done.sem, 1)

        def exp(b, t):
            g, i, s = t // TILES, t % TILES, ROW[t % ST]
            w = (s + 1) * P
            act.wait_ge(max_done.sem, max_done.at(b, t + 1))
            act.activation(prob[:, t % PROBS, 0:w], prob[:, t % PROBS, 0:w], ACT.Exp, bias=nmax[:, g % 2, i:i + 1], scale=-1.0,
                           accum_out=rsum[:, g % 2, s, i // ST:i // ST + 1]).then_inc(exp_done.sem, 1)

        def move_a(b, h):
            if h >= 4:
                act.wait_ge(av_done.sem, av_done.at(b, h // 4))
            act.wait_ge(t_done.sem, t_done.at(b, ST * h + 1))
            act.copy(pT[:, h % 4, 0:8 * P].rearrange("p (k u m) -> p u k m", u=2, m=P)[:, 1, :, :],
                     pa[:].rearrange("p (k m) -> p k m", m=P)).then_inc(a_moved.sem, 1)

        def o_half(b, g):
            act.wait_ge(o_done.sem, o_done.at(b, g + 1))
            act.copy(oT_hi[:, g, :], o[:]).then_inc(ohi_done.sem, 1)

        def split_context():
            act.wait_ge(m.p_in.sem, 32)
            act.copy(m.p_hi[:].rearrange("p u k m -> p (u k m)"), m.p_raw[:].rearrange("p u k m -> p (u k m)")).then_inc(m.p_hi_done.sem, 1)
            act.wait_ge(m.c_in.sem, 16)
            act.copy(m.c_hi[:].rearrange("p k s -> p (k s)"), m.c_raw[:].rearrange("p k s -> p (k s)")).then_inc(m.chi_done.sem, 1)

        def context_query():
            for u in range(2):
                act.wait_ge(m.qk_full.sem, u + 1)
                act.activation(m.qk[:, u, :], pj[:, u, :], ACT.Identity, bias=m.pbias[:, u:u + 1]).then_inc(m.qk_moved.sem, 1)
            for u in range(2):
                act.wait_ge(m.qk_moved.sem, u + 1)
                act.copy(m.qk_hi[:, u, :], m.qk[:, u, :]).then_inc(m.qkhi_done.sem, 1)

        def slots(b, turn):
            end = SLOTS if turn == "last" else FIRST + SLOTS
            for t in span(turn):
                if t < end:
                    exp(b, t)
                if t % ST == 0 and ST <= t < end + ST:
                    move_a(b, t // ST - 1)
                for (kind, g), first in plan(turn).items():
                    if t == first + (3 if kind in "qkv" else 0):
                        from_pj(b, turn, kind, g)
                for (kind, g), first in halves(turn, SPLIT_QK):
                    if t == first:
                        qk_half(b, "qk".index(kind), g)
                for g in range(G):
                    if turn != "first" and t == PLAN["r", g] + SPLIT_O:
                        o_half(b, g)
                if turn == "last" and t == SPLIT_CONTEXT:
                    split_context()
                if turn == "last" and t == SPLIT_CONTEXT + 6:
                    context_query()
                if turn == "first" and t in SPLIT_WO:
                    wo_half(SPLIT_WO.index(t))
                if turn == "loop" and t in SPLIT_X:
                    x_half(b, SPLIT_X.index(t))

        w_half(0)
        act.wait_ge(x_in.sem, 16)
        for k in range(KT):
            x_half(0, k, True)
        act.wait_ge(const_in.sem, 16 * 6)
        for u in range(2):
            from_pj(0, "first", "qk"[u], 0)
        w_half(1)
        qk_half(0, 0, 0)
        from_pj(0, "first", "v", 0)
        qk_half(0, 1, 0)
        from_pj(0, "first", "t", 0)
        from_pj(0, "first", "q", 1)
        for c in range(2, G):
            w_half(c)
        slots(0, "first")
        with act.Fori(0, B - 1) as b:
            slots(b, "loop")
        slots(B - 1, "last")

    @block.vector
    def _(dve):
        def w_half(c):
            dve.wait_ge(w_hi_done.sem, c + 1)
            hi, lo = (w[:, 3 * c:3 * c + 3, :, :].rearrange("p a k m -> p (a k m)") for w in (w_hi, w_lo))
            dve.tensor_tensor(lo, w_stage(c), hi.bitcast(F32), ALU.subtract).then_inc(w_lo_done.sem, 1)

        def wo_half(k):
            dve.wait_ge(w_hi_done.sem, G + k + 1)
            dve.tensor_tensor(wo_lo[:, k, :], w_stage(G)[:, k * E:(k + 1) * E], wo_hi[:, k, :].bitcast(F32),
                              ALU.subtract).then_inc(w_lo_done.sem, 1)

        def rotate(b, turn, u, g):
            m = 2 * (g - 1) + u
            wait_moved(dve, b, turn, "qk"[u], g)
            if g or u:
                dve.wait_ge(rot_done.sem, rot_done.at(b, m))
            passed(dve, b, dve_passed)
            dve.stream_shuffle(swp[:], raw[:, u, :], SWAP).then_inc(swap_done.sem, 1)
            dve.wait_ge(swap_done.sem, swap_done.at(b, m + 1))
            dve.tensor_tensor(swp[:], swp[:], sin[:], ALU.mult).then_inc(sin_done.sem, 1)

        def row_max(b, t):
            g, i, s = t // TILES, t % TILES, ROW[t % ST]
            w = (s + 1) * P
            dve.wait_ge(s_done.sem, s_done.at(b, t + 1))
            if t >= PROBS:
                dve.wait_ge(t_done.sem, t_done.at(b, t + 1 - PROBS))
            passed(dve, b, dve_passed)
            dve.tensor_tensor_reduce(prob[:, t % PROBS, 0:w], ps[:, t % 2, 0:w], mask[:, S - w:S], -D ** -0.5, 3e38,
                                     ALU.add, ALU.min, accum_out=nmax[:, g % 2, i:i + 1]).then_inc(max_done.sem, 1)

        def move_b(b, h):
            if h >= 4:
                dve.wait_ge(av_done.sem, av_done.at(b, h // 4))
            dve.wait_ge(t_done.sem, t_done.at(b, ST * h + 3))
            dve.tensor_copy(pT[:, h % 4, 0:8 * P].rearrange("p (k u m) -> p u k m", u=2, m=P)[:, 0, :, :],
                            pb[:].rearrange("p (k m) -> p k m", m=P)).then_inc(b_moved.sem, 1)

        def move_c(b, h):
            dve.wait_ge(t_done.sem, t_done.at(b, ST * h + 4))
            dve.tensor_copy(pT[:, h % 4, 8 * P:10 * P], pc[:, 0:2 * P]).then_inc(c_moved.sem, 1)

        def recips(b, g):
            dve.wait_ge(exp_done.sem, exp_done.at(b, TILES * (g + 1)))
            dve.reciprocal(rrec[:], rsum[:, g % 2, :, :].rearrange("p s r -> p (s r)")).then_inc(rec_done.sem, 1)
            dve.wait_ge(rec_done.sem, rec_done.at(b, g + 1))
            dve.tensor_copy(rb[:], rrec[:].rearrange("p (s r) -> p s r", r=4).unsqueeze(3)
                            .to_broadcast([P, ST, 4, D])).then_inc(rb_done.sem, 1)

        def normalize(b, turn, g):
            dve.wait_ge(av_done.sem, av_done.at(b, g + 1))
            wait_moved(dve, b, turn, "r", g)
            dve.tensor_tensor(o[:], pv[:], o[:], ALU.mult).then_inc(o_done.sem, 1)

        def x_half(b, k, first=False):
            dve.wait_ge(xhi_done.sem, k + 1 if first else xhi_done.at(b, k + 1))
            dve.tensor_tensor(xT_lo[:, k, :], x_raw[:, k, :], xT_hi[:, k, :].bitcast(F32),
                              ALU.subtract).then_inc(xlo_done.sem, 1)

        def summed(b, turn, s):
            if s == 0:
                dve.wait_ge(res_done.sem, res_done.at(b, ST))
            dve.wait_ge(wo_done.sem, wo_done.at(b, s + 1))
            dve.tensor_tensor(res[:, s, :], output_bank(turn, s), res[:, s, :], ALU.add).then_inc(z_done.sem, 1)

        def moments(b, s):
            dve.wait_ge(z_done.sem, z_done.at(b, s + 1))
            dve.bn_stats(stats[:, s, :], res[:, s, :]).then_inc(stats_done.sem, 1)
            dve.wait_ge(stats_done.sem, stats_done.at(b, s + 1))
            passed(dve, b, dve_passed)
            dve.bn_aggr(mv[:, s, :], stats[:, s, :]).then_inc(mv_done.sem, 1)

        def layer_norm(b, s):
            dve.wait_ge(rstd_done.sem, rstd_done.at(b, s + 1))
            dve.tensor_scalar(res[:, s, :], res[:, s, :], mv[:, s, 0:1], rstd[:, s:s + 1],
                              ALU.subtract, ALU.mult).then_inc(x1_done.sem, 1)

        def split_context():
            dve.wait_ge(m.p_hi_done.sem, 1)
            dve.tensor_tensor(m.p_lo[:].rearrange("p u k m -> p (u k m)"), m.p_raw[:].rearrange("p u k m -> p (u k m)"),
                              m.p_hi[:].rearrange("p u k m -> p (u k m)").bitcast(F32), ALU.subtract).then_inc(m.p_lo_done.sem, 1)
            dve.wait_ge(m.chi_done.sem, 1)
            dve.tensor_tensor(m.c_lo[:].rearrange("p k s -> p (k s)"), m.c_raw[:].rearrange("p k s -> p (k s)"),
                              m.c_hi[:].rearrange("p k s -> p (k s)").bitcast(F32), ALU.subtract).then_inc(m.clo_done.sem, 1)

        def slots(b, turn):
            end = SLOTS if turn == "last" else FIRST + SLOTS
            for t in span(turn):
                if t < end:
                    row_max(b, t)
                if t % ST == 1 and ST <= t < end + ST:
                    move_b(b, t // ST - 1)
                if t % ST == 2 and ST <= t < end + ST:
                    move_c(b, t // ST - 1)
                if turn != "first" and t % TILES == 3 and t // TILES <= G:
                    recips(b, t // TILES - 1)
                for (kind, g), first in halves(turn, ROTATE):
                    if t == first:
                        rotate(b, turn, "qk".index(kind), g)
                if turn == "last" and t == SPLIT_CONTEXT + 1:
                    split_context()
                if turn == "first" and t in SPLIT_WO:
                    wo_half(SPLIT_WO.index(t))
                if turn == "first":
                    continue
                if turn == "loop" and t - 1 in SPLIT_X:
                    x_half(b, SPLIT_X.index(t - 1))
                for g in range(G):
                    if t == PLAN["r", g] + NORMALIZE:
                        normalize(b, turn, g)
                if t - 1 in OUTPUT:
                    summed(b, turn, OUTPUT[t - 1])
                if t - 2 in OUTPUT:
                    moments(b, OUTPUT[t - 2])
                if t - 4 in OUTPUT:
                    layer_norm(b, OUTPUT[t - 4])

        w_half(0)
        for k in range(KT):
            x_half(0, k, True)
        dve.wait_ge(const_in.sem, 16 * 6)
        rotate(0, "first", 0, 0)
        rotate(0, "first", 1, 0)
        for c in range(1, G):
            w_half(c)
        slots(0, "first")
        with dve.Fori(0, B - 1) as b:
            slots(b, "loop")
        slots(B - 1, "last")

    @block.gpsimd
    def _(pool):
        def rotate(b, turn, u, g):
            m = 2 * (g - 1) + u
            wait_moved(pool, b, turn, "qk"[u], g)
            if g or u:
                pool.wait_ge(qklo_done.sem, qklo_done.at(b, m))
            pool.tensor_tensor(rot[:], raw[:, u, :], cos[:], ALU.mult).then_inc(cos_done.sem, 1)
            pool.wait_ge(cos_done.sem, cos_done.at(b, m + 1))
            pool.wait_ge(sin_done.sem, sin_done.at(b, m + 1))
            pool.tensor_tensor(rot[:], rot[:], swp[:], ALU.add).then_inc(rot_done.sem, 1)

        def qk_half(b, u, g):
            m = 2 * (g - 1) + u
            pool.wait_ge(qkhi_done.sem, qkhi_done.at(b, m + 1))
            pool.tensor_tensor(qk_lo[:, u, :], rot[:], qk_hi[:, u, :].bitcast(F32),
                               ALU.subtract).then_inc(qklo_done.sem, 1)

        def o_half(b, g):
            pool.wait_ge(ohi_done.sem, ohi_done.at(b, g + 1))
            pool.tensor_tensor(oT_lo[:, g, :], o[:], oT_hi[:, g, :].bitcast(F32),
                               ALU.subtract).then_inc(olo_done.sem, 1)

        def residual(b):
            pool.wait_ge(res_in.sem, res_in.at(b, 16))
            for s in range(ST):
                pool.tensor_tensor(res[:, s, :], res[:, s, :], bo[:], ALU.add).then_inc(res_done.sem, 1)

        def root(b, s):
            pool.wait_ge(mv_done.sem, mv_done.at(b, s + 1))
            passed(pool, b, pool_passed)
            pool.tensor_scalar(veps[:, s:s + 1], mv[:, s, 1:2], EPS, None, ALU.add).then_inc(veps_done.sem, 1)
            pool.wait_ge(veps_done.sem, veps_done.at(b, s + 1))
            pool.tensor_tensor(rstd[:, s:s + 1], veps[:, s:s + 1], mhalf[:], ALU.pow).then_inc(rstd_done.sem, 1)

        def context_query():
            for u in range(2):
                pool.wait_ge(m.qkhi_done.sem, u + 1)
                pool.tensor_tensor(m.qk_lo[:, u, :], m.qk[:, u, :], m.qk_hi[:, u, :].bitcast(F32),
                                   ALU.subtract).then_inc(m.qklo_done.sem, 1)

        def slots(b, turn):
            for t in span(turn):
                if turn != "first" and t - 2 in OUTPUT:
                    root(b, OUTPUT[t - 2])
                if turn == "last" and t == SPLIT_CONTEXT + 7:
                    context_query()
                for (kind, g), first in halves(turn, ROTATE):
                    if t == first:
                        rotate(b, turn, "qk".index(kind), g)
                for (kind, g), first in halves(turn, SPLIT_QK):
                    if t == first:
                        qk_half(b, "qk".index(kind), g)
                if turn == "first":
                    continue
                for g in range(G):
                    if t == PLAN["r", g] + SPLIT_O:
                        o_half(b, g)
                if t == PLAN["q", G]:
                    residual(b)

        pool.memset(mhalf[:], -0.5).then_inc(mhalf_done.sem, 1)
        pool.wait_ge(const_in.sem, 16 * 6)
        for u in range(2):
            rotate(0, "first", u, 0)
            qk_half(0, u, 0)
        pool.wait_ge(mhalf_done.sem, 1)
        slots(0, "first")
        with pool.Fori(0, B - 1) as b:
            slots(b, "loop")
        slots(B - 1, "last")


NR = 4
BESIDE = {3: [("ctx", 0)], 4: [("qk", 0)], 5: [("e", 0), ("e", 1)], 6: [("e", 2), ("e", 3)],
          7: [("t", 0), ("t", 1)], 8: [("t", 2), ("t", 3)], 9: [("a", 0), ("a", 1)], 10: [("a", 2), ("a", 3)],
          11: [("m", 0)], 12: [("m", 1)], 13: [("m", 2)], 14: [("m", 3)]}
AHEAD = 2


def tiles(turn):
    return range(*{"first": (0, AHEAD), "loop": (AHEAD, HT + AHEAD), "last": (AHEAD, HT)}[turn])


def feed_forward_phase(nc, ctx, d, x1_dram, out, m):
    def sb(name, shape, dt=F32):
        return ctx.enter_context(nc.sbuf_tensor(name, shape, dt))

    def sem(name, per=0, base=0):
        return Count(ctx.enter_context(nc.semaphore(name)), per, base)

    f_raw, p_hi, p_lo, c_raw, c_hi, c_lo, pbias, x = m.f_raw, m.p_hi, m.p_lo, m.c_raw, m.c_hi, m.c_lo, m.pbias, m.x
    ident, mhalf = m.ident, m.mhalf
    x1_in, c_in, chi_done, clo_done, raw_in = m.x1_in, m.c_in, m.chi_done, m.clo_done, m.raw_in
    qk, qk_hi, qk_lo = m.qk, m.qk_hi, m.qk_lo
    qk_full, qk_moved, qkhi_done, qklo_done = m.qk_full, m.qk_moved, m.qkhi_done, m.qklo_done

    gu_hi = sb("gu_hi", [P, 2, 2, KT, P], F32R)
    gu_lo = sb("gu_lo", [P, 2, 2, KT, P], F32R)
    fin = sb("fin", [P, ST, E])
    dn_hi = sb("dn_hi", [P, 2, E], F32R)
    dn_lo = sb("dn_lo", [P, 2, E], F32R)
    e = sb("e", [P, KT, S])
    att_hi = sb("att_hi", [P, KT, S], F32R)
    att_lo = sb("att_lo", [P, KT, S], F32R)
    emax = sb("emax", [P, KT])
    nemax = sb("nemax", [P, KT])
    esum = sb("esum", [P, KT])
    erec = sb("erec", [P, KT])
    x1T_hi = sb("x1T_hi", [P, KT, S], F32R)
    x1T_lo = sb("x1T_lo", [P, KT, S], F32R)
    x2T_hi = sb("x2T_hi", [P, KT, S], F32R)
    x2T_lo = sb("x2T_lo", [P, KT, S], F32R)
    th = sb("th", [P, S])
    half = sb("half", [P, S])
    gated = sb("gated", [P, S])
    g_hi = sb("g_hi", [P, 2, S], F32R)
    g_lo = sb("g_lo", [P, 2, S], F32R)
    stats, mv, veps, rstd = ([sb(f"{n}{k}", [P, ST, w]) for k in (2, 3)]
                             for n, w in (("stats", 6), ("mv", 2), ("veps", 1), ("rstd", 1)))

    pg = ctx.enter_context(nc.psum_tensor("pg", [P, S], F32))
    pu = ctx.enter_context(nc.psum_tensor("pu", [P, S], F32))
    pd = ctx.enter_context(nc.psum_tensor("pd", [P, ST, E], F32))
    px = ctx.enter_context(nc.psum_tensor("px", [P, 2, S], F32))

    sp_passed, dve_passed, pool_passed = (sem(f"{n}_passed2") for n in ("sp", "dve", "pool"))
    e_full = sem("e_full", KT, KT)
    emax_done, nemax_done = sem("emax_done", KT, KT), sem("nemax_done", KT, KT)
    e_done = sem("e_done", KT, KT)
    erec_done, att_done = sem("erec_done", KT, KT), sem("att_done", KT, KT)
    a_full = sem("a_full", KT, KT)
    ahi_done, alo_done = sem("ahi_done", KT, KT), sem("alo_done", KT, KT)
    t1_full, t1hi_done, t1lo_done = (sem(n, ST, ST) for n in ("t1_full", "t1hi_done", "t1lo_done"))
    t2_full, t2hi_done, t2lo_done = (sem(n, ST, ST) for n in ("t2_full", "t2hi_done", "t2lo_done"))
    m_full = sem("m_full", ST, ST)
    guhi_done, gulo_done = sem("guhi_done", HT), sem("gulo_done", HT)
    dnhi_done, dnlo_done = sem("dnhi_done", HT), sem("dnlo_done", HT)
    g_full, u_full, d_full = sem("g_full", HT), sem("u_full", HT), sem("d_full", HT)
    th_done, gate_read, gated_done = sem("th_done", HT), sem("gate_read", HT), sem("gated_done", HT)
    ghi_done, glo_done = sem("ghi_done", HT), sem("glo_done", HT)
    fin_in = sem("fin_in", 16)
    out_done = sem("out_done", 16, 16)
    z_done = [sem("z2_done", ST, ST), sem("z3_done", ST, 1)]
    stats_done, mv_done, veps_done, rstd_done, ln_done = (
        [sem(f"{n}{k}_done", ST, (ST, 0)[k - 2]) for k in (2, 3)] for n in ("stats", "mv", "veps", "rstd", "ln"))

    block = ctx.enter_context(nc.Block())

    @block.sync
    def _(sp):
        def context(b):
            sp.dma_start(c_raw[:], d["cT"][bass.ts(b + 1, P), :]).then_inc(c_in.sem, 16)

        def features(b):
            sp.dma_start(x[:], x1_dram[bass.ts(b + 1, P), :]).then_inc(x1_in.sem, 16)

        def weights(c):
            sp.dma_start(f_raw[:, c % NR, :], d["w_ffn"][c * P:(c + 1) * P, :]).then_inc(raw_in[c % NR].sem, 16)

        def reload(b, js):
            for j in js:
                sp.wait_ge(gulo_done.sem, gulo_done.at(b, j + 1))
                passed(sp, b, sp_passed)
                sp.wait_ge(dnlo_done.sem, dnlo_done.at(b, j + 1))
                weights((j + NR) % HT)

        def slots(b, turn):
            if turn == "loop":
                sp.wait_ge(chi_done.sem, chi_done.at(b, 0))
                passed(sp, b, sp_passed)
                sp.wait_ge(clo_done.sem, clo_done.at(b, 0))
                passed(sp, b, sp_passed)
                context(b)
            sp.wait_ge(ln_done[0].sem, ln_done[0].at(b, 0))
            passed(sp, b, sp_passed)
            sp.wait_ge(out_done.sem, out_done.at(b, 0))
            sp.dma_start(fin[:], x[:]).then_inc(fin_in.sem, 16)
            sp.wait_ge(fin_in.sem, fin_in.at(b, 16))
            passed(sp, b, sp_passed)
            if turn == "loop":
                sp.wait_ge(t2lo_done.sem, t2lo_done.at(b, 0))
                passed(sp, b, sp_passed)
                features(b)
            reload(b, tiles("loop") if turn == "loop" else range(AHEAD, HT - NR))
            sp.wait_ge(ln_done[1].sem, ln_done[1].at(b, ST))
            passed(sp, b, sp_passed)
            sp.dma_start(out[bass.ts(b, P), :], fin[:]).then_inc(out_done.sem, 16)

        sp.sem_inc(out_done.sem, 16)
        sp.wait_ge(m.x1_stored.sem, m.x1_stored.at(B - 1, 16))
        reload(0, tiles("first"))
        with sp.Fori(0, B - 1) as b:
            slots(b, "loop")
        slots(B - 1, "last")
        sp.wait_ge(out_done.sem, out_done.at(B - 1, 16))

    @block.tensor
    def _(pe):
        def close(mm, count):
            mm.then_inc(count.sem, 1)

        def three(dst, n, stationary, moving, first=True, final=True):
            for part, (a, c) in enumerate(((0, 0), (1, 0), (0, 1))):
                for k in range(n):
                    mm = pe.matmul(dst, stationary(k)[a], moving(k)[c], start=(first and part == 0 and k == 0),
                                   stop=(final and part == 2 and k == n - 1))
            return mm

        def transposed(b, full, s, bank, src=x):
            for k in range(KT):
                mm = pe.transpose(px[:, bank, k * P:(k + 1) * P], src[:, s, k * P:(k + 1) * P], ident[:])
            close(mm, full)

        def beside(b, kind, n):
            if kind == "qk":
                pe.wait_ge(clo_done.sem, clo_done.at(b, 1))
                pe.wait_ge(chi_done.sem, chi_done.at(b, 1))
                for u in range(2):
                    close(three(px[:, u, :], CT, lambda k: (p_hi[:, u, k, :], p_lo[:, u, k, :]),
                                lambda k: (c_hi[:, k, :], c_lo[:, k, :])), qk_full)
            elif kind == "e":
                if n < 2:
                    pe.wait_ge(qk_moved.sem, qk_moved.at(b, 2))
                    pe.wait_ge(qkhi_done.sem, qkhi_done.at(b, 2))
                    pe.wait_ge(qklo_done.sem, qklo_done.at(b, 2))
                else:
                    pe.wait_ge(e_done.sem, e_done.at(b, n - 1))
                cols = slice(n * P, (n + 1) * P)
                close(three(px[:, n % 2, :], 1, lambda k: (qk_hi[:, 0, cols], qk_lo[:, 0, cols]),
                            lambda k: (qk_hi[:, 1, :], qk_lo[:, 1, :])), e_full)
            elif kind == "a":
                pe.wait_ge(att_done.sem, att_done.at(b, n + 1))
                if n < 2:
                    pe.wait_ge(t1lo_done.sem, t1lo_done.at(b, n + 3))
                else:
                    pe.wait_ge(alo_done.sem, alo_done.at(b, n - 1))
                transposed(b, a_full, n, n % 2, e)
            elif kind == "t":
                if n == 0:
                    pe.wait_ge(x1_in.sem, x1_in.at(b, 16))
                if n < 2:
                    pe.wait_ge(e_done.sem, e_done.at(b, n + 3))
                else:
                    pe.wait_ge(t1lo_done.sem, t1lo_done.at(b, n - 1))
                transposed(b, t1_full, n, n % 2)
            elif kind == "m":
                if n == 0:
                    pe.wait_ge(ahi_done.sem, ahi_done.at(b, KT))
                    pe.wait_ge(alo_done.sem, alo_done.at(b, KT))
                    pe.wait_ge(t1lo_done.sem, t1lo_done.at(b, ST))
                if n >= 2:
                    pe.wait_ge(z_done[0].sem, z_done[0].at(b, n - 1))
                cols = slice(n * P, (n + 1) * P)
                close(three(px[:, n % 2, :], KT, lambda k: (x1T_hi[:, k, cols], x1T_lo[:, k, cols]),
                            lambda k: (att_hi[:, k, :], att_lo[:, k, :])), m_full)
            elif kind == "u":
                for s in range(ST):
                    pe.wait_ge(ln_done[0].sem, ln_done[0].at(b, s + 1))
                    if s < 2:
                        pe.wait_ge(z_done[0].sem, z_done[0].at(b, s + 3))
                    else:
                        pe.wait_ge(t2lo_done.sem, t2lo_done.at(b, s - 1))
                    transposed(b, t2_full, s, s % 2)

        def hidden(b, j, u):
            if u == 0:
                pe.wait_ge(guhi_done.sem, guhi_done.at(b, j + 1))
                pe.wait_ge(gulo_done.sem, gulo_done.at(b, j + 1))
                if j % HT == 0:
                    pe.wait_ge(t2hi_done.sem, t2hi_done.at(b, ST * (j // HT)))
                    pe.wait_ge(t2lo_done.sem, t2lo_done.at(b, ST * (j // HT)))
                if j:
                    pe.wait_ge(gate_read.sem, gate_read.at(b, j))
            elif j:
                pe.wait_ge(gated_done.sem, gated_done.at(b, j))
            close(three((pg, pu)[u][:], KT, lambda k: (gu_hi[:, j % 2, u, k, :], gu_lo[:, j % 2, u, k, :]),
                        lambda k: (x2T_hi[:, k, :], x2T_lo[:, k, :])), (g_full, u_full)[u])

        def down(b, j):
            if j % HT == 0:
                pe.wait_ge(z_done[1].sem, z_done[1].at(b, ST * (j // HT)))
            pe.wait_ge(dnhi_done.sem, dnhi_done.at(b, j + 1))
            pe.wait_ge(dnlo_done.sem, dnlo_done.at(b, j + 1))
            pe.wait_ge(ghi_done.sem, ghi_done.at(b, j + 1))
            pe.wait_ge(glo_done.sem, glo_done.at(b, j + 1))
            for s in range(ST):
                cols = slice(s * P, (s + 1) * P)
                mm = three(pd[:, s, :], 1, lambda k: (g_hi[:, j % 2, cols], g_lo[:, j % 2, cols]),
                           lambda k: (dn_hi[:, j % 2, :], dn_lo[:, j % 2, :]), j % HT == 0, j % HT == HT - 1)
            close(mm, d_full)

        def slots(b, turn):
            for j in tiles(turn):
                hidden(b, j, 0)
                hidden(b, j, 1)
                if turn == "loop":
                    for kind, n in BESIDE.get(j, []):
                        beside(b, kind, n)
                    if j == HT - 1:
                        beside(b, "u", 0)
                if j:
                    down(b, j - 1)
            if turn == "last":
                down(b, HT - 1)

        for steps in list(BESIDE.values())[2:]:
            for kind, n in steps:
                beside(-1, kind, n)
        beside(-1, "u", 0)
        slots(0, "first")
        with pe.Fori(0, B - 1) as b:
            slots(b, "loop")
        slots(B - 1, "last")

    @block.scalar
    def _(act):
        def gu_half(b, j):
            act.wait_ge(raw_in[j % NR].sem, raw_in[j % NR].at(b, 16 * (j // NR + 1)))
            if j >= 2:
                act.wait_ge(u_full.sem, u_full.at(b, j - 1))
            act.copy(gu_hi[:, j % 2, :, :, :].rearrange("p u k m -> p (u k m)"),
                     f_raw[:, j % NR, 0:2 * KT * P]).then_inc(guhi_done.sem, 1)

        def dn_half(b, j):
            if j >= 2:
                act.wait_ge(d_full.sem, d_full.at(b, j - 1))
            act.copy(dn_hi[:, j % 2, :], f_raw[:, j % NR, 2 * KT * P:]).then_inc(dnhi_done.sem, 1)

        def t_half(b, full, done, dst, s):
            act.wait_ge(full.sem, full.at(b, s + 1))
            act.copy(dst[:, :, s * P:(s + 1) * P], px[:, s % 2, :].rearrange("p (k m) -> p k m", m=P)).then_inc(done.sem, 1)

        def beside(b, steps):
            for kind, n in steps:
                if kind == "ctx":
                    act.wait_ge(c_in.sem, c_in.at(b, 16))
                    act.copy(c_hi[:].rearrange("p k s -> p (k s)"), c_raw[:].rearrange("p k s -> p (k s)")).then_inc(chi_done.sem, 1)
                elif kind == "qk":
                    for u in range(2):
                        act.wait_ge(qk_full.sem, qk_full.at(b, u + 1))
                        act.activation(qk[:, u, :], px[:, u, :], ACT.Identity, bias=pbias[:, u:u + 1]).then_inc(qk_moved.sem, 1)
                    for u in range(2):
                        act.wait_ge(qk_moved.sem, qk_moved.at(b, u + 1))
                        act.copy(qk_hi[:, u, :], qk[:, u, :]).then_inc(qkhi_done.sem, 1)
                elif kind == "e":
                    act.wait_ge(nemax_done.sem, nemax_done.at(b, n + 1))
                    act.activation(e[:, n, :], px[:, n % 2, :], ACT.Exp, bias=nemax[:, n:n + 1], scale=1.0,
                                   accum_out=esum[:, n:n + 1]).then_inc(e_done.sem, 1)
                elif kind == "a":
                    t_half(b, a_full, ahi_done, att_hi, n)
                elif kind == "t":
                    t_half(b, t1_full, t1hi_done, x1T_hi, n)

        def transposed(b):
            for s in range(ST):
                t_half(b, t2_full, t2hi_done, x2T_hi, s)

        def slots(b, turn):
            for j in tiles(turn):
                act.wait_ge(g_full.sem, g_full.at(b, j + 1))
                if j:
                    act.wait_ge(gate_read.sem, gate_read.at(b, j))
                act.activation(th[:], pg[:], ACT.Tanh, scale=0.5).then_inc(th_done.sem, 1)
                more = turn != "last" or j < HT - 1
                if more:
                    gu_half(b, j + 1)
                if j == HT - 1 and turn == "loop":
                    transposed(b)
                act.wait_ge(gated_done.sem, gated_done.at(b, j + 1))
                if j >= 2:
                    act.wait_ge(d_full.sem, d_full.at(b, j - 1))
                act.copy(g_hi[:, j % 2, :], gated[:]).then_inc(ghi_done.sem, 1)
                if turn == "loop":
                    beside(b, BESIDE.get(j, []))
                if more:
                    dn_half(b, j + 1)

        steps = list(BESIDE.values())
        for step in steps[2:]:
            beside(-1, step)
            if step is steps[3]:
                gu_half(0, 0)
                dn_half(0, 0)
        transposed(-1)
        slots(0, "first")
        with act.Fori(0, B - 1) as b:
            slots(b, "loop")
        slots(B - 1, "last")

    @block.vector
    def _(dve):
        def gu_half(b, j):
            dve.wait_ge(guhi_done.sem, guhi_done.at(b, j + 1))
            if j >= 2:
                dve.wait_ge(u_full.sem, u_full.at(b, j - 1))
            flat = "p u k m -> p (u k m)"
            dve.tensor_tensor(gu_lo[:, j % 2, :, :, :].rearrange(flat), f_raw[:, j % NR, 0:2 * KT * P],
                              gu_hi[:, j % 2, :, :, :].rearrange(flat).bitcast(F32), ALU.subtract).then_inc(gulo_done.sem, 1)

        def dn_half(b, j):
            dve.wait_ge(dnhi_done.sem, dnhi_done.at(b, j + 1))
            if j >= 2:
                dve.wait_ge(d_full.sem, d_full.at(b, j - 1))
            dve.tensor_tensor(dn_lo[:, j % 2, :], f_raw[:, j % NR, 2 * KT * P:], dn_hi[:, j % 2, :].bitcast(F32),
                              ALU.subtract).then_inc(dnlo_done.sem, 1)

        def t_half(b, hi_done, done, hi, lo, s):
            cols = slice(s * P, (s + 1) * P)
            dve.wait_ge(hi_done.sem, hi_done.at(b, s + 1))
            dve.tensor_tensor(lo[:, :, cols], px[:, s % 2, :].rearrange("p (k m) -> p k m", m=P),
                              hi[:, :, cols].bitcast(F32), ALU.subtract).then_inc(done.sem, 1)

        def summed(b, which, full, src, dst, s, n):
            if which == 1 and s == 0:
                dve.wait_ge(fin_in.sem, fin_in.at(b, 16))
            dve.wait_ge(full.sem, full.at(b, n))
            dve.tensor_tensor(dst[:, s, :], src, dst[:, s, :], ALU.add).then_inc(z_done[which].sem, 1)

        def moments(b, which, dst, s):
            z, st, m = z_done[which], stats_done[which], mv_done[which]
            dve.wait_ge(z.sem, z.at(b, s + 1))
            dve.bn_stats(stats[which][:, s, :], dst[:, s, :]).then_inc(st.sem, 1)
            dve.wait_ge(st.sem, st.at(b, s + 1))
            passed(dve, b, dve_passed)
            dve.bn_aggr(mv[which][:, s, :], stats[which][:, s, :]).then_inc(m.sem, 1)

        def normalized(b, which, dst, s):
            dve.wait_ge(rstd_done[which].sem, rstd_done[which].at(b, s + 1))
            dve.tensor_scalar(dst[:, s, :], dst[:, s, :], mv[which][:, s, 0:1], rstd[which][:, s, :],
                              ALU.subtract, ALU.mult).then_inc(ln_done[which].sem, 1)

        def beside(b, steps):
            for kind, n in steps:
                if kind == "e":
                    dve.wait_ge(e_full.sem, e_full.at(b, n + 1))
                    dve.reduce_max(emax[:, n:n + 1], px[:, n % 2, :], AX.X).then_inc(emax_done.sem, 1)
                    dve.wait_ge(emax_done.sem, emax_done.at(b, n + 1))
                    dve.tensor_scalar(nemax[:, n:n + 1], emax[:, n:n + 1], -1.0, None, ALU.mult).then_inc(nemax_done.sem, 1)
                elif kind == "a":
                    t_half(b, ahi_done, alo_done, att_hi, att_lo, n)
                elif kind == "t":
                    t_half(b, t1hi_done, t1lo_done, x1T_hi, x1T_lo, n)
                elif kind == "m":
                    summed(b, 0, m_full, px[:, n % 2, :], x, n, n + 1)
                    moments(b, 0, x, n)
            for kind, n in steps:
                if kind == "e":
                    dve.wait_ge(e_done.sem, e_done.at(b, n + 1))
                    dve.reciprocal(erec[:, n:n + 1], esum[:, n:n + 1]).then_inc(erec_done.sem, 1)
                    dve.wait_ge(erec_done.sem, erec_done.at(b, n + 1))
                    dve.tensor_scalar(e[:, n, :], e[:, n, :], erec[:, n:n + 1], None, ALU.mult).then_inc(att_done.sem, 1)

        def after(b, steps):
            for kind, n in steps:
                if kind == "m":
                    normalized(b, 0, x, n)

        def transposed(b):
            for s in range(ST):
                t_half(b, t2hi_done, t2lo_done, x2T_hi, x2T_lo, s)

        def slots(b, turn):
            for j in tiles(turn):
                dve.wait_ge(th_done.sem, th_done.at(b, j + 1))
                if j:
                    dve.wait_ge(gated_done.sem, gated_done.at(b, j))
                dve.scalar_tensor_tensor(half[:], th[:], 1.0, pg[:], ALU.add, ALU.mult).then_inc(gate_read.sem, 1)
                more = turn != "last" or j < HT - 1
                if more:
                    gu_half(b, j + 1)
                dve.wait_ge(u_full.sem, u_full.at(b, j + 1))
                dve.wait_ge(gate_read.sem, gate_read.at(b, j + 1))
                if j:
                    dve.wait_ge(glo_done.sem, glo_done.at(b, j))
                dve.scalar_tensor_tensor(gated[:], half[:], 0.5, pu[:], ALU.mult, ALU.mult).then_inc(gated_done.sem, 1)
                if j == HT - 1 and turn == "loop":
                    transposed(b)
                if turn == "loop":
                    beside(b, BESIDE.get(j, []))
                if j == HT + 1:
                    for s in range(ST):
                        moments(b, 1, fin, s)
                if more:
                    dn_half(b, j + 1)
                if j == HT:
                    for s in range(ST):
                        summed(b, 1, d_full, pd[:, s, :], fin, s, HT)
                if j == HT + 1:
                    for s in range(ST):
                        normalized(b, 1, fin, s)
                if turn == "loop":
                    after(b, BESIDE.get(j, []))
            if turn == "last":
                for s in range(ST):
                    summed(b, 1, d_full, pd[:, s, :], fin, s, HT)
                    moments(b, 1, fin, s)
                for s in range(ST):
                    normalized(b, 1, fin, s)

        dve.sem_inc(z_done[1].sem, 1)
        for j, steps in BESIDE.items():
            beside(-1, steps)
            after(-1, steps)
            if steps == [("e", 2), ("e", 3)]:
                gu_half(0, 0)
                dn_half(0, 0)
        transposed(-1)
        slots(0, "first")
        with dve.Fori(0, B - 1) as b:
            slots(b, "loop")
        slots(B - 1, "last")

    @block.gpsimd
    def _(pool):
        def root(b, which, s):
            pool.wait_ge(mv_done[which].sem, mv_done[which].at(b, s + 1))
            passed(pool, b, pool_passed)
            pool.tensor_scalar(veps[which][:, s, :], mv[which][:, s, 1:2], EPS, None, ALU.add).then_inc(veps_done[which].sem, 1)
            pool.wait_ge(veps_done[which].sem, veps_done[which].at(b, s + 1))
            pool.tensor_tensor(rstd[which][:, s, :], veps[which][:, s, :], mhalf[:], ALU.pow).then_inc(rstd_done[which].sem, 1)

        def beside(b, steps):
            for kind, n in steps:
                if kind == "ctx":
                    pool.wait_ge(chi_done.sem, chi_done.at(b, 1))
                    pool.tensor_tensor(c_lo[:].rearrange("p k s -> p (k s)"), c_raw[:].rearrange("p k s -> p (k s)"),
                                       c_hi[:].rearrange("p k s -> p (k s)").bitcast(F32), ALU.subtract).then_inc(clo_done.sem, 1)
                elif kind == "qk":
                    for u in range(2):
                        pool.wait_ge(qkhi_done.sem, qkhi_done.at(b, u + 1))
                        pool.tensor_tensor(qk_lo[:, u, :], qk[:, u, :], qk_hi[:, u, :].bitcast(F32),
                                           ALU.subtract).then_inc(qklo_done.sem, 1)
                elif kind == "m":
                    root(b, 0, n)

        def slots(b, turn):
            for j in tiles(turn):
                pool.wait_ge(ghi_done.sem, ghi_done.at(b, j + 1))
                if j >= 2:
                    pool.wait_ge(d_full.sem, d_full.at(b, j - 1))
                pool.tensor_tensor(g_lo[:, j % 2, :], gated[:], g_hi[:, j % 2, :].bitcast(F32),
                                   ALU.subtract).then_inc(glo_done.sem, 1)
                if turn == "loop":
                    beside(b, BESIDE.get(j, []))
                if j == HT + 1:
                    for s in range(ST):
                        root(b, 1, s)
            if turn == "last":
                for s in range(ST):
                    root(b, 1, s)

        for steps in list(BESIDE.values())[2:]:
            beside(-1, steps)
        slots(0, "first")
        with pool.Fori(0, B - 1) as b:
            slots(b, "loop")
        slots(B - 1, "last")


def layouts(a):
    def tiles(w):
        return w.reshape(-1, P, w.shape[1]).transpose(1, 0, 2)

    pos = np.arange(S, dtype=np.float32)
    theta = np.power(np.float32(10000.0), -np.arange(0, D, 2, dtype=np.float32) / D)
    angle = pos[None, :] * np.tile(np.repeat(theta, 2), 4)[:, None]
    sign = np.tile(np.array([-1.0, 1.0], np.float32), P // 2)[:, None]
    mask = np.zeros((P, S), np.float32)
    mask[:, S - P:] = np.triu(np.full((P, P), MASKED, np.float32), 1)
    x = a["x"]
    qkv = np.stack([tiles(a[f"L0_attn_W{n}"]).reshape(P, KT, G, P) for n in "qkv"])
    return {
        "xT": x.reshape(B, S, KT, P).transpose(0, 3, 2, 1).reshape(B * P, KT * S),
        "x": x.reshape(B, ST, P, E).transpose(0, 2, 1, 3).reshape(B * P, ST * E),
        "w_qkv": qkv.transpose(3, 1, 0, 2, 4).reshape(G * P, 3 * KT * P),
        "wo": tiles(a["L0_attn_Wo"]).reshape(P, KT * E),
        "bcol": np.stack([a[f"L0_attn_b{n}"].reshape(G, P) for n in "qkv"]).transpose(2, 1, 0).reshape(P, 3 * G),
        "bo": np.broadcast_to(a["L0_attn_bo"], (P, E)),
        "cos": np.cos(angle), "sin": np.sin(angle) * sign,
        "mask": mask, "ident": np.eye(P, dtype=np.float32),
        "cT": a["ctx_1024"].reshape(B, S, CT, P).transpose(0, 3, 2, 1).reshape(B * P, CT * S),
        "w_ctx": np.stack([tiles(a[f"L0_xattn_W{n}"].T) for n in "qk"]).transpose(1, 0, 2, 3).reshape(P, 2 * CT * DK),
        "bctx": np.stack([a["L0_xattn_bq"], a["L0_xattn_bk"]]).T,
        "w_ffn": np.concatenate(
            [w.reshape(HT, P, KT, P).transpose(0, 3, 2, 1).reshape(HT, P, KT * P)
             for w in (a["L0_ffn_w_gate"], a["L0_ffn_w_up"])] +
            [a["L0_ffn_w_down"].T.reshape(HT, P, E)], axis=2).reshape(HT * P, 2 * KT * P + E),
    }


def decoder_layer(nc, d, out):
    x1_dram = nc.dram_tensor("x1_scratch", (B * P, ST * E), F32, kind="Internal").ap()
    with ExitStack() as both:
        between = Between(nc, both)
        with ExitStack() as ctx:
            attention_phase(nc, ctx, d, x1_dram, between)
        with ExitStack() as ctx:
            feed_forward_phase(nc, ctx, d, x1_dram, out, between)


def kernel(**inputs):
    import concourse.bacc as bacc
    from concourse.bass_utils import run_bass_kernel_spmd

    nc = bacc.Bacc("TRN2", target_bir_lowering=False, num_devices=1)
    arrays, d = {}, {}
    for name, a in layouts({k: np.asarray(v) for k, v in inputs.items()}).items():
        a = np.ascontiguousarray(a)
        arrays[f"in_{name}"] = a
        d[name] = nc.dram_tensor(f"in_{name}", a.shape, F32, kind="ExternalInput").ap()
    out = nc.dram_tensor("out", (B * P, ST * E), F32, kind="ExternalOutput").ap()
    decoder_layer(nc, d, out)
    got = run_bass_kernel_spmd(nc, [arrays], core_ids=[0]).results[0]["out"]
    return got.reshape(B, P, ST, E).transpose(0, 2, 1, 3).reshape(B, S, E)
```
